# Optimizing a Trainium2 kernel written in Bass

```python
import numpy as np
import jax
import jax.numpy as jnp

def _softmax(x, axis=-1):
    return jax.nn.softmax(x, axis=axis)

def _gelu(x):
    return jax.nn.gelu(x, approximate=True)

def _silu(x):
    return jax.nn.silu(x)

def _sigmoid(x):
    return jax.nn.sigmoid(x)

def _layernorm(x, axis=-1, eps=1e-05):
    m = jnp.mean(x, axis=axis, keepdims=True)
    v = jnp.var(x, axis=axis, keepdims=True)
    return (x - m) / jnp.sqrt(v + eps)

def _scatter_add(tgt, idx, src, axis=0):
    return tgt.at[idx].add(src)

def _segment_sum(src, seg, n):
    return jax.ops.segment_sum(src, seg, n)
kernel_name = 'mk_conv_seq_d4_conv_nchw512_r4_3bade0'

def setup_inputs(seed: int=0):
    np.random.seed(seed)
    _w = jnp.asarray

    def _rec_inputs():
        import jax
        import jax.numpy as jnp
        _gk = jax.random.key(seed)
        x = 7.22e-05 + 1 * jax.random.normal(jax.random.fold_in(_gk, 1), (4, 128, 16, 16), jnp.float32)
        return x
    x = _rec_inputs()

    def _L0_conv_setup():
        import jax, jax.numpy as jnp
        import numpy as np
        EPS = 1e-05

        def conv2d(x, w, pad):
            return jax.lax.conv_general_dilated(x, w, window_strides=(1, 1), padding=[(pad, pad), (pad, pad)], dimension_numbers=('NCHW', 'OIHW', 'NCHW'))

        def bn_relu(x, scale, bias, mean, var):
            inv = scale * jax.lax.rsqrt(var + EPS)
            return jax.nn.relu(x * inv[None, :, None, None] + (bias - mean * inv)[None, :, None, None])

        def sam(x, w_qk, w_v, gamma, latent_channels=16):
            b, c, h, w = x.shape
            s = h * w
            qk = conv2d(x, w_qk, 0).reshape(b, 2 * latent_channels, s)
            q, k = (qk[:, :latent_channels], qk[:, latent_channels:])
            v = conv2d(x, w_v, 0).reshape(b, c, s)
            scale = 1.0 / latent_channels ** 0.25
            m = jnp.einsum('bcs,bct->bst', scale * q, scale * k)
            m = jax.nn.softmax(m, axis=-1)
            a = jnp.einsum('bst,bct->bcs', m, v).reshape(b, c, h, w)
            return gamma * a + x

        def cam(x, gamma):
            b, c, h, w = x.shape
            y = x.reshape(b, c, h * w)
            scale = 1.0 / (h * w) ** 0.25
            m = jnp.einsum('bcs,bds->bcd', scale * y, scale * y)
            m = jax.nn.softmax(m, axis=-1)
            a = jnp.einsum('bcd,bds->bcs', m, y).reshape(b, c, h, w)
            return gamma * a + x
        key = jax.random.key(seed)
        ks = jax.random.split(key, 12)
        B, C, H, W = (4, 128, 16, 16)
        L = 16
        d = {}
        d['x'] = jax.random.normal(ks[0], (B, C, H, W), jnp.float32)
        d['w_sam'] = jax.random.normal(ks[1], (128, 128, 3, 3), jnp.float32) * (1.0 / np.sqrt(128 * 9))
        d['bn_sam_scale'] = jax.random.uniform(ks[2], (128,), jnp.float32, 0.5, 1.5)
        d['bn_sam_bias'] = jax.random.normal(ks[3], (128,), jnp.float32) * 0.1
        d['bn_sam_mean'] = jnp.zeros((128,), jnp.float32)
        d['bn_sam_var'] = jnp.ones((128,), jnp.float32)
        d['w_cam'] = jax.random.normal(ks[4], (128, 128, 3, 3), jnp.float32) * (1.0 / np.sqrt(128 * 9))
        d['bn_cam_scale'] = jax.random.uniform(ks[5], (128,), jnp.float32, 0.5, 1.5)
        d['bn_cam_bias'] = jax.random.normal(ks[6], (128,), jnp.float32) * 0.1
        d['bn_cam_mean'] = jnp.zeros((128,), jnp.float32)
        d['bn_cam_var'] = jnp.ones((128,), jnp.float32)
        d['w_qk'] = jax.random.normal(ks[7], (2 * L, 128, 1, 1), jnp.float32) * (1.0 / np.sqrt(128))
        d['w_v'] = jax.random.normal(ks[8], (128, 128, 1, 1), jnp.float32) * (1.0 / np.sqrt(128))
        d['gamma_sam'] = jax.random.uniform(ks[9], (1,), jnp.float32)
        d['gamma_cam'] = jax.random.uniform(ks[10], (1,), jnp.float32)
        d['w_out'] = jax.random.normal(ks[11], (128, 256, 3, 3), jnp.float32) * (1.0 / np.sqrt(256 * 9))
        return d
    _L0_conv_all = _L0_conv_setup()
    _L0_conv_in = {k: v for k, v in _L0_conv_all.items() if k in ('w_sam', 'bn_sam_scale', 'bn_sam_bias', 'bn_sam_mean', 'bn_sam_var', 'w_cam', 'bn_cam_scale', 'bn_cam_bias', 'bn_cam_mean', 'bn_cam_var', 'w_qk', 'w_v', 'gamma_sam', 'gamma_cam', 'w_out')}
    del _L0_conv_all

    def _L1_conv_setup():
        import jax, jax.numpy as jnp
        import numpy as np

        def _conv(x, w, b, stride=1, pad=0):
            y = jax.lax.conv_general_dilated(x, w, (stride, stride), [(pad, pad), (pad, pad)], dimension_numbers=('NCHW', 'OIHW', 'NCHW'))
            return y + b[None, :, None, None]

        def _channel_mask(x, w, b):
            pooled = jnp.mean(x, axis=(2, 3))
            logits = pooled @ w.T + b
            return (logits > 0).astype(x.dtype)[:, :, None, None]

        def _maxpool3(m):
            return jax.lax.reduce_window(m, -jnp.inf, jax.lax.max, (1, 1, 3, 3), (1, 1, 1, 1), [(0, 0), (0, 0), (1, 1), (1, 1)])

        def _hswish(x):
            return x * jax.nn.relu6(x + 3.0) / 6.0

        def _coord_att(x, w1, b1, wh, bh, ww, bw):
            B, C, H, W = x.shape
            xh = jnp.mean(x, axis=3, keepdims=True)
            xw = jnp.mean(x, axis=2, keepdims=True).transpose(0, 1, 3, 2)
            y = _hswish(_conv(jnp.concatenate([xh, xw], axis=2), w1, b1))
            yh, yw = (y[:, :, :H], y[:, :, H:])
            ah = jax.nn.sigmoid(_conv(yh, wh, bh))
            aw = jax.nn.sigmoid(_conv(yw, ww, bw)).transpose(0, 1, 3, 2)
            return x * ah * aw
        key = jax.random.key(seed)
        ks = jax.random.split(key, 16)
        B, INP, WID, OUP, H, W, MIP = (16, 128, 32, 128, 56, 56, 16)
        f32 = jnp.float32
        rn = lambda k, s, sc: jax.random.normal(k, s, f32) * sc
        return {'x': rn(ks[0], (B, INP, H, W), 1.0), 'sm_w': rn(ks[1], (1, INP, 1, 1), 0.05), 'sm_b': jnp.zeros((1,), f32), 'cm1_w': rn(ks[2], (WID, INP), 0.05), 'cm1_b': jnp.zeros((WID,), f32), 'cm2_w': rn(ks[3], (WID, WID), 0.09), 'cm2_b': jnp.zeros((WID,), f32), 'cm3_w': rn(ks[4], (OUP, WID), 0.09), 'cm3_b': jnp.zeros((OUP,), f32), 'w1': rn(ks[5], (WID, INP, 1, 1), 0.044), 'b1': jnp.zeros((WID,), f32), 'w2': rn(ks[6], (WID, WID, 3, 3), 0.029), 'b2': jnp.zeros((WID,), f32), 'w3': rn(ks[7], (OUP, WID, 1, 1), 0.088), 'b3': jnp.zeros((OUP,), f32), 'ca_w1': rn(ks[8], (MIP, OUP, 1, 1), 0.044), 'ca_b1': jnp.zeros((MIP,), f32), 'ca_wh': rn(ks[9], (OUP, MIP, 1, 1), 0.25), 'ca_bh': jnp.zeros((OUP,), f32), 'ca_ww': rn(ks[10], (OUP, MIP, 1, 1), 0.25), 'ca_bw': jnp.zeros((OUP,), f32)}
    _L1_conv_all = _L1_conv_setup()
    _L1_conv_in = {k: v for k, v in _L1_conv_all.items() if k in ('sm_w', 'sm_b', 'cm1_w', 'cm1_b', 'cm2_w', 'cm2_b', 'cm3_w', 'cm3_b', 'w1', 'b1', 'w2', 'b2', 'w3', 'b3', 'ca_w1', 'ca_b1', 'ca_wh', 'ca_bh', 'ca_ww', 'ca_bw')}
    del _L1_conv_all

    def _L2_conv_setup():
        import jax, jax.numpy as jnp
        import numpy as np
        LATENT_CH = 16

        def conv1x1(x, w):
            gain = 1.0 / np.sqrt(w.shape[1])
            return jnp.einsum('bchw,oc->bohw', x, w * gain)

        def casual_attention(q, k, v):
            score = jnp.einsum('bcn,bcm->bnm', q, k)
            score = jax.nn.softmax(score, axis=-1)
            return jnp.einsum('bnm,bcm->bnc', score, v)
        key = jax.random.key(seed)
        ks = jax.random.split(key, 8)
        B, C, H, W = (8, 128, 16, 16)
        L, P = (LATENT_CH, 64)
        return {'feature_map': jax.random.normal(ks[0], (B, C, H, W), jnp.float32), 'concepts': jax.random.normal(ks[1], (P, L), jnp.float32), 'w_theta': jax.random.normal(ks[2], (L, C), jnp.float32), 'w_phi': jax.random.normal(ks[3], (L, C), jnp.float32), 'w_g': jax.random.normal(ks[4], (L, C), jnp.float32), 'w_o': jax.random.normal(ks[5], (C, L), jnp.float32), 'gamma_sa': jnp.float32(0.1), 'gamma_moca': jnp.float32(0.1)}
    _L2_conv_all = _L2_conv_setup()
    _L2_conv_in = {k: v for k, v in _L2_conv_all.items() if k in ('concepts', 'w_theta', 'w_phi', 'w_g', 'w_o', 'gamma_sa', 'gamma_moca')}
    del _L2_conv_all

    def _L3_conv_setup():
        import jax, jax.numpy as jnp
        import numpy as np

        def _conv1x1(x, W, b):
            return jnp.einsum('bchw,oc->bohw', x, W) + b[None, :, None, None]
        key = jax.random.key(seed)
        ks = jax.random.split(key, 8)
        B, C, H, W = (16, 128, 48, 48)
        d = C // 8
        scale = 0.02
        return {'feat_map': jax.random.normal(ks[0], (B, C, H, W), dtype=jnp.float32), 'Wq': jax.random.normal(ks[1], (d, C), dtype=jnp.float32) * scale, 'bq': jax.random.normal(ks[2], (d,), dtype=jnp.float32) * scale, 'Wk': jax.random.normal(ks[3], (d, C), dtype=jnp.float32) * scale, 'bk': jax.random.normal(ks[4], (d,), dtype=jnp.float32) * scale, 'Wv': jax.random.normal(ks[5], (C, C), dtype=jnp.float32) * scale, 'bv': jax.random.normal(ks[6], (C,), dtype=jnp.float32) * scale, 'gamma': jnp.ones((1,), dtype=jnp.float32)}
    _L3_conv_all = _L3_conv_setup()
    _L3_conv_in = {k: v for k, v in _L3_conv_all.items() if k in ('Wq', 'bq', 'Wk', 'bk', 'Wv', 'bv', 'gamma')}
    del _L3_conv_all
    return {'x': x, 'L0_conv_w_sam': _L0_conv_in['w_sam'], 'L0_conv_bn_sam_scale': _L0_conv_in['bn_sam_scale'], 'L0_conv_bn_sam_bias': _L0_conv_in['bn_sam_bias'], 'L0_conv_bn_sam_mean': _L0_conv_in['bn_sam_mean'], 'L0_conv_bn_sam_var': _L0_conv_in['bn_sam_var'], 'L0_conv_w_cam': _L0_conv_in['w_cam'], 'L0_conv_bn_cam_scale': _L0_conv_in['bn_cam_scale'], 'L0_conv_bn_cam_bias': _L0_conv_in['bn_cam_bias'], 'L0_conv_bn_cam_mean': _L0_conv_in['bn_cam_mean'], 'L0_conv_bn_cam_var': _L0_conv_in['bn_cam_var'], 'L0_conv_w_qk': _L0_conv_in['w_qk'], 'L0_conv_w_v': _L0_conv_in['w_v'], 'L0_conv_gamma_sam': _L0_conv_in['gamma_sam'], 'L0_conv_gamma_cam': _L0_conv_in['gamma_cam'], 'L0_conv_w_out': _L0_conv_in['w_out'], 'L1_conv_sm_w': _L1_conv_in['sm_w'], 'L1_conv_sm_b': _L1_conv_in['sm_b'], 'L1_conv_cm1_w': _L1_conv_in['cm1_w'], 'L1_conv_cm1_b': _L1_conv_in['cm1_b'], 'L1_conv_cm2_w': _L1_conv_in['cm2_w'], 'L1_conv_cm2_b': _L1_conv_in['cm2_b'], 'L1_conv_cm3_w': _L1_conv_in['cm3_w'], 'L1_conv_cm3_b': _L1_conv_in['cm3_b'], 'L1_conv_w1': _L1_conv_in['w1'], 'L1_conv_b1': _L1_conv_in['b1'], 'L1_conv_w2': _L1_conv_in['w2'], 'L1_conv_b2': _L1_conv_in['b2'], 'L1_conv_w3': _L1_conv_in['w3'], 'L1_conv_b3': _L1_conv_in['b3'], 'L1_conv_ca_w1': _L1_conv_in['ca_w1'], 'L1_conv_ca_b1': _L1_conv_in['ca_b1'], 'L1_conv_ca_wh': _L1_conv_in['ca_wh'], 'L1_conv_ca_bh': _L1_conv_in['ca_bh'], 'L1_conv_ca_ww': _L1_conv_in['ca_ww'], 'L1_conv_ca_bw': _L1_conv_in['ca_bw'], 'L2_conv_concepts': _L2_conv_in['concepts'], 'L2_conv_w_theta': _L2_conv_in['w_theta'], 'L2_conv_w_phi': _L2_conv_in['w_phi'], 'L2_conv_w_g': _L2_conv_in['w_g'], 'L2_conv_w_o': _L2_conv_in['w_o'], 'L2_conv_gamma_sa': _L2_conv_in['gamma_sa'], 'L2_conv_gamma_moca': _L2_conv_in['gamma_moca'], 'L3_conv_Wq': _L3_conv_in['Wq'], 'L3_conv_bq': _L3_conv_in['bq'], 'L3_conv_Wk': _L3_conv_in['Wk'], 'L3_conv_bk': _L3_conv_in['bk'], 'L3_conv_Wv': _L3_conv_in['Wv'], 'L3_conv_bv': _L3_conv_in['bv'], 'L3_conv_gamma': _L3_conv_in['gamma']}

def reference(x, L0_conv_w_sam, L0_conv_bn_sam_scale, L0_conv_bn_sam_bias, L0_conv_bn_sam_mean, L0_conv_bn_sam_var, L0_conv_w_cam, L0_conv_bn_cam_scale, L0_conv_bn_cam_bias, L0_conv_bn_cam_mean, L0_conv_bn_cam_var, L0_conv_w_qk, L0_conv_w_v, L0_conv_gamma_sam, L0_conv_gamma_cam, L0_conv_w_out, L1_conv_sm_w, L1_conv_sm_b, L1_conv_cm1_w, L1_conv_cm1_b, L1_conv_cm2_w, L1_conv_cm2_b, L1_conv_cm3_w, L1_conv_cm3_b, L1_conv_w1, L1_conv_b1, L1_conv_w2, L1_conv_b2, L1_conv_w3, L1_conv_b3, L1_conv_ca_w1, L1_conv_ca_b1, L1_conv_ca_wh, L1_conv_ca_bh, L1_conv_ca_ww, L1_conv_ca_bw, L2_conv_concepts, L2_conv_w_theta, L2_conv_w_phi, L2_conv_w_g, L2_conv_w_o, L2_conv_gamma_sa, L2_conv_gamma_moca, L3_conv_Wq, L3_conv_bq, L3_conv_Wk, L3_conv_bk, L3_conv_Wv, L3_conv_bv, L3_conv_gamma):
    import jax
    import jax.numpy as jnp

    def _L0_conv_ref(x, w_sam, bn_sam_scale, bn_sam_bias, bn_sam_mean, bn_sam_var, w_cam, bn_cam_scale, bn_cam_bias, bn_cam_mean, bn_cam_var, w_qk, w_v, gamma_sam, gamma_cam, w_out):
        import jax, jax.numpy as jnp
        import numpy as np
        EPS = 1e-05

        def conv2d(x, w, pad):
            return jax.lax.conv_general_dilated(x, w, window_strides=(1, 1), padding=[(pad, pad), (pad, pad)], dimension_numbers=('NCHW', 'OIHW', 'NCHW'))

        def bn_relu(x, scale, bias, mean, var):
            inv = scale * jax.lax.rsqrt(var + EPS)
            return jax.nn.relu(x * inv[None, :, None, None] + (bias - mean * inv)[None, :, None, None])

        def sam(x, w_qk, w_v, gamma, latent_channels=16):
            b, c, h, w = x.shape
            s = h * w
            qk = conv2d(x, w_qk, 0).reshape(b, 2 * latent_channels, s)
            q, k = (qk[:, :latent_channels], qk[:, latent_channels:])
            v = conv2d(x, w_v, 0).reshape(b, c, s)
            scale = 1.0 / latent_channels ** 0.25
            m = jnp.einsum('bcs,bct->bst', scale * q, scale * k)
            m = jax.nn.softmax(m, axis=-1)
            a = jnp.einsum('bst,bct->bcs', m, v).reshape(b, c, h, w)
            return gamma * a + x

        def cam(x, gamma):
            b, c, h, w = x.shape
            y = x.reshape(b, c, h * w)
            scale = 1.0 / (h * w) ** 0.25
            m = jnp.einsum('bcs,bds->bcd', scale * y, scale * y)
            m = jax.nn.softmax(m, axis=-1)
            a = jnp.einsum('bcd,bds->bcs', m, y).reshape(b, c, h, w)
            return gamma * a + x
        xs = bn_relu(conv2d(x, w_sam, 1), bn_sam_scale, bn_sam_bias, bn_sam_mean, bn_sam_var)
        xs = sam(xs, w_qk, w_v, gamma_sam)
        xc = bn_relu(conv2d(x, w_cam, 1), bn_cam_scale, bn_cam_bias, bn_cam_mean, bn_cam_var)
        xc = cam(xc, gamma_cam)
        xcat = jnp.concatenate([xs, xc], axis=1)
        return conv2d(xcat, w_out, 1)

    def _L1_conv_ref(x, sm_w, sm_b, cm1_w, cm1_b, cm2_w, cm2_b, cm3_w, cm3_b, w1, b1, w2, b2, w3, b3, ca_w1, ca_b1, ca_wh, ca_bh, ca_ww, ca_bw):
        import jax, jax.numpy as jnp
        import numpy as np

        def _conv(x, w, b, stride=1, pad=0):
            y = jax.lax.conv_general_dilated(x, w, (stride, stride), [(pad, pad), (pad, pad)], dimension_numbers=('NCHW', 'OIHW', 'NCHW'))
            return y + b[None, :, None, None]

        def _channel_mask(x, w, b):
            pooled = jnp.mean(x, axis=(2, 3))
            logits = pooled @ w.T + b
            return (logits > 0).astype(x.dtype)[:, :, None, None]

        def _maxpool3(m):
            return jax.lax.reduce_window(m, -jnp.inf, jax.lax.max, (1, 1, 3, 3), (1, 1, 1, 1), [(0, 0), (0, 0), (1, 1), (1, 1)])

        def _hswish(x):
            return x * jax.nn.relu6(x + 3.0) / 6.0

        def _coord_att(x, w1, b1, wh, bh, ww, bw):
            B, C, H, W = x.shape
            xh = jnp.mean(x, axis=3, keepdims=True)
            xw = jnp.mean(x, axis=2, keepdims=True).transpose(0, 1, 3, 2)
            y = _hswish(_conv(jnp.concatenate([xh, xw], axis=2), w1, b1))
            yh, yw = (y[:, :, :H], y[:, :, H:])
            ah = jax.nn.sigmoid(_conv(yh, wh, bh))
            aw = jax.nn.sigmoid(_conv(yw, ww, bw)).transpose(0, 1, 3, 2)
            return x * ah * aw
        identity = x
        s_mask = (_conv(x, sm_w, sm_b) > 0).astype(x.dtype)
        s_mask_dil = _maxpool3(s_mask)
        cm1 = _channel_mask(x, cm1_w, cm1_b)
        h = jax.nn.relu(_conv(x, w1, b1)) * cm1 * s_mask_dil
        cm2 = _channel_mask(h, cm2_w, cm2_b)
        h = jax.nn.relu(_conv(h, w2, b2, pad=1)) * cm2 * s_mask
        cm3 = _channel_mask(h, cm3_w, cm3_b)
        h = _conv(h, w3, b3) * cm3 * s_mask
        out = _coord_att(h, ca_w1, ca_b1, ca_wh, ca_bh, ca_ww, ca_bw)
        return jax.nn.relu(out + identity)

    def _L2_conv_ref(feature_map, concepts, w_theta, w_phi, w_g, w_o, gamma_sa, gamma_moca):
        import jax, jax.numpy as jnp
        import numpy as np
        LATENT_CH = 16

        def conv1x1(x, w):
            gain = 1.0 / np.sqrt(w.shape[1])
            return jnp.einsum('bchw,oc->bohw', x, w * gain)

        def casual_attention(q, k, v):
            score = jnp.einsum('bcn,bcm->bnm', q, k)
            score = jax.nn.softmax(score, axis=-1)
            return jnp.einsum('bnm,bcm->bnc', score, v)
        B, C, H, W = feature_map.shape
        L = LATENT_CH
        HW = H * W
        th = conv1x1(feature_map, w_theta).reshape(B, L, HW)
        ph = conv1x1(feature_map, w_phi).reshape(B, L, HW)
        g = conv1x1(feature_map, w_g).reshape(B, L, HW)
        lat = casual_attention(th, ph, g).reshape(B, L, H, W)
        sa_out = gamma_sa * conv1x1(lat, w_o) + feature_map
        enc = conv1x1(sa_out, w_theta).reshape(B, L, HW)
        phi_c = concepts.T[None]
        phi_c = jnp.broadcast_to(phi_c, (B, L, concepts.shape[0]))
        lat2 = casual_attention(enc, phi_c, phi_c).reshape(B, L, H, W)
        out = gamma_moca * conv1x1(lat2, w_o) + sa_out
        return out

    def _L3_conv_ref(feat_map, Wq, bq, Wk, bk, Wv, bv, gamma):
        import jax, jax.numpy as jnp
        import numpy as np

        def _conv1x1(x, W, b):
            return jnp.einsum('bchw,oc->bohw', x, W) + b[None, :, None, None]
        B, C, H, W = feat_map.shape
        HW = H * W
        q = _conv1x1(feat_map, Wq, bq).reshape(B, -1, HW).transpose(0, 2, 1)
        k = _conv1x1(feat_map, Wk, bk).reshape(B, -1, HW)
        attn = jax.nn.softmax(jnp.einsum('bnd,bdm->bnm', q, k), axis=-1)
        v = _conv1x1(feat_map, Wv, bv).reshape(B, C, HW)
        out = jnp.einsum('bcm,bnm->bcn', v, attn).reshape(B, C, H, W)
        return gamma * out + feat_map

    def _gn(v, G=32, eps=1e-05):
        B_, C_, H_, W_ = v.shape
        g = v.reshape(B_, G, C_ // G, H_, W_)
        m = jnp.mean(g, axis=(2, 3, 4), keepdims=True)
        s = jnp.var(g, axis=(2, 3, 4), keepdims=True)
        return ((g - m) / jnp.sqrt(s + eps)).reshape(v.shape)

    def _ln_c(v, eps=1e-06):
        m = jnp.mean(v, axis=1, keepdims=True)
        s = jnp.var(v, axis=1, keepdims=True)
        return (v - m) / jnp.sqrt(s + eps)

    def _ln_t(v, eps=1e-05):
        m = jnp.mean(v, axis=-1, keepdims=True)
        s = jnp.var(v, axis=-1, keepdims=True)
        return (v - m) / jnp.sqrt(s + eps)

    def _to_tokens(v):
        B_, C_, H_, W_ = v.shape
        return v.reshape(B_, C_, H_ * W_).transpose(0, 2, 1)

    def _from_tokens(t, like):
        B_, C_, H_, W_ = like.shape
        return t.transpose(0, 2, 1).reshape(B_, C_, H_, W_)
    x = _L0_conv_ref(x, L0_conv_w_sam, L0_conv_bn_sam_scale, L0_conv_bn_sam_bias, L0_conv_bn_sam_mean, L0_conv_bn_sam_var, L0_conv_w_cam, L0_conv_bn_cam_scale, L0_conv_bn_cam_bias, L0_conv_bn_cam_mean, L0_conv_bn_cam_var, L0_conv_w_qk, L0_conv_w_v, L0_conv_gamma_sam, L0_conv_gamma_cam, L0_conv_w_out)
    x = _L1_conv_ref(x, L1_conv_sm_w, L1_conv_sm_b, L1_conv_cm1_w, L1_conv_cm1_b, L1_conv_cm2_w, L1_conv_cm2_b, L1_conv_cm3_w, L1_conv_cm3_b, L1_conv_w1, L1_conv_b1, L1_conv_w2, L1_conv_b2, L1_conv_w3, L1_conv_b3, L1_conv_ca_w1, L1_conv_ca_b1, L1_conv_ca_wh, L1_conv_ca_bh, L1_conv_ca_ww, L1_conv_ca_bw)
    x = _L2_conv_ref(x, L2_conv_concepts, L2_conv_w_theta, L2_conv_w_phi, L2_conv_w_g, L2_conv_w_o, L2_conv_gamma_sa, L2_conv_gamma_moca)
    x = _L3_conv_ref(x, L3_conv_Wq, L3_conv_bq, L3_conv_Wk, L3_conv_bk, L3_conv_Wv, L3_conv_bv, L3_conv_gamma)
    return x

_drawn_inputs = setup_inputs


def setup_inputs(seed=0):
    import zlib

    import numpy as np

    out = dict(_drawn_inputs(seed))
    spreads = {'L0_conv_bn_sam_mean': (0.0, 0.1),
     'L0_conv_bn_sam_var': (1.0, 0.2),
     'L0_conv_bn_cam_mean': (0.0, 0.1),
     'L0_conv_bn_cam_var': (1.0, 0.2),
     'L1_conv_cm1_b': (0.0, 0.8),
     'L1_conv_cm2_b': (0.0, 0.8),
     'L1_conv_cm3_b': (0.0, 0.572),
     'L1_conv_b1': (0.0, 0.8),
     'L1_conv_b2': (0.0, 0.8),
     'L1_conv_b3': (0.0, 0.563),
     'L1_conv_ca_b1': (0.0, 0.8),
     'L1_conv_ca_bh': (0.0, 0.8),
     'L1_conv_ca_bw': (0.0, 0.8)}
    factors = {'L0_conv_w_qk': 4.647,
     'L1_conv_sm_w': 7.946,
     'L1_conv_cm1_w': 8.0,
     'L1_conv_cm2_w': 8.0,
     'L1_conv_cm3_w': 8.0,
     'L1_conv_w1': 8.0,
     'L1_conv_w2': 8.0,
     'L1_conv_w3': 8.0,
     'L1_conv_ca_w1': 8.0,
     'L1_conv_ca_wh': 8.0,
     'L1_conv_ca_ww': 8.0,
     'L2_conv_w_phi': 5.183,
     'L3_conv_Wq': 8.0,
     'L3_conv_bq': 8.0,
     'L3_conv_Wk': 8.0,
     'L3_conv_bk': 64.0,
     'L3_conv_bv': 8.0}
    for name, (base, spread) in spreads.items():
        noise = np.random.default_rng([zlib.crc32(name.encode()), seed]).standard_normal(out[name].shape)
        drawn = base * np.exp(spread * noise) if base else spread * noise
        out[name] = jnp.asarray(drawn.astype(out[name].dtype))
    for name, factor in factors.items():
        out[name] = (out[name] * factor).astype(out[name].dtype)
    return out
```

```python
from contextlib import ExitStack

import concourse.bass as bass
from concourse import mybir

F32 = mybir.dt.float32
F32R = mybir.dt.float32r
ALU = mybir.AluOpType
ACT = mybir.ActivationFunctionType
AX = mybir.AxisListType

B, C, H, W = 4, 128, 16, 16
HW = H * W
P = 128
HP, WP = H + 2, W + 2
TAPS = [(dy, dx) for dy in range(3) for dx in range(3)]
NT = len(TAPS)
L = 16
WID = 32
MIP = 16
NCON = 64
NCH = HW // P
KCOL = 32
WIN = P - WID

EARLY = [("bn_scale", 2), ("bn_bias", 2), ("bn_mean", 2), ("bn_var", 2), ("gam_sam", 1), ("gam_cam", 1),
         ("ident", P), ("w_qk", KCOL + L), ("w_v", C)]
LATE = [("sm_b", 1), ("b1", 1), ("b2", 1), ("cm1_b", 1), ("cm2_b", 1), ("cm3_b", 1), ("ca_b1", 1),
        ("ca_bh", 1), ("ca_bw", 1), ("gam_sa", 1), ("gam_moca", 1), ("gam3", 1), ("bq", 1), ("bk", 1),
        ("bv", 1), ("group", B), ("sel16", L),
        ("sm_win", WIN + WID + WIN), ("w1_win", WIN + WID + WIN), ("cm1_win", WIN + WID + WIN),
        ("w2_rep", NT * WID), ("cm2_rep", WID), ("cm3_rep", C), ("w3_rep", C), ("b3_row", C),
        ("ca_w1", MIP), ("ca_wh", C), ("ca_ww", C),
        ("w_thph", KCOL + L), ("w_g", L), ("w_o_rep", NCH * C), ("con_t", NCON), ("con", L),
        ("w_qk3", KCOL + L), ("w_v3", C)]


def columns(table):
    at, out = 0, {}
    for name, width in table:
        out[name] = (at, width)
        at += width
    return out, at


EARLY_AT, EARLY_W = columns(EARLY)
LATE_AT, LATE_W = columns(LATE)


def build(nc, x, w_sam, w_cam, w_out, early, late, out):
    with ExitStack() as ctx:
        def sb(name, shape, dt=F32):
            return ctx.enter_context(nc.sbuf_tensor(name, shape, dt))

        def sem(name):
            return ctx.enter_context(nc.semaphore(name))

        bank = [ctx.enter_context(nc.psum_tensor(f"bank{i}", [P, 512], F32)) for i in range(8)]

        par0 = sb("par0", [P, EARLY_W])
        par1 = sb("par1", [P, LATE_W])

        def p0(name, rows=P):
            a, w = EARLY_AT[name]
            return par0[0:rows, a:a + w]

        def p1(name, rows=P):
            a, w = LATE_AT[name]
            return par1[0:rows, a:a + w]

        ident = p0("ident")

        ws = {n: sb(f"w_{n}", [P, NT * C]) for n in ("sam", "cam", "out_s", "out_c")}
        wh = {n: sb(f"wh_{n}", [P, NT * C], F32R) for n in ws}
        wl = {n: sb(f"wl_{n}", [P, NT * C], F32R) for n in ws}
        x_sb = sb("x_sb", [P, B, HW])
        padh = {n: sb(f"padh_{n}", [P, B, HP, WP], F32R) for n in ("x", "s", "c")}
        padl = {n: sb(f"padl_{n}", [P, B, HP, WP], F32R) for n in ("x", "s", "c")}

        bn_inv = sb("bn_inv", [P, 2])
        bn_shift = sb("bn_shift", [P, 2])
        bn_tmp = sb("bn_tmp", [P, 4, 2])
        xs = sb("xs", [P, B, HW])
        xc = sb("xc", [P, B, HW])
        q_sb = sb("q_sb", [L, 2, HW])
        k_sb = sb("k_sb", [L, 2, HW])
        vt_sb = sb("vt_sb", [P, B, NCH, C])
        prob = sb("prob", [P, B, NCH, HW])
        pt_sb = sb("pt_sb", [P, B, NCH, HW])
        nmax = sb("nmax", [P, B, NCH])
        rsum = sb("rsum", [P, B, NCH])
        rinv = sb("rinv", [P, B, NCH])
        yt_sb = sb("yt_sb", [P, B, NCH, C])
        cprob = sb("cprob", [P, B, C])
        cpt = sb("cpt", [P, B, C])
        cmax = sb("cmax", [P, B])
        cnm = sb("cnm", [P, B])
        csum = sb("csum", [P, B])
        cinv = sb("cinv", [P, B])
        att_s = sb("att_s", [P, B, HW])
        att_c = sb("att_c", [P, B, HW])

        x1 = sb("x1", [P, B, HW])
        pool1 = sb("pool1", [P, B])
        w2bd = sb("w2bd", [P, NT, P])
        cm2bd = sb("cm2bd", [P, P])
        w3z = sb("w3z", [P, B, C])
        b3z = sb("b3z", [P, B, C])
        thr = sb("thr", [P, 3])
        hb = sb("hb", [P, 2])
        cm = sb("cm", [P, 2])
        mpad = sb("mpad", [P, HP, WP])
        mflat = sb("mflat", [P, H, W])
        mrow = sb("mrow", [P, 2, HP, W])
        mdil = sb("mdil", [P, 2, H, W])
        hr = sb("hr", [P, 2, H, W])
        hpad = sb("hpad", [P, HP, WP])
        h2 = sb("h2", [P, H, W])
        pool2 = sb("pool2", [P, 2])
        pool3g = sb("pool3g", [P, B])
        cm3 = sb("cm3", [P, B])
        cm3s = sb("cm3s", [P, B])
        linem = sb("linem", [P, 2, H])
        lineh = sb("lineh", [P, 2, H])
        yin = sb("yin", [P, B, 2, H])
        yb = sb("yb", [MIP, B, 2, H])
        yr = sb("yr", [MIP, B, 2, H])
        ys = sb("ys", [MIP, B, 2, H])
        gate = sb("gate", [P, 2, B, H])
        gate1 = sb("gate1", [P, 2, B, H])
        t1 = xs[:, :, :].rearrange("p b (h w) -> p b h w", h=H)
        t2 = xc[:, :, :].rearrange("p b (h w) -> p b h w", h=H)
        t3 = att_s
        x2 = sb("x2", [P, B, HW])

        th = sb("th", [L, B, HW])
        ph = sb("ph", [L, B, HW])
        gt = sb("gt", [P, B, NCH, L])
        gsc = sb("gsc", [P, 2])
        wide = sb("wide", [P, B, NCH, L, L])
        sa = sb("sa", [P, B, HW])
        enc = th
        prob2 = sb("prob2", [P, B, NCH, NCON])
        pt2 = pt_sb[0:NCON, :, 0, :]
        nmax2 = sb("nmax2", [P, B, NCH])
        rsum2 = sb("rsum2", [P, B, NCH])
        rinv2 = sb("rinv2", [P, B, NCH])
        wide2 = wide
        x3 = x1

        q3 = th
        k3 = ph
        vt3 = vt_sb
        gbv = sb("gbv", [P, 1])
        x3b = att_c
        y = x_sb

        d_x = [sem(f"d_x{i}") for i in range(2)]
        d_w = {n: [sem(f"d_w_{n}{i}") for i in range(3)] for n in ws}
        d_early, d_late, d_y = sem("d_early"), sem("d_late"), sem("d_y")
        border = sem("border")
        x_hi, x_lo = sem("x_hi"), sem("x_lo")
        w_hi, w_lo = sem("w_hi"), sem("w_lo")
        bn_var = sem("bn_var")
        bn_std = sem("bn_std")
        bn_step = sem("bn_step")
        sam_conv, cam_conv = sem("sam_conv"), sem("cam_conv")
        xs_done, xc_done = sem("xs_done"), sem("xc_done")
        s_proj, s_qkv_sb, s_score, s_max = sem("s_proj"), sem("s_qkv_sb"), sem("s_score"), sem("s_max")
        s_exp, s_rinv, s_norm, s_tp, s_pt_sb = sem("s_exp"), sem("s_rinv"), sem("s_norm"), sem("s_tp"), sem("s_pt_sb")
        s_av, s_att, s_hi, s_lo = sem("s_av"), sem("s_att"), sem("s_hi"), sem("s_lo")
        c_yt, c_yt_sb, c_gram, c_max = sem("c_yt"), sem("c_yt_sb"), sem("c_gram"), sem("c_max")
        c_nm, c_exp, c_rinv, c_norm = sem("c_nm"), sem("c_exp"), sem("c_rinv"), sem("c_norm")
        c_tp, c_pt_sb, c_av, c_att = sem("c_tp"), sem("c_pt_sb"), sem("c_av"), sem("c_att")
        c_hi, c_lo = sem("c_hi"), sem("c_lo")
        out_conv, x1_done = sem("out_conv"), sem("x1_done")
        zeroed, spread = sem("zeroed"), sem("spread")
        prep = sem("prep")
        m_logit, h1_conv, cm1_logit = sem("m_logit"), sem("h1_conv"), sem("cm1_logit")
        m_step, m_lines = sem("m_step"), sem("m_lines")
        h1_relu, h1_done, cm1_done = sem("h1_relu"), sem("h1_done"), sem("cm1_done")
        h2_conv, cm2_logit, h2_relu, h2_done, cm2_done = (sem("h2_conv"), sem("cm2_logit"), sem("h2_relu"),
                                                          sem("h2_done"), sem("cm2_done"))
        h2_lines, h2_pool = sem("h2_lines"), sem("h2_pool")
        cm3_logit, cm3_done, line_mm, yin_done = (sem("cm3_logit"), sem("cm3_done"), sem("line_mm"),
                                                  sem("yin_done"))
        y_mm, y_step, gate_mm, gate_tanh, gate_done = (sem("y_mm"), sem("y_step"), sem("gate_mm"),
                                                       sem("gate_tanh"), sem("gate_done"))
        h3_mm, t1_done, t2_done, t3_done, x2_done = (sem("h3_mm"), sem("t1_done"), sem("t2_done"),
                                                     sem("t3_done"), sem("x2_done"))
        a_proj, a_qk_sb, a_g_sb, a_score, a_max = (sem("a_proj"), sem("a_qk_sb"), sem("a_g_sb"),
                                                   sem("a_score"), sem("a_max"))
        a_exp, a_rinv, a_tp, a_pt_sb, a_av, a_wide, a_o, a_done = (
            sem("a_exp"), sem("a_rinv"), sem("a_tp"), sem("a_pt_sb"), sem("a_av"), sem("a_wide"), sem("a_o"),
            sem("a_done"))
        e_proj, e_sb, e_score, e_max = sem("e_proj"), sem("e_sb"), sem("e_score"), sem("e_max")
        e_exp, e_rinv, e_tp, e_pt_sb, e_av, e_wide, e_o, e_done = (
            sem("e_exp"), sem("e_rinv"), sem("e_tp"), sem("e_pt_sb"), sem("e_av"), sem("e_wide"), sem("e_o"),
            sem("e_done"))
        f_proj, f_qkv_sb, f_score, f_max = sem("f_proj"), sem("f_qkv_sb"), sem("f_score"), sem("f_max")
        f_exp, f_rinv, f_norm, f_tp, f_pt_sb, f_av, f_xb, f_done = (
            sem("f_exp"), sem("f_rinv"), sem("f_norm"), sem("f_tp"), sem("f_pt_sb"), sem("f_av"), sem("f_xb"),
            sem("f_done"))

        x_dram = x.rearrange("b c h w -> c b (h w)")
        out_dram = out.rearrange("b c h w -> c b (h w)")
        w_dram = {"sam": w_sam, "cam": w_cam, "out_s": w_out[:, 0:NT * C], "out_c": w_out[:, NT * C:2 * NT * C]}
        third = NT * C // 3
        W_ORDER = ["sam", "cam", "out_s", "out_c"]

        def inner(pad, b, n=1):
            return pad[:, b:b + n, 1:1 + H, 1:1 + W]

        def flat4(ap):
            return ap.rearrange("p b (h w) -> p b h w", h=H)

        block = ctx.enter_context(nc.Block())

        @block.sync
        def _(sp):
            for i in range(2):
                sp.dma_start(x_sb[:, 2 * i:2 * i + 2, :], x_dram[:, 2 * i:2 * i + 2, :]).then_inc(d_x[i], 16)
            sp.dma_start(par0[:, :], early).then_inc(d_early, 16)
            for n in ("cam", "out_s", "out_c"):
                for i in range(3):
                    sp.dma_start(ws[n][:, third * i:third * (i + 1)],
                                 w_dram[n][:, third * i:third * (i + 1)]).then_inc(d_w[n][i], 16)
            sp.dma_start(par1[:, :], late).then_inc(d_late, 16)
            for b in range(B):
                sp.wait_ge(f_done, b + 1)
                sp.dma_start(out_dram[:, b, :], y[:, b, :]).then_inc(d_y, 16)
            sp.wait_ge(d_y, 16 * B)

        @block.gpsimd
        def _(pool):
            for n in ("s", "c"):
                for pad in (padh[n], padl[n]):
                    nc.gpsimd.memset(pad[:, :, 0:HP:HP - 1, :].bitcast(F32), 0.0).then_inc(border, 1)
                    nc.gpsimd.memset(pad[:, :, 1:1 + H, 0:WP:WP - 1].bitcast(F32), 0.0).then_inc(border, 1)
            for t in (mpad, hpad, w2bd, cm2bd, w3z, b3z):
                nc.gpsimd.memset(t[:], 0.0).then_inc(zeroed, 1)
            pool.wait_ge(zeroed, 6)
            pool.wait_ge(d_late, 16)
            for b in range(B):
                r = slice(WID * b, WID * (b + 1))
                nc.gpsimd.tensor_copy(w2bd[r, :, WID * b:WID * (b + 1)],
                                      par1[r, LATE_AT["w2_rep"][0]:LATE_AT["w2_rep"][0] + NT * WID]
                                      .rearrange("p (t o) -> p t o", t=NT)).then_inc(spread, 1)
                nc.gpsimd.tensor_copy(cm2bd[r, WID * b:WID * (b + 1)],
                                      par1[r, LATE_AT["cm2_rep"][0]:LATE_AT["cm2_rep"][0] + WID]).then_inc(spread, 1)
                nc.gpsimd.tensor_copy(w3z[r, b, :],
                                      par1[r, LATE_AT["w3_rep"][0]:LATE_AT["w3_rep"][0] + C]).then_inc(spread, 1)
                nc.gpsimd.tensor_copy(b3z[WID * b:WID * b + 1, b, :],
                                      par1[WID * b:WID * b + 1, LATE_AT["b3_row"][0]:LATE_AT["b3_row"][0] + C]
                                      ).then_inc(spread, 1)
            for b in range(B):
                pool.wait_ge(t2_done, b + 1)
                pool.wait_ge(x1_done, b + 1)
                nc.gpsimd.tensor_tensor(t3[:, b, :], t2[:, b, :, :].rearrange("p h w -> p (h w)"), x1[:, b, :],
                                        ALU.add).then_inc(t3_done, 1)

        @block.scalar
        def _(act):
            for i in range(3):
                act.dma_start(ws["sam"][:, third * i:third * (i + 1)],
                              w_dram["sam"][:, third * i:third * (i + 1)]).then_inc(d_w["sam"][i], 16)

            def x_high(i):
                act.wait_ge(d_x[i], 16)
                nc.scalar.copy(inner(padh["x"], 2 * i, 2), flat4(x_sb[:, 2 * i:2 * i + 2, :])).then_inc(x_hi, 1)

            def w_high(n, i):
                act.wait_ge(d_w[n][i], 16)
                nc.scalar.copy(wh[n][:, third * i:third * (i + 1)],
                               ws[n][:, third * i:third * (i + 1)]).then_inc(w_hi, 1)

            x_high(0)
            for i in range(3):
                w_high("sam", i)
            x_high(1)
            act.wait_ge(bn_var, 1)
            nc.scalar.activation(bn_tmp[:, 1, :], bn_tmp[:, 0, :], ACT.Sqrt).then_inc(bn_std, 1)
            for i in range(3):
                w_high("cam", i)
            act.wait_ge(bn_step, 4)
            for i in range(2):
                act.wait_ge(sam_conv, i + 1)
                nc.scalar.activation(xs[:, 2 * i:2 * i + 2, :].rearrange("p b s -> p (b s)"), bank[i][:, :],
                                     ACT.Relu, bias=bn_shift[:, 0:1], scale=bn_inv[:, 0:1]).then_inc(xs_done, 1)
                for j in range(3):
                    w_high(("out_s", "out_c")[i], j)

            for t in range(B + 3):
                if 0 <= t - 2 < B:
                    b = t - 2
                    act.wait_ge(s_tp, b + 1)
                    nc.scalar.copy(pt_sb[:, b, :, :].rearrange("p j s -> p (j s)"), bank[6][:, :]).then_inc(s_pt_sb, 1)
                if 0 <= t - 1 < B:
                    b = t - 1
                    act.wait_ge(s_max, b + 1)
                    for i in range(NCH):
                        nc.scalar.activation(prob[:, b, i, :], bank[5][:, HW * i:HW * (i + 1)], ACT.Exp,
                                             bias=nmax[:, b, i:i + 1],
                                             accum_out=rsum[:, b, i:i + 1]).then_inc(s_exp, 1)
                if 0 <= t - 3 < B:
                    b = t - 3
                    act.wait_ge(s_att, b + 1)
                    nc.scalar.copy(inner(padh["s"], b), flat4(att_s[:, b:b + 1, :])).then_inc(s_hi, 1)
                if t in (4, 6):
                    i = (t - 4) // 2
                    act.wait_ge(cam_conv, i + 1)
                    nc.scalar.activation(xc[:, 2 * i:2 * i + 2, :].rearrange("p b s -> p (b s)"), bank[2 + i][:, :],
                                         ACT.Relu, bias=bn_shift[:, 1:2], scale=bn_inv[:, 1:2]).then_inc(xc_done, 1)
            for t in range(B + 3):
                if 0 <= t - 2 < B:
                    b = t - 2
                    act.wait_ge(c_tp, b + 1)
                    nc.scalar.copy(cpt[:, b, :], bank[6][:, 0:C]).then_inc(c_pt_sb, 1)
                if 0 <= t - 1 < B:
                    b = t - 1
                    act.wait_ge(c_nm, b + 1)
                    nc.scalar.activation(cprob[:, b, :], bank[5][:, 0:C], ACT.Exp, bias=cnm[:, b:b + 1],
                                         scale=1.0 / 16, accum_out=csum[:, b:b + 1]).then_inc(c_exp, 1)
                if 0 <= t - 3 < B:
                    b = t - 3
                    act.wait_ge(c_att, b + 1)
                    nc.scalar.copy(inner(padh["c"], b), flat4(att_c[:, b:b + 1, :])).then_inc(c_hi, 1)

            for b in range(B):
                act.wait_ge(out_conv, b // 2 + 1)
                nc.scalar.activation(x1[:, b, :], bank[b // 2][:, HW * (b % 2):HW * (b % 2 + 1)], ACT.Copy,
                                     accum_out=pool1[:, b:b + 1]).then_inc(x1_done, 1)
            act.wait_ge(h1_conv, 1)
            nc.scalar.activation(hr[:, 0, :, :].rearrange("p h w -> p (h w)"), bank[3][:, 0:HW], ACT.Relu,
                                 bias=p1("b1")).then_inc(h1_relu, 1)
            act.wait_ge(h2_conv, 1)
            nc.scalar.activation(hr[:, 1, :, :].rearrange("p h w -> p (h w)"), bank[5][:, 0:HW], ACT.Relu,
                                 bias=p1("b2")).then_inc(h2_relu, 1)
            act.wait_ge(gate_mm, 1)
            act.wait_ge(prep, 2)
            for i in range(2):
                nc.scalar.activation(gate[:, i, :, :].rearrange("p b h -> p (b h)"),
                                     bank[3][:, B * H * i:B * H * (i + 1)], ACT.Tanh, bias=hb[:, i:i + 1],
                                     scale=1.0 / 12).then_inc(gate_tanh, 1)
            for b in range(B):
                act.wait_ge(t3_done, b + 1)
                nc.scalar.activation(x2[:, b, :], t3[:, b, :], ACT.Relu).then_inc(x2_done, 1)

            for b in range(B):
                act.wait_ge(a_proj, b + 1)
                o = bank[b % 2]
                nc.scalar.mul(th[:, b, :], o[0:L, 0:HW], 1.0 / C)
                nc.scalar.copy(ph[:, b, :], o[KCOL:KCOL + L, 0:HW])
                nc.scalar.copy(gt[:, b, :, :].rearrange("p j l -> p (j l)"), o[:, HW:HW + NCH * L]).then_inc(a_qk_sb, 1)
            for b in range(B):
                act.wait_ge(a_max, b + 1)
                for i in range(NCH):
                    nc.scalar.activation(prob[:, b, i, :], bank[2 + b % 2][:, HW * i:HW * (i + 1)], ACT.Exp,
                                         bias=nmax[:, b, i:i + 1], accum_out=rsum[:, b, i:i + 1]).then_inc(a_exp, 1)
            for b in range(B):
                act.wait_ge(e_proj, b + 1)
                nc.scalar.mul(enc[:, b, :], bank[b % 2][0:L, 0:HW], float(C) ** -0.5).then_inc(e_sb, 1)
            for b in range(B):
                act.wait_ge(e_max, b + 1)
                for i in range(NCH):
                    nc.scalar.activation(prob2[:, b, i, :], bank[2 + b % 2][:, NCON * i:NCON * (i + 1)], ACT.Exp,
                                         bias=nmax2[:, b, i:i + 1], accum_out=rsum2[:, b, i:i + 1]).then_inc(e_exp, 1)
            for b in range(B):
                act.wait_ge(e_tp, b + 1)
                nc.scalar.copy(pt2[:, b, :], bank[4 + b % 2][0:NCON, 0:HW]).then_inc(e_pt_sb, 1)
            for b in range(B):
                act.wait_ge(f_proj, b + 1)
                o = bank[b % 2]
                nc.scalar.activation(q3[:, b, :], o[0:L, 0:HW], ACT.Identity, bias=p1("bq", L))
                nc.scalar.activation(k3[:, b, :], o[KCOL:KCOL + L, 0:HW], ACT.Identity, bias=p1("bk", L))
                nc.scalar.copy(vt3[:, b, :, :].rearrange("p j c -> p (j c)"), o[:, HW:2 * HW]).then_inc(f_qkv_sb, 1)
            for b in range(B):
                act.wait_ge(f_max, b + 1)
                for i in range(NCH):
                    nc.scalar.activation(prob[:, b, i, :], bank[2 + b % 2][:, HW * i:HW * (i + 1)], ACT.Exp,
                                         bias=nmax[:, b, i:i + 1], accum_out=rsum[:, b, i:i + 1]).then_inc(f_exp, 1)
            for b in range(B):
                act.wait_ge(f_tp, b + 1)
                nc.scalar.copy(pt_sb[:, b, :, :].rearrange("p j s -> p (j s)"),
                               bank[4 + b % 2][:, :]).then_inc(f_pt_sb, 1)

        @block.vector
        def _(dve):
            for pad in (padh["x"], padl["x"]):
                nc.vector.memset(pad[:, :, 0:HP:HP - 1, :].bitcast(F32), 0.0)
                nc.vector.memset(pad[:, :, 1:1 + H, 0:WP:WP - 1].bitcast(F32), 0.0).then_inc(border, 2)

            def x_low(i):
                dve.wait_ge(x_hi, i + 1)
                nc.vector.tensor_tensor(inner(padl["x"], 2 * i, 2), flat4(x_sb[:, 2 * i:2 * i + 2, :]),
                                        inner(padh["x"], 2 * i, 2).bitcast(F32), ALU.subtract).then_inc(x_lo, 1)

            def w_low(n, i):
                dve.wait_ge(w_hi, 3 * W_ORDER.index(n) + i + 1)
                c = slice(third * i, third * (i + 1))
                nc.vector.tensor_tensor(wl[n][:, c], ws[n][:, c], wh[n][:, c].bitcast(F32),
                                        ALU.subtract).then_inc(w_lo, 1)

            x_low(0)
            for i in range(3):
                w_low("sam", i)
            x_low(1)
            dve.wait_ge(d_early, 16)
            nc.vector.tensor_scalar(bn_tmp[:, 0, :], p0("bn_var"), 1e-5, None, ALU.add).then_inc(bn_var, 1)
            dve.wait_ge(bn_std, 1)
            nc.vector.reciprocal(bn_tmp[:, 2, :], bn_tmp[:, 1, :]).then_inc(bn_step, 1)
            dve.wait_ge(bn_step, 1)
            nc.vector.tensor_tensor(bn_inv[:, :], bn_tmp[:, 2, :], p0("bn_scale"), ALU.mult).then_inc(bn_step, 1)
            dve.wait_ge(bn_step, 2)
            nc.vector.tensor_tensor(bn_tmp[:, 3, :], bn_inv[:, :], p0("bn_mean"), ALU.mult).then_inc(bn_step, 1)
            dve.wait_ge(bn_step, 3)
            nc.vector.tensor_tensor(bn_shift[:, :], p0("bn_bias"), bn_tmp[:, 3, :], ALU.subtract).then_inc(bn_step, 1)
            for n in ("cam", "out_s", "out_c"):
                for i in range(3):
                    w_low(n, i)

            for t in range(B + 4):
                if 0 <= t - 2 < B:
                    b = t - 2
                    dve.wait_ge(s_exp, NCH * (b + 1))
                    nc.vector.reciprocal(rinv[:, b, :], rsum[:, b, :]).then_inc(s_rinv, 1)
                    dve.wait_ge(s_rinv, b + 1)
                    for i in range(NCH):
                        nc.vector.tensor_scalar(prob[:, b, i, :], prob[:, b, i, :], rinv[:, b, i:i + 1], None,
                                                ALU.mult).then_inc(s_norm, 1)
                if t < B:
                    dve.wait_ge(s_proj, t + 1)
                    if t >= 2:
                        dve.wait_ge(s_score, t - 1)
                    nc.vector.tensor_scalar(q_sb[:, t % 2, :], bank[4][0:L, 0:HW], 0.25, None, ALU.mult)
                    nc.vector.tensor_copy(k_sb[:, t % 2, :], bank[4][KCOL:KCOL + L, 0:HW])
                    nc.vector.tensor_copy(vt_sb[:, t, :, :].rearrange("p j c -> p (j c)"),
                                          bank[4][:, HW:2 * HW]).then_inc(s_qkv_sb, 1)
                if 0 <= t - 1 < B:
                    b = t - 1
                    dve.wait_ge(s_score, b + 1)
                    nc.vector.tensor_reduce(nmax[:, b, :], bank[5][:, :].rearrange("p (i s) -> p i s", i=NCH), AX.X,
                                            ALU.max, negate=True).then_inc(s_max, 1)
                if 0 <= t - 4 < B:
                    b = t - 4
                    dve.wait_ge(s_hi, b + 1)
                    nc.vector.tensor_tensor(inner(padl["s"], b), flat4(att_s[:, b:b + 1, :]),
                                            inner(padh["s"], b).bitcast(F32), ALU.subtract).then_inc(s_lo, 1)
                if 0 <= t - 3 < B:
                    b = t - 3
                    dve.wait_ge(s_av, b + 1)
                    dve.wait_ge(xs_done, b // 2 + 1)
                    nc.vector.scalar_tensor_tensor(att_s[:, b, :], bank[7][:, 0:HW], p0("gam_sam"), xs[:, b, :],
                                                   ALU.mult, ALU.add).then_inc(s_att, 1)
            for t in range(B + 4):
                if 0 <= t - 2 < B:
                    b = t - 2
                    dve.wait_ge(c_exp, b + 1)
                    nc.vector.reciprocal(cinv[:, b:b + 1], csum[:, b:b + 1]).then_inc(c_rinv, 1)
                    dve.wait_ge(c_rinv, b + 1)
                    nc.vector.tensor_scalar(cprob[:, b, :], cprob[:, b, :], cinv[:, b:b + 1], None,
                                            ALU.mult).then_inc(c_norm, 1)
                if t < B:
                    dve.wait_ge(c_yt, t + 1)
                    nc.vector.tensor_copy(yt_sb[:, t, :, :].rearrange("p j c -> p (j c)"),
                                          bank[4][:, 0:NCH * C]).then_inc(c_yt_sb, 1)
                if 0 <= t - 1 < B:
                    b = t - 1
                    dve.wait_ge(c_gram, b + 1)
                    nc.vector.tensor_reduce(cmax[:, b:b + 1], bank[5][:, 0:C], AX.X, ALU.max).then_inc(c_max, 1)
                    dve.wait_ge(c_max, b + 1)
                    nc.vector.tensor_scalar(cnm[:, b:b + 1], cmax[:, b:b + 1], -1.0 / 16, None,
                                            ALU.mult).then_inc(c_nm, 1)
                if 0 <= t - 4 < B:
                    b = t - 4
                    dve.wait_ge(c_hi, b + 1)
                    nc.vector.tensor_tensor(inner(padl["c"], b), flat4(att_c[:, b:b + 1, :]),
                                            inner(padh["c"], b).bitcast(F32), ALU.subtract).then_inc(c_lo, 1)
                if 0 <= t - 3 < B:
                    b = t - 3
                    dve.wait_ge(c_av, b + 1)
                    dve.wait_ge(xc_done, b // 2 + 1)
                    nc.vector.scalar_tensor_tensor(att_c[:, b, :], bank[7][:, 0:HW], p0("gam_cam"), xc[:, b, :],
                                                   ALU.mult, ALU.add).then_inc(c_att, 1)

            dve.wait_ge(d_late, 16)
            a = LATE_AT["cm1_b"][0]
            nc.vector.tensor_scalar(thr[:, :], par1[:, a:a + 3], -float(HW), None, ALU.mult).then_inc(prep, 1)
            a = LATE_AT["ca_bh"][0]
            nc.vector.tensor_scalar(hb[:, :], par1[:, a:a + 2], 0.5, None, ALU.mult).then_inc(prep, 1)
            nc.vector.tensor_scalar(gsc[:, 0:1], p1("gam_sa"), 0.25 * float(C) ** -0.5, None,
                                    ALU.mult).then_inc(prep, 1)
            nc.vector.tensor_scalar(gsc[:, 1:2], p1("gam_moca"), 0.25, None, ALU.mult).then_inc(prep, 1)
            nc.vector.tensor_tensor(gbv[:, :], p1("gam3"), p1("bv"), ALU.mult).then_inc(prep, 1)

            dve.wait_ge(m_logit, 1)
            dve.wait_ge(zeroed, 2)
            nc.vector.tensor_scalar(mpad[:, 1:1 + H, 1:1 + W], bank[2][:, 0:HW].rearrange("p (h w) -> p h w", h=H),
                                    p1("sm_b"), 0.0, ALU.add, ALU.is_gt).then_inc(m_step, 1)
            dve.wait_ge(m_step, 1)
            nc.vector.tensor_tensor(mrow[:, 0, :, :], mpad[:, :, 0:W], mpad[:, :, 1:1 + W], ALU.max).then_inc(m_step, 1)
            dve.wait_ge(m_step, 2)
            nc.vector.tensor_tensor(mrow[:, 1, :, :], mrow[:, 0, :, :], mpad[:, :, 2:2 + W], ALU.max).then_inc(m_step, 1)
            dve.wait_ge(m_step, 3)
            nc.vector.tensor_tensor(mdil[:, 0, :, :], mrow[:, 1, 0:H, :], mrow[:, 1, 1:1 + H, :],
                                    ALU.max).then_inc(m_step, 1)
            dve.wait_ge(m_step, 4)
            nc.vector.tensor_tensor(mdil[:, 1, :, :], mdil[:, 0, :, :], mrow[:, 1, 2:2 + H, :],
                                    ALU.max).then_inc(m_step, 1)
            dve.wait_ge(cm1_logit, 1)
            dve.wait_ge(prep, 1)
            nc.vector.tensor_scalar(cm[:, 0:1], bank[4][:, 0:1], thr[:, 0:1], None, ALU.is_gt).then_inc(cm1_done, 1)
            dve.wait_ge(cm1_done, 1)
            dve.wait_ge(m_step, 5)
            dve.wait_ge(h1_relu, 1)
            nc.vector.scalar_tensor_tensor(hpad[:, 1:1 + H, 1:1 + W], hr[:, 0, :, :], cm[:, 0:1], mdil[:, 1, :, :],
                                           ALU.mult, ALU.mult, accum_out=pool2[:, 0:1]).then_inc(h1_done, 1)
            nc.vector.tensor_copy(mflat[:, :, :], mpad[:, 1:1 + H, 1:1 + W]).then_inc(m_lines, 1)
            nc.vector.tensor_reduce(linem[:, 0, :], mpad[:, 1:1 + H, 1:1 + W], AX.X, ALU.add).then_inc(m_lines, 1)
            nc.vector.tensor_reduce(linem[:, 1, :], mpad[:, 1:1 + H, 1:1 + W].rearrange("p h w -> p w h"), AX.X,
                                    ALU.add).then_inc(m_lines, 1)
            dve.wait_ge(cm2_logit, 1)
            nc.vector.tensor_scalar(cm[:, 1:2], bank[6][:, 0:1], thr[:, 1:2], None, ALU.is_gt).then_inc(cm2_done, 1)
            dve.wait_ge(cm2_done, 1)
            dve.wait_ge(m_lines, 1)
            dve.wait_ge(h2_relu, 1)
            nc.vector.scalar_tensor_tensor(h2[:, :, :], hr[:, 1, :, :], cm[:, 1:2], mflat[:, :, :], ALU.mult,
                                           ALU.mult, accum_out=pool2[:, 1:2]).then_inc(h2_done, 1)
            dve.wait_ge(h2_done, 1)
            nc.vector.tensor_scalar(pool3g[:, :], p1("group"), pool2[:, 1:2], None, ALU.mult).then_inc(h2_pool, 1)
            nc.vector.tensor_reduce(lineh[:, 0, :], h2[:, :, :], AX.X, ALU.add).then_inc(h2_lines, 1)
            nc.vector.tensor_reduce(lineh[:, 1, :], h2[:, :, :].rearrange("p h w -> p w h"), AX.X,
                                    ALU.add).then_inc(h2_lines, 1)
            dve.wait_ge(cm3_logit, 1)
            nc.vector.tensor_scalar(cm3[:, :], bank[7][:, 0:B], thr[:, 2:3], None, ALU.is_gt).then_inc(cm3_done, 1)
            dve.wait_ge(cm3_done, 1)
            nc.vector.tensor_scalar(cm3s[:, :], cm3[:, :], 1.0 / W, None, ALU.mult).then_inc(cm3_done, 1)
            dve.wait_ge(cm3_done, 2)
            dve.wait_ge(line_mm, 1)
            nc.vector.tensor_tensor(yin[:, :, :, :].rearrange("p b i h -> p b (i h)"),
                                    bank[6][:, 0:B * 2 * H].rearrange("p (b l) -> p b l", b=B),
                                    cm3s[:, :].unsqueeze(2).broadcast_to([P, B, 2 * H]), ALU.mult).then_inc(yin_done, 1)
            f = lambda t: t[:, :, :, :].rearrange("p b i h -> p (b i h)")
            dve.wait_ge(y_mm, 1)
            nc.vector.tensor_scalar(f(yb), bank[2][0:MIP, 0:B * 2 * H], p1("ca_b1", MIP), None,
                                    ALU.add).then_inc(y_step, 1)
            dve.wait_ge(y_step, 1)
            nc.vector.tensor_scalar(f(yr), f(yb), 3.0, 0.0, ALU.add, ALU.max).then_inc(y_step, 1)
            dve.wait_ge(y_step, 2)
            nc.vector.scalar_tensor_tensor(f(ys), f(yr), 6.0, f(yb), ALU.min, ALU.mult).then_inc(y_step, 1)
            dve.wait_ge(gate_tanh, 2)
            nc.vector.tensor_scalar(gate1[:, :, :, :].rearrange("p i b h -> p (i b h)"),
                                    gate[:, :, :, :].rearrange("p i b h -> p (i b h)"), 1.0, None,
                                    ALU.add).then_inc(gate_done, 1)
            dve.wait_ge(gate_done, 1)
            nc.vector.scalar_tensor_tensor(gate[:, 0, :, :], gate1[:, 0, :, :], 0.25,
                                           cm3[:, :].unsqueeze(2).broadcast_to([P, B, H]), ALU.mult,
                                           ALU.mult).then_inc(gate_done, 1)
            dve.wait_ge(gate_done, 2)
            dve.wait_ge(h3_mm, 2)
            for b in range(B):
                nc.vector.tensor_tensor(t1[:, b, :, :],
                                        bank[b // 2][:, HW * (b % 2):HW * (b % 2 + 1)].rearrange("p (h w) -> p h w", h=H),
                                        gate[:, 0, b, :].unsqueeze(2).broadcast_to([P, H, W]),
                                        ALU.mult).then_inc(t1_done, 1)
                dve.wait_ge(t1_done, b + 1)
                nc.vector.tensor_tensor(t2[:, b, :, :], t1[:, b, :, :],
                                        gate1[:, 1, b, :].unsqueeze(1).broadcast_to([P, H, W]),
                                        ALU.mult).then_inc(t2_done, 1)

            for b in range(B):
                dve.wait_ge(a_score, b + 1)
                nc.vector.tensor_reduce(nmax[:, b, :], bank[2 + b % 2][:, :].rearrange("p (i s) -> p i s", i=NCH), AX.X,
                                        ALU.max, negate=True).then_inc(a_max, 1)
            for b in range(B):
                dve.wait_ge(a_exp, NCH * (b + 1))
                nc.vector.reciprocal(rinv[:, b, :], rsum[:, b, :]).then_inc(a_rinv, 1)
                dve.wait_ge(a_tp, b + 1)
                nc.vector.tensor_copy(pt_sb[:, b, :, :].rearrange("p j s -> p (j s)"),
                                      bank[4 + b % 2][:, :]).then_inc(a_pt_sb, 1)
            sel = p1("sel16").unsqueeze(2).broadcast_to([P, L, L])
            for b in range(B):
                dve.wait_ge(a_av, b + 1)
                dve.wait_ge(a_rinv, b + 1)
                for i in range(NCH):
                    nc.vector.scalar_tensor_tensor(wide[:, b, i, :, :],
                                                   bank[6 + b % 2][:, L * i:L * (i + 1)].unsqueeze(1).broadcast_to([P, L, L]),
                                                   rinv[:, b, i:i + 1], sel, ALU.mult, ALU.mult).then_inc(a_wide, 1)
                dve.wait_ge(a_o, b + 1)
                nc.vector.scalar_tensor_tensor(sa[:, b, :], bank[6 + b % 2][:, HW:2 * HW], gsc[:, 0:1], x2[:, b, :],
                                               ALU.mult, ALU.add).then_inc(a_done, 1)
            for b in range(B):
                dve.wait_ge(e_score, b + 1)
                nc.vector.tensor_reduce(nmax2[:, b, :],
                                        bank[2 + b % 2][:, 0:NCH * NCON].rearrange("p (i s) -> p i s", i=NCH), AX.X,
                                        ALU.max, negate=True).then_inc(e_max, 1)
            for b in range(B):
                dve.wait_ge(e_exp, NCH * (b + 1))
                nc.vector.reciprocal(rinv2[:, b, :], rsum2[:, b, :]).then_inc(e_rinv, 1)
            for b in range(B):
                dve.wait_ge(e_av, b + 1)
                dve.wait_ge(e_rinv, b + 1)
                for i in range(NCH):
                    nc.vector.scalar_tensor_tensor(wide2[:, b, i, :, :],
                                                   bank[6 + b % 2][:, L * i:L * (i + 1)].unsqueeze(1).broadcast_to([P, L, L]),
                                                   rinv2[:, b, i:i + 1], sel, ALU.mult, ALU.mult).then_inc(e_wide, 1)
                dve.wait_ge(e_o, b + 1)
                nc.vector.scalar_tensor_tensor(x3[:, b, :], bank[6 + b % 2][:, HW:2 * HW], gsc[:, 1:2], sa[:, b, :],
                                               ALU.mult, ALU.add).then_inc(e_done, 1)
            for b in range(B):
                dve.wait_ge(e_done, b + 1)
                nc.vector.tensor_scalar(x3b[:, b, :], x3[:, b, :], gbv[:, 0:1], None, ALU.add).then_inc(f_xb, 1)
                dve.wait_ge(f_score, b + 1)
                nc.vector.tensor_reduce(nmax[:, b, :], bank[2 + b % 2][:, :].rearrange("p (i s) -> p i s", i=NCH), AX.X,
                                        ALU.max, negate=True).then_inc(f_max, 1)
            for b in range(B):
                dve.wait_ge(f_exp, NCH * (b + 1))
                nc.vector.reciprocal(rinv[:, b, :], rsum[:, b, :]).then_inc(f_rinv, 1)
                dve.wait_ge(f_rinv, b + 1)
                for i in range(NCH):
                    nc.vector.tensor_scalar(prob[:, b, i, :], prob[:, b, i, :], rinv[:, b, i:i + 1], None,
                                            ALU.mult).then_inc(f_norm, 1)
            for b in range(B):
                dve.wait_ge(f_av, b + 1)
                dve.wait_ge(f_xb, b + 1)
                nc.vector.scalar_tensor_tensor(y[:, b, :], bank[6 + b % 2][:, 0:HW], p1("gam3"), x3b[:, b, :],
                                               ALU.mult, ALU.add).then_inc(f_done, 1)

        @block.tensor
        def _(pe):
            mm = nc.tensor.matmul

            def tap(n, pad, o, half, t, first, last):
                dy, dx = TAPS[t]
                view = lambda p: p[:, 2 * half:2 * half + 2, dy:dy + H, dx:dx + W]
                ov = o[:, :].rearrange("p (b h w) -> p b h w", b=2, h=H)
                c = slice(C * t, C * (t + 1))
                mm(ov, wh[n][:, c], view(padh[pad]), start=first, stop=False, skip_group_check=True)
                mm(ov, wh[n][:, c], view(padl[pad]), start=False, stop=False, skip_group_check=True)
                return mm(ov, wl[n][:, c], view(padh[pad]), start=False, stop=last, skip_group_check=True)

            def weights_split(n, t):
                pe.wait_ge(w_lo, 3 * W_ORDER.index(n) + t // 3 + 1)

            pe.wait_ge(border, 4)
            for half in range(2):
                pe.wait_ge(x_lo, half + 1)
                for t in range(NT):
                    if half == 0 and t % 3 == 0:
                        weights_split("sam", t)
                    m = tap("sam", "x", bank[half], half, t, t == 0, t == NT - 1)
                m.then_inc(sam_conv, 1)

            def cam_taps(k0, k1):
                for k in range(k0, k1):
                    half, t = divmod(k, NT)
                    if t % 3 == 0:
                        weights_split("cam", t)
                    m = tap("cam", "x", bank[2 + half], half, t, t == 0, t == NT - 1)
                    if t == NT - 1:
                        m.then_inc(cam_conv, 1)

            pe.wait_ge(d_early, 16)
            done = 0
            for t in range(B + 3):
                if 0 <= t - 2 < B:
                    b = t - 2
                    pe.wait_ge(s_norm, NCH * (b + 1))
                    if b >= 1:
                        pe.wait_ge(s_pt_sb, b)
                    for i in range(NCH):
                        for j in range(NCH):
                            m = nc.tensor.transpose(bank[6][:, HW * j + P * i:HW * j + P * (i + 1)],
                                                    prob[:, b, i, P * j:P * (j + 1)], ident)
                    m.then_inc(s_tp, 1)
                if t < B:
                    pe.wait_ge(xs_done, t // 2 + 1)
                    if t >= 1:
                        pe.wait_ge(s_qkv_sb, t)
                    mm(bank[4][0:KCOL + L, 0:HW], p0("w_qk"), xs[:, t, :], start=True, stop=True)
                    for j in range(NCH):
                        m = mm(bank[4][:, HW + C * j:HW + C * (j + 1)], xs[:, t, P * j:P * (j + 1)], p0("w_v"),
                               start=True, stop=True)
                    m.then_inc(s_proj, 1)
                cam_taps(done, min(18, done + 2))
                done = min(18, done + 2)
                if 0 <= t - 1 < B:
                    b = t - 1
                    pe.wait_ge(s_qkv_sb, b + 1)
                    if b >= 1:
                        pe.wait_ge(s_exp, NCH * b)
                    for i in range(NCH):
                        m = mm(bank[5][:, HW * i:HW * (i + 1)], q_sb[:, b % 2, P * i:P * (i + 1)], k_sb[:, b % 2, :],
                               start=True, stop=True)
                    m.then_inc(s_score, 1)
                if 0 <= t - 3 < B:
                    b = t - 3
                    pe.wait_ge(s_pt_sb, b + 1)
                    if b >= 1:
                        pe.wait_ge(s_att, b)
                    for j in range(NCH):
                        m = mm(bank[7][:, 0:HW], vt_sb[:, b, j, :], pt_sb[:, b, j, :], start=(j == 0),
                               stop=(j == NCH - 1))
                    m.then_inc(s_av, 1)
                cam_taps(done, min(18, done + 1))
                done = min(18, done + 1)

            def out_taps(k0, k1):
                for k in range(k0, k1):
                    half, t = divmod(k, NT)
                    if t == 0:
                        pe.wait_ge(border, 12)
                        pe.wait_ge(s_lo, 2 * half + 2)
                    if t % 3 == 0:
                        weights_split("out_s", t)
                    tap("out_s", "s", bank[half], half, t, t == 0, False)

            done = 0
            for t in range(B + 3):
                if 0 <= t - 2 < B:
                    b = t - 2
                    pe.wait_ge(c_norm, b + 1)
                    if b >= 1:
                        pe.wait_ge(c_pt_sb, b)
                    nc.tensor.transpose(bank[6][:, 0:C], cprob[:, b, :], ident).then_inc(c_tp, 1)
                if t < B:
                    pe.wait_ge(xc_done, t // 2 + 1)
                    if t >= 1:
                        pe.wait_ge(c_yt_sb, t)
                    for j in range(NCH):
                        m = nc.tensor.transpose(bank[4][:, C * j:C * (j + 1)], xc[:, t, P * j:P * (j + 1)], ident)
                    m.then_inc(c_yt, 1)
                out_taps(done, min(18, done + 2))
                done = min(18, done + 2)
                if 0 <= t - 1 < B:
                    b = t - 1
                    pe.wait_ge(c_yt_sb, b + 1)
                    if b >= 1:
                        pe.wait_ge(c_exp, b)
                    for j in range(NCH):
                        m = mm(bank[5][:, 0:C], yt_sb[:, b, j, :], yt_sb[:, b, j, :], start=(j == 0),
                               stop=(j == NCH - 1))
                    m.then_inc(c_gram, 1)
                if 0 <= t - 3 < B:
                    b = t - 3
                    pe.wait_ge(c_pt_sb, b + 1)
                    if b >= 1:
                        pe.wait_ge(c_att, b)
                    mm(bank[7][:, 0:HW], cpt[:, b, :], xc[:, b, :], start=True, stop=True).then_inc(c_av, 1)
                out_taps(done, min(18, done + 1))
                done = min(18, done + 1)
            for half in range(2):
                pe.wait_ge(c_lo, 2 * half + 2)
                for t in range(NT):
                    if half == 0 and t % 3 == 0:
                        weights_split("out_c", t)
                    m = tap("out_c", "c", bank[half], half, t, False, t == NT - 1)
                m.then_inc(out_conv, 1)

            def window(name, b):
                a = LATE_AT[name][0] + WIN - WID * b
                return par1[:, a:a + P]

            pe.wait_ge(d_late, 16)
            for b in range(B):
                pe.wait_ge(x1_done, b + 1)
                m = mm(bank[2][:, 0:HW], window("sm_win", b), x1[:, b, :], start=(b == 0), stop=(b == B - 1))
                if b == B - 1:
                    m.then_inc(m_logit, 1)
                m = mm(bank[3][:, 0:HW], window("w1_win", b), x1[:, b, :], start=(b == 0), stop=(b == B - 1))
            m.then_inc(h1_conv, 1)
            for b in range(B):
                m = mm(bank[4][:, 0:1], window("cm1_win", b), pool1[:, b:b + 1], start=(b == 0), stop=(b == B - 1))
            m.then_inc(cm1_logit, 1)
            pe.wait_ge(spread, 4 * B)
            pe.wait_ge(h1_done, 1)
            mm(bank[6][:, 0:1], cm2bd[:, :], pool2[:, 0:1], start=True, stop=True).then_inc(cm2_logit, 1)
            for t, (dy, dx) in enumerate(TAPS):
                m = mm(bank[5][:, 0:HW].rearrange("p (h w) -> p h w", h=H), w2bd[:, t, :],
                       hpad[:, dy:dy + H, dx:dx + W], start=(t == 0), stop=(t == NT - 1))
            m.then_inc(h2_conv, 1)
            pe.wait_ge(h2_pool, 1)
            mm(bank[7][:, 0:B], p1("cm3_rep"), pool3g[:, :], start=True, stop=True).then_inc(cm3_logit, 1)
            pe.wait_ge(h2_lines, 2)
            pe.wait_ge(m_lines, 3)
            pe.wait_ge(cm2_done, 1)
            for b in range(B):
                o = bank[6][:, 2 * H * b:2 * H * (b + 1)]
                mm(o, w3z[:, b, :], lineh[:, :, :].rearrange("p i h -> p (i h)"), start=True, stop=False)
                m = mm(o, b3z[:, b, :], linem[:, :, :].rearrange("p i h -> p (i h)"), start=False, stop=True)
            m.then_inc(line_mm, 1)
            for b in range(B):
                o = bank[b // 2][:, HW * (b % 2):HW * (b % 2 + 1)]
                mm(o, b3z[:, b, :], mflat[:, :, :].rearrange("p h w -> p (h w)"), start=True, stop=False)
                m = mm(o, w3z[:, b, :], h2[:, :, :].rearrange("p h w -> p (h w)"), start=False, stop=True)
                if b == 1:
                    m.then_inc(h3_mm, 1)
                    pe.wait_ge(yin_done, 1)
                    mm(bank[2][0:MIP, 0:B * 2 * H], p1("ca_w1"), yin[:, :, :, :].rearrange("p b i h -> p (b i h)"),
                       start=True, stop=True).then_inc(y_mm, 1)
            m.then_inc(h3_mm, 1)
            pe.wait_ge(y_step, 3)
            mm(bank[3][:, 0:B * H].rearrange("p (b h) -> p b h", b=B), p1("ca_wh", MIP), ys[:, :, 0, :],
               start=True, stop=True)
            mm(bank[3][:, B * H:2 * B * H].rearrange("p (b h) -> p b h", b=B), p1("ca_ww", MIP), ys[:, :, 1, :],
               start=True, stop=True).then_inc(gate_mm, 1)

            pe.wait_ge(t1_done, B)
            for b in range(B):
                pe.wait_ge(x2_done, b + 1)
                if b >= 2:
                    pe.wait_ge(a_qk_sb, b - 1)
                mm(bank[b % 2][0:KCOL + L, 0:HW], p1("w_thph"), x2[:, b, :], start=True, stop=True)
                for j in range(NCH):
                    m = mm(bank[b % 2][:, HW + L * j:HW + L * (j + 1)], x2[:, b, P * j:P * (j + 1)], p1("w_g"),
                           start=True, stop=True)
                m.then_inc(a_proj, 1)
            for b in range(B):
                pe.wait_ge(a_qk_sb, b + 1)
                if b >= 2:
                    pe.wait_ge(a_exp, NCH * (b - 1))
                for i in range(NCH):
                    m = mm(bank[2 + b % 2][:, HW * i:HW * (i + 1)], th[:, b, P * i:P * (i + 1)], ph[:, b, :],
                           start=True, stop=True)
                m.then_inc(a_score, 1)
            for b in range(B):
                pe.wait_ge(a_exp, NCH * (b + 1))
                if b >= 2:
                    pe.wait_ge(a_pt_sb, b - 1)
                for i in range(NCH):
                    for j in range(NCH):
                        m = nc.tensor.transpose(bank[4 + b % 2][:, HW * j + P * i:HW * j + P * (i + 1)],
                                                prob[:, b, i, P * j:P * (j + 1)], ident)
                m.then_inc(a_tp, 1)
            for s in range(B + 1):
                if s < B:
                    b = s
                    pe.wait_ge(a_pt_sb, b + 1)
                    if b >= 2:
                        pe.wait_ge(a_done, b - 1)
                    for i in range(NCH):
                        for j in range(NCH):
                            m = mm(bank[6 + b % 2][:, L * i:L * (i + 1)], pt_sb[:, b, j, P * i:P * (i + 1)],
                                   gt[:, b, j, :], start=(j == 0), stop=(j == NCH - 1))
                    m.then_inc(a_av, 1)
                if s >= 1:
                    b = s - 1
                    pe.wait_ge(a_wide, NCH * (b + 1))
                    for i in range(NCH):
                        m = mm(bank[6 + b % 2][:, HW:2 * HW], p1("w_o_rep")[:, C * i:C * (i + 1)],
                               wide[:, b, i, :, :].rearrange("p l m -> p (l m)"), start=(i == 0), stop=(i == NCH - 1))
                    m.then_inc(a_o, 1)
            for b in range(B):
                pe.wait_ge(a_done, b + 1)
                if b >= 2:
                    pe.wait_ge(e_sb, b - 1)
                mm(bank[b % 2][0:L, 0:HW], p1("w_thph")[:, 0:L], sa[:, b, :], start=True, stop=True).then_inc(e_proj, 1)
            for b in range(B):
                pe.wait_ge(e_sb, b + 1)
                if b >= 2:
                    pe.wait_ge(e_exp, NCH * (b - 1))
                for i in range(NCH):
                    m = mm(bank[2 + b % 2][:, NCON * i:NCON * (i + 1)], enc[:, b, P * i:P * (i + 1)], p1("con_t", L),
                           start=True, stop=True)
                m.then_inc(e_score, 1)
            for b in range(B):
                pe.wait_ge(e_exp, NCH * (b + 1))
                if b >= 2:
                    pe.wait_ge(e_pt_sb, b - 1)
                for i in range(NCH):
                    m = nc.tensor.transpose(bank[4 + b % 2][0:NCON, P * i:P * (i + 1)], prob2[:, b, i, :], ident)
                m.then_inc(e_tp, 1)
            for s in range(B + 1):
                if s < B:
                    b = s
                    pe.wait_ge(e_pt_sb, b + 1)
                    if b >= 2:
                        pe.wait_ge(e_done, b - 1)
                    for i in range(NCH):
                        m = mm(bank[6 + b % 2][:, L * i:L * (i + 1)], pt2[:, b, P * i:P * (i + 1)], p1("con", NCON),
                               start=True, stop=True)
                    m.then_inc(e_av, 1)
                if s >= 1:
                    b = s - 1
                    pe.wait_ge(e_wide, NCH * (b + 1))
                    for i in range(NCH):
                        m = mm(bank[6 + b % 2][:, HW:2 * HW], p1("w_o_rep")[:, C * i:C * (i + 1)],
                               wide2[:, b, i, :, :].rearrange("p l m -> p (l m)"), start=(i == 0), stop=(i == NCH - 1))
                    m.then_inc(e_o, 1)
            for b in range(B):
                pe.wait_ge(e_done, b + 1)
                if b >= 2:
                    pe.wait_ge(f_qkv_sb, b - 1)
                mm(bank[b % 2][0:KCOL + L, 0:HW], p1("w_qk3"), x3[:, b, :], start=True, stop=True)
                for j in range(NCH):
                    m = mm(bank[b % 2][:, HW + C * j:HW + C * (j + 1)], x3[:, b, P * j:P * (j + 1)], p1("w_v3"),
                           start=True, stop=True)
                m.then_inc(f_proj, 1)
            for b in range(B):
                pe.wait_ge(f_qkv_sb, b + 1)
                if b >= 2:
                    pe.wait_ge(f_exp, NCH * (b - 1))
                for i in range(NCH):
                    m = mm(bank[2 + b % 2][:, HW * i:HW * (i + 1)], q3[:, b, P * i:P * (i + 1)], k3[:, b, :],
                           start=True, stop=True)
                m.then_inc(f_score, 1)
            for b in range(B):
                pe.wait_ge(f_norm, NCH * (b + 1))
                if b >= 2:
                    pe.wait_ge(f_pt_sb, b - 1)
                for i in range(NCH):
                    for j in range(NCH):
                        m = nc.tensor.transpose(bank[4 + b % 2][:, HW * j + P * i:HW * j + P * (i + 1)],
                                                prob[:, b, i, P * j:P * (j + 1)], ident)
                m.then_inc(f_tp, 1)
            for b in range(B):
                pe.wait_ge(f_pt_sb, b + 1)
                if b >= 2:
                    pe.wait_ge(f_done, b - 1)
                for j in range(NCH):
                    m = mm(bank[6 + b % 2][:, 0:HW], vt3[:, b, j, :], pt_sb[:, b, j, :], start=(j == 0),
                           stop=(j == NCH - 1))
                m.then_inc(f_av, 1)


def kernel(**inputs):
    import numpy as np
    import concourse.bacc as bacc
    from concourse.bass_utils import run_bass_kernel_spmd

    a = {k: np.asarray(v) for k, v in inputs.items()}
    g0 = lambda n: a["L0_conv_" + n]
    g1 = lambda n: a["L1_conv_" + n]
    g2 = lambda n: a["L2_conv_" + n]
    g3 = lambda n: a["L3_conv_" + n]
    f32 = a["x"].dtype

    def taps(w):
        return np.transpose(w, (1, 2, 3, 0)).reshape(w.shape[1], -1)

    def pair(u, v):
        w = np.zeros((C, KCOL + L), f32)
        w[:, 0:L] = u.T
        w[:, KCOL:KCOL + L] = v.T
        return w

    def window(w):
        z = np.zeros((C, WIN), f32)
        return np.concatenate([z, w, z], axis=1)

    def pack(table, values):
        cols, width = columns(table)
        m = np.zeros((P, width), f32)
        for name, (at, w) in cols.items():
            v = np.asarray(values[name], f32)
            v = v.reshape(-1, w)
            m[0:v.shape[0], at:at + w] = v
        return m

    col = lambda v: np.reshape(v, (-1, 1))
    full = lambda v: np.broadcast_to(np.reshape(v, (1, 1)), (P, 1))
    four = lambda v: np.concatenate([v] * B, axis=0)

    early = pack(EARLY, {
        "bn_scale": np.stack([g0("bn_sam_scale"), g0("bn_cam_scale")], 1),
        "bn_bias": np.stack([g0("bn_sam_bias"), g0("bn_cam_bias")], 1),
        "bn_mean": np.stack([g0("bn_sam_mean"), g0("bn_cam_mean")], 1),
        "bn_var": np.stack([g0("bn_sam_var"), g0("bn_cam_var")], 1),
        "gam_sam": full(g0("gamma_sam")), "gam_cam": full(g0("gamma_cam")),
        "ident": np.eye(P, dtype=f32),
        "w_qk": pair(g0("w_qk")[0:L, :, 0, 0], g0("w_qk")[L:2 * L, :, 0, 0]),
        "w_v": g0("w_v")[:, :, 0, 0].T,
    })
    w2t = np.transpose(g1("w2"), (1, 2, 3, 0)).reshape(WID, NT * WID)
    sel16 = np.zeros((P, L), f32)
    sel16[np.arange(P), np.arange(P) % L] = 1
    group = np.zeros((P, B), f32)
    group[np.arange(P), np.arange(P) // WID] = 1
    late = pack(LATE, {
        "sm_b": full(g1("sm_b")), "b1": four(col(g1("b1"))), "b2": four(col(g1("b2"))),
        "cm1_b": four(col(g1("cm1_b"))), "cm2_b": four(col(g1("cm2_b"))), "cm3_b": col(g1("cm3_b")),
        "ca_b1": col(g1("ca_b1")), "ca_bh": col(g1("ca_bh")), "ca_bw": col(g1("ca_bw")),
        "gam_sa": full(g2("gamma_sa")), "gam_moca": full(g2("gamma_moca")), "gam3": full(g3("gamma")),
        "bq": col(g3("bq")), "bk": col(g3("bk")), "bv": col(g3("bv")),
        "group": group, "sel16": sel16,
        "sm_win": window(np.repeat(g1("sm_w").reshape(C, 1), WID, axis=1)),
        "w1_win": window(g1("w1")[:, :, 0, 0].T), "cm1_win": window(g1("cm1_w").T),
        "w2_rep": four(w2t), "cm2_rep": four(g1("cm2_w").T), "cm3_rep": four(g1("cm3_w").T),
        "w3_rep": four(g1("w3")[:, :, 0, 0].T), "b3_row": np.broadcast_to(g1("b3").reshape(1, C), (P, C)),
        "ca_w1": g1("ca_w1")[:, :, 0, 0].T, "ca_wh": g1("ca_wh")[:, :, 0, 0].T, "ca_ww": g1("ca_ww")[:, :, 0, 0].T,
        "w_thph": pair(g2("w_theta"), g2("w_phi")), "w_g": g2("w_g").T,
        "w_o_rep": np.concatenate(np.split(np.repeat(g2("w_o").T, HW // L, axis=0), NCH, axis=0), axis=1),
        "con_t": g2("concepts").T, "con": g2("concepts"),
        "w_qk3": pair(g3("Wq"), g3("Wk")), "w_v3": g3("Wv").T,
    })
    w_out = g0("w_out")
    arrays = {
        "x": a["x"],
        "w_sam": taps(g0("w_sam")), "w_cam": taps(g0("w_cam")),
        "w_out": np.concatenate([taps(w_out[:, 0:C]), taps(w_out[:, C:2 * C])], axis=1),
        "early": early, "late": late,
    }
    arrays = {k: np.ascontiguousarray(v) for k, v in arrays.items()}
    nc = bacc.Bacc("TRN2", target_bir_lowering=False, num_devices=1)
    args = [nc.dram_tensor(f"in_{k}", v.shape, mybir.dt.from_np(v.dtype), kind="ExternalInput").ap()
            for k, v in arrays.items()]
    out = nc.dram_tensor("out_0", a["x"].shape, F32, kind="ExternalOutput").ap()
    build(nc, *args, out)
    r = run_bass_kernel_spmd(nc, [{f"in_{k}": v for k, v in arrays.items()}], core_ids=[0])
    return r.results[0]["out_0"]
```

```python
from contextlib import ExitStack

import concourse.bass as bass
from concourse import mybir

F32 = mybir.dt.float32
F32R = mybir.dt.float32r
ALU = mybir.AluOpType
ACT = mybir.ActivationFunctionType
AX = mybir.AxisListType

B, C, H, W = 4, 128, 16, 16
HW = H * W
P = 128
HP, WP = H + 2, W + 2
TAPS = [(dy, dx) for dy in range(3) for dx in range(3)]
NT = len(TAPS)
L = 16
WID = 32
MIP = 16
NCON = 64
NCH = HW // P
QK_BANK = [4, 5, 0, 1]
GAP = 32
ST = 3 * GAP
START = 26
WIN = P - WID

EARLY = [("bn_scale", 2), ("bn_bias", 2), ("bn_mean", 2), ("bn_var", 2), ("gam_sam", 1), ("gam_cam", 1),
         ("ident", P)]
EARLY_SPLIT = [("w_q", ST), ("w_k", ST), ("w_v", C)]
LATE = [("sm_b", 1), ("b1", 1), ("b2", 1), ("cm1_b", 1), ("cm2_b", 1), ("cm3_b", 1), ("ca_b1", 1),
        ("ca_bh", 1), ("ca_bw", 1), ("gam_sa", 1), ("gam_moca", 1), ("gam3", 1), ("bq", 1), ("bk", 1),
        ("bv", 1), ("group", B), ("sel16", L), ("cm1_win", WIN + WID + WIN),
        ("w2_rep", NT * WID), ("cm2_rep", WID), ("cm3_rep", C), ("w3_rep", C), ("b3_row", C),
        ("ca_w1", MIP), ("ca_wh", C), ("ca_ww", C), ("con_t", NCON), ("con", L),
        ("w_o_rep", NCH * C)]
LATE_SPLIT = [("sm_win", WIN + WID + WIN), ("w1_win", WIN + WID + WIN),
              ("w_th", ST), ("w_ph", ST), ("w_g", L),
              ("w_q3", ST), ("w_k3", ST), ("w_v3", C)]


def columns(table):
    at, out = 0, {}
    for name, width in table:
        out[name] = (at, width)
        at += width
    return out, at


EARLY_AT, EARLY_W = columns(EARLY + EARLY_SPLIT)
LATE_AT, LATE_W = columns(LATE + LATE_SPLIT)
EARLY_KEEP = columns(EARLY)[1]
LATE_KEEP = columns(LATE)[1]


def build(nc, x, w_sam, w_cam, w_out, early, late, out):
    with ExitStack() as ctx:
        def sb(name, shape, dt=F32):
            return ctx.enter_context(nc.sbuf_tensor(name, shape, dt))

        def sem(name):
            return ctx.enter_context(nc.semaphore(name))

        bank = [ctx.enter_context(nc.psum_tensor(f"bank{i}", [P, 512], F32)) for i in range(8)]

        par0 = sb("par0", [P, EARLY_W])
        par1 = sb("par1", [P, LATE_W])

        def p0(name, rows=P):
            a, w = EARLY_AT[name]
            return par0[0:rows, a:a + w]

        def p1(name, rows=P):
            a, w = LATE_AT[name]
            return par1[0:rows, a:a + w]

        ident = p0("ident")
        par0_p = [sb(f"par0_{n}", [P, EARLY_W - EARLY_KEEP], F32R) for n in ("hi", "lo")]
        par1_p = [sb(f"par1_{n}", [P, LATE_W - LATE_KEEP], F32R) for n in ("hi", "lo")]

        def parts(name):
            if name in EARLY_AT:
                a, w = EARLY_AT[name]
                return [t[:, a - EARLY_KEEP:a - EARLY_KEEP + w] for t in par0_p]
            a, w = LATE_AT[name]
            return [t[:, a - LATE_KEEP:a - LATE_KEEP + w] for t in par1_p]

        W_ORDER = ["sam", "cam", "out_s", "out_c"]
        w_raw = sb("w_raw", [P, 2, NT * C])
        w_hi = sb("w_hi", [P, len(W_ORDER), NT * C], F32R)
        w_lo = sb("w_lo", [P, len(W_ORDER), NT * C], F32R)
        ws = {n: w_raw[:, i % 2, :] for i, n in enumerate(W_ORDER)}
        wh = {n: w_hi[:, i, :] for i, n in enumerate(W_ORDER)}
        wl = {n: w_lo[:, i, :] for i, n in enumerate(W_ORDER)}
        x_sb = sb("x_sb", [P, B, HW])
        padh = {n: sb(f"padh_{n}", [P, B, HP, WP], F32R) for n in ("x", "s", "c")}
        padl = {n: sb(f"padl_{n}", [P, B, HP, WP], F32R) for n in ("x", "s", "c")}

        bn_inv = sb("bn_inv", [P, 2])
        bn_shift = sb("bn_shift", [P, 2])
        bn_tmp = sb("bn_tmp", [P, 4, 2])
        xs = sb("xs", [P, B, HW])
        xc = sb("xc", [P, B, HW])
        map_a = [sb(f"map_a{i}", [P, B, HW], F32R) for i in range(2)]
        map_b = [sb(f"map_b{i}", [P, B, HW], F32R) for i in range(2)]
        qst = sb("qst", [ST, B, HW], F32R)
        kst = sb("kst", [ST, B, HW], F32R)
        vt = [sb(f"vt{i}", [P, B, NCH, C], F32R) for i in range(2)]
        ptp = [sb(f"ptp{i}", [P, B, NCH, HW], F32R) for i in range(2)]
        prob = sb("prob", [P, B, NCH, HW])
        raw = w_raw[:, :, :].rearrange("p a n -> p (a n)")
        pt_sb = raw[:, 0:B * NCH * HW].rearrange("p (b j s) -> p b j s", b=B, j=NCH)
        nmax = sb("nmax", [P, B, NCH])
        rsum = sb("rsum", [P, B, NCH])
        rinv = sb("rinv", [P, B, NCH])
        cprob = prob[:, :, 0, 0:C]
        cmax = sb("cmax", [P, B])
        cnm = sb("cnm", [P, B])
        csum = sb("csum", [P, B])
        cinv = sb("cinv", [P, B])
        att_s = sb("att_s", [P, B, HW])
        att_c = sb("att_c", [P, B, HW])

        x1 = sb("x1", [P, B, HW])
        pool1 = sb("pool1", [P, B])
        w2bd = [w[:, 0, :].rearrange("p (t o) -> p t o", t=NT) for w in (w_hi, w_lo)]
        cm2bd = sb("cm2bd", [P, P])
        w3z = sb("w3z", [P, B, C])
        b3z = sb("b3z", [P, B, C])
        spare = [p[:, :, :, :].rearrange("p b h w -> p (b h w)") for p in (padh["x"], padl["x"])]
        w3p = [t[:, 0:B * C].rearrange("p (b c) -> p b c", b=B) for t in spare]
        b3p = [t[:, B * C:2 * B * C].rearrange("p (b c) -> p b c", b=B) for t in spare]
        thr = sb("thr", [P, 3])
        hb = sb("hb", [P, 2])
        cm = sb("cm", [P, 2])
        mpad = sb("mpad", [P, HP, WP])
        mflat = sb("mflat", [P, H, W], F32R)
        mrow = sb("mrow", [P, 2, HP, W])
        mdil = sb("mdil", [P, 2, H, W])
        hr = sb("hr", [P, 2, H, W])
        h1 = sb("h1", [P, H, W])
        hpad = [sb(f"hpad{i}", [P, HP, WP], F32R) for i in range(2)]
        h2 = sb("h2", [P, H, W])
        h2p = [sb(f"h2p{i}", [P, H, W], F32R) for i in range(2)]
        pool2 = sb("pool2", [P, 2])
        pool3g = sb("pool3g", [P, B])
        cm3 = sb("cm3", [P, B])
        cm3s = sb("cm3s", [P, B])
        linem = sb("linem", [P, 2, H])
        lineh = sb("lineh", [P, 2, H])
        yin = sb("yin", [P, B, 2, H])
        yb = sb("yb", [MIP, B, 2, H])
        yr = sb("yr", [MIP, B, 2, H])
        ys = sb("ys", [MIP, B, 2, H])
        gate = sb("gate", [P, 2, B, H])
        gate1 = sb("gate1", [P, 2, B, H])
        t1 = xs[:, :, :].rearrange("p b (h w) -> p b h w", h=H)
        t2 = xc[:, :, :].rearrange("p b (h w) -> p b h w", h=H)
        t3 = att_s
        x2 = xc

        gt = sb("gt", [P, B, NCH, L])
        gsc = sb("gsc", [P, 2])
        con_st = sb("con_st", [ST, NCON], F32R)
        wide = prob
        sa = xs
        prob2 = prob[:, :, :, 0:NCON]
        pt2 = pt_sb[0:NCON, :, 0, :]
        nmax2 = sb("nmax2", [P, B, NCH])
        rsum2 = sb("rsum2", [P, B, NCH])
        rinv2 = sb("rinv2", [P, B, NCH])
        x3 = x1

        gbv = sb("gbv", [P, 1])
        vt3 = att_s
        x3b = att_c
        y = x_sb

        d_x = [sem(f"d_x{i}") for i in range(2)]
        d_w = [[sem(f"d_w{k}_{i}") for i in range(3)] for k in range(2)]
        d_early, d_late, d_y = sem("d_early"), sem("d_late"), sem("d_y")
        ev = {n: sem(n) for n in (
            "border_x border x_hi x_lo w_hi w_lo par0_hi par0_lo par1_hi par1_lo bn_var bn_std bn_step sam_conv cam_conv "
            "out_conv xs_done xs_hi xs_lo xc_done xc_hi xc_lo x1_done x1_hi x1_lo "
            "s_proj s_vt s_qk_hi s_qk_lo s_vt_hi s_vt_lo s_score s_max s_exp s_rinv s_norm s_tp s_pt_hi s_pt_lo "
            "s_av s_att s_hi s_lo "
            "c_yt c_yt_hi c_yt_lo c_gram c_max c_nm c_exp c_rinv c_norm c_tp c_pt_hi c_pt_lo c_av c_att c_hi c_lo "
            "zeroed spread_raw spread_hi spread prep m_logit h1_conv cm1_logit m_step m_lines h1_relu h1_done h1_hi "
            "h1_lo cm1_done h2_conv cm2_logit h2_relu h2_done h2_hi h2_lo cm2_done h2_lines h2_pool cm3_logit "
            "cm3_done line_mm yin_done y_mm y_step gate_mm gate_tanh gate_done h3_mm t1_done t2_done t3_done "
            "x2_done x2_hi x2_lo "
            "n_proj n_qk_hi n_qk_lo n_score n_max n_exp n_rinv n_tp n_pt_sb n_av "
            "a_g a_g_sb a_wide a_out a_done con_hi con_lo "
            "e_proj e_q_hi e_q_lo e_score e_max e_exp e_rinv e_tp e_pt_sb e_av e_wide e_out e_done e_hi e_lo "
            "f_vt f_vt_sb f_norm f_xb f_done").split()}

        x_dram = x.rearrange("b c h w -> c b (h w)")
        out_dram = out.rearrange("b c h w -> c b (h w)")
        w_dram = {"sam": w_sam, "cam": w_cam, "out_s": w_out[:, 0:NT * C], "out_c": w_out[:, NT * C:2 * NT * C]}
        third = NT * C // 3
        HALF = 2 * HW

        def inner(pad, b, n=1):
            return pad[:, b:b + n, 1:1 + H, 1:1 + W]

        def flat4(ap):
            return ap.rearrange("p b (h w) -> p b h w", h=H)

        def two(t, i):
            return t[:, 2 * i:2 * i + 2, :].rearrange("p b s -> p (b s)")

        def cols(t, b):
            return t[:, b, :, :].rearrange("p j s -> p (j s)")

        def pair(t, i):
            return t[:, 2 * i:2 * i + 2, :, :].rearrange("p b j c -> p (b j c)")

        def hw(t):
            return t[:, :, :].rearrange("p h w -> p (h w)")

        block = ctx.enter_context(nc.Block())

        @block.sync
        def _(sp):
            for i in range(2):
                sp.dma_start(x_sb[:, 2 * i:2 * i + 2, :], x_dram[:, 2 * i:2 * i + 2, :]).then_inc(d_x[i], 16)
            sp.dma_start(par0[:, :], early).then_inc(d_early, 16)
            for k, n in enumerate(("cam", "out_s", "out_c")):
                for i in range(3):
                    if n != "cam":
                        sp.wait_ge(ev["w_lo"], 3 * (k - 1) + i + 1)
                    sp.dma_start(ws[n][:, third * i:third * (i + 1)],
                                 w_dram[n][:, third * i:third * (i + 1)]).then_inc(d_w[(k + 1) % 2][i], 16)
            sp.dma_start(par1[:, :], late).then_inc(d_late, 16)
            for b in range(B):
                sp.wait_ge(ev["f_done"], b + 1)
                sp.dma_start(out_dram[:, b, :], y[:, b, :]).then_inc(d_y, 16)
            sp.wait_ge(d_y, 16 * B)

        @block.gpsimd
        def _(pool):
            for n in ("s", "c"):
                for pad in (padh[n], padl[n]):
                    nc.gpsimd.memset(pad[:, :, 0:HP:HP - 1, :].bitcast(F32), 0.0).then_inc(ev["border"], 1)
                    nc.gpsimd.memset(pad[:, :, 1:1 + H, 0:WP:WP - 1].bitcast(F32), 0.0).then_inc(ev["border"], 1)
            for t in (mpad, cm2bd, w3z, b3z):
                nc.gpsimd.memset(t[:], 0.0).then_inc(ev["zeroed"], 1)
            pool.wait_ge(ev["sam_conv"], 2)
            for t in (*hpad, *w2bd):
                nc.gpsimd.memset(t[:, :, :].bitcast(F32), 0.0).then_inc(ev["zeroed"], 1)
            pool.wait_ge(ev["zeroed"], 8)
            pool.wait_ge(d_late, 16)
            n_raw = 0
            for b in range(B):
                r, c = slice(WID * b, WID * (b + 1)), slice(WID * b, WID * (b + 1))
                a = LATE_AT["w2_rep"][0]
                w2 = par1[r, a:a + NT * WID].rearrange("p (t o) -> p t o", t=NT)
                nc.gpsimd.tensor_copy(w2bd[0][r, :, c], w2).then_inc(ev["spread_hi"], 1)
                pool.wait_ge(ev["spread_hi"], b + 1)
                nc.gpsimd.tensor_tensor(w2bd[1][r, :, c], w2, w2bd[0][r, :, c].bitcast(F32),
                                        ALU.subtract).then_inc(ev["spread"], 1)
                a = LATE_AT["cm2_rep"][0]
                nc.gpsimd.tensor_copy(cm2bd[r, c], par1[r, a:a + WID]).then_inc(ev["spread_raw"], 1)
                a = LATE_AT["w3_rep"][0]
                nc.gpsimd.tensor_copy(w3z[r, b, :], par1[r, a:a + C]).then_inc(ev["spread_raw"], 1)
                a = LATE_AT["b3_row"][0]
                nc.gpsimd.tensor_copy(b3z[WID * b:WID * b + 1, b, :],
                                      par1[WID * b:WID * b + 1, a:a + C]).then_inc(ev["spread_raw"], 1)
            pool.wait_ge(ev["spread_raw"], 3 * B)
            pool.wait_ge(ev["cam_conv"], 2)
            for k, (whole, p) in enumerate(((w3z, w3p), (b3z, b3p))):
                nc.gpsimd.tensor_copy(p[0][:, :, :], whole[:, :, :]).then_inc(ev["spread_hi"], 1)
                pool.wait_ge(ev["spread_hi"], B + k + 1)
                nc.gpsimd.tensor_tensor(p[1][:, :, :], whole[:, :, :], p[0][:, :, :].bitcast(F32),
                                        ALU.subtract).then_inc(ev["spread"], 1)
            for b in range(B):
                pool.wait_ge(ev["t2_done"], b + 1)
                pool.wait_ge(ev["x1_done"], b + 1)
                nc.gpsimd.tensor_tensor(t3[:, b, :], t2[:, b, :, :].rearrange("p h w -> p (h w)"), x1[:, b, :],
                                        ALU.add).then_inc(ev["t3_done"], 1)
            pool.wait_ge(ev["prep"], 5)
            for b in range(B):
                pool.wait_ge(ev["e_done"], b + 1)
                nc.gpsimd.tensor_scalar(x3b[:, b, :], x3[:, b, :], gbv[:, 0:1], None, ALU.add).then_inc(ev["f_xb"], 1)

        @block.scalar
        def _(act):
            for i in range(3):
                act.dma_start(ws["sam"][:, third * i:third * (i + 1)],
                              w_dram["sam"][:, third * i:third * (i + 1)]).then_inc(d_w[0][i], 16)

            def x_high(i):
                act.wait_ge(d_x[i], 16)
                nc.scalar.copy(inner(padh["x"], 2 * i, 2), flat4(x_sb[:, 2 * i:2 * i + 2, :])).then_inc(ev["x_hi"], 1)

            def w_high(n, i):
                k = W_ORDER.index(n)
                act.wait_ge(d_w[k % 2][i], 16 * (k // 2 + 1))
                nc.scalar.copy(wh[n][:, third * i:third * (i + 1)],
                               ws[n][:, third * i:third * (i + 1)]).then_inc(ev["w_hi"], 1)

            act.wait_ge(ev["border_x"], 5)
            x_high(0)
            for i in range(3):
                w_high("sam", i)
            x_high(1)
            for i in range(3):
                w_high("cam", i)
            act.wait_ge(ev["bn_var"], 1)
            nc.scalar.activation(bn_tmp[:, 1, :], bn_tmp[:, 0, :], ACT.Sqrt).then_inc(ev["bn_std"], 1)
            nc.scalar.copy(par0_p[0][:, :], par0[:, EARLY_KEEP:EARLY_W]).then_inc(ev["par0_hi"], 1)
            for i in range(3):
                w_high("out_s", i)
            act.wait_ge(ev["bn_step"], 4)
            for i in range(2):
                act.wait_ge(ev["sam_conv"], i + 1)
                nc.scalar.activation(two(xs, i), bank[i][:, :], ACT.Relu, bias=bn_shift[:, 0:1],
                                     scale=bn_inv[:, 0:1]).then_inc(ev["xs_done"], 1)
                if i == 0:
                    for j in range(3):
                        w_high("out_c", j)

            def qk_high(b):
                act.wait_ge(ev["s_proj"], b + 1)
                o = bank[QK_BANK[b]]
                nc.scalar.mul(qst[:, b, :], o[0:ST, 0:HW], 0.25).then_inc(ev["s_qk_hi"], 1)
                nc.scalar.copy(kst[:, b, :], o[0:ST, HW:2 * HW]).then_inc(ev["s_qk_hi"], 1)

            def v_high(i):
                act.wait_ge(ev["s_vt"], i + 1)
                nc.scalar.copy(pair(vt[0], i), bank[6 + i][:, :]).then_inc(ev["s_vt_hi"], 1)

            def s_exp(b):
                act.wait_ge(ev["s_max"], b + 1)
                for i in range(NCH):
                    nc.scalar.activation(prob[:, b, i, :], bank[QK_BANK[b]][:, HW * i:HW * (i + 1)], ACT.Exp,
                                         bias=nmax[:, b, i:i + 1],
                                         accum_out=rsum[:, b, i:i + 1]).then_inc(ev["s_exp"], 1)

            def s_pt_high(b):
                act.wait_ge(ev["s_tp"], b + 1)
                nc.scalar.copy(cols(ptp[0], b), bank[6 + b % 2][:, :]).then_inc(ev["s_pt_hi"], 1)

            def s_high(i):
                act.wait_ge(ev["s_att"], 2 * i + 2)
                act.wait_ge(ev["border"], 8)
                nc.scalar.copy(inner(padh["s"], 2 * i, 2), flat4(att_s[:, 2 * i:2 * i + 2, :])).then_inc(ev["s_hi"], 1)

            def xc_relu(i):
                act.wait_ge(ev["cam_conv"], i + 1)
                nc.scalar.activation(two(xc, i), bank[2 + i][:, :], ACT.Relu, bias=bn_shift[:, 1:2],
                                     scale=bn_inv[:, 1:2]).then_inc(ev["xc_done"], 1)

            def yt_high(i):
                act.wait_ge(ev["c_yt"], i + 1)
                nc.scalar.copy(pair(vt[0], i), bank[2 + i][:, :]).then_inc(ev["c_yt_hi"], 1)

            def c_exp(i):
                act.wait_ge(ev["c_nm"], i + 1)
                for b in (2 * i, 2 * i + 1):
                    nc.scalar.activation(cprob[:, b, :], bank[2 + i][:, C * (b % 2):C * (b % 2 + 1)], ACT.Exp,
                                         bias=cnm[:, b:b + 1], scale=float(HW) ** -0.5,
                                         accum_out=csum[:, b:b + 1]).then_inc(ev["c_exp"], 1)

            def c_pt_high(i):
                act.wait_ge(ev["c_tp"], i + 1)
                nc.scalar.copy(ptp[0][:, 2 * i:2 * i + 2, 0, 0:C],
                               bank[6 + i][:, 0:2 * C].rearrange("p (b c) -> p b c", b=2)).then_inc(ev["c_pt_hi"], 1)

            def c_high(i):
                act.wait_ge(ev["c_att"], i + 1)
                nc.scalar.copy(inner(padh["c"], 2 * i, 2), flat4(att_c[:, 2 * i:2 * i + 2, :])).then_inc(ev["c_hi"], 1)

            qk_high(0)
            qk_high(1)
            v_high(0)
            qk_high(2)
            qk_high(3)
            v_high(1)
            s_exp(0)
            s_exp(1)
            s_exp(2)
            s_exp(3)
            s_pt_high(0)
            s_pt_high(1)
            xc_relu(0)
            s_pt_high(2)
            s_high(0)
            s_pt_high(3)
            yt_high(0)
            s_high(1)
            c_exp(0)
            xc_relu(1)
            c_pt_high(0)
            yt_high(1)
            c_exp(1)
            c_high(0)
            c_pt_high(1)
            c_high(1)
            act.wait_ge(d_late, 16)
            nc.scalar.copy(par1_p[0][:, :], par1[:, LATE_KEEP:LATE_W]).then_inc(ev["par1_hi"], 1)
            a = LATE_AT["con_t"][0]
            nc.scalar.copy(con_st[:, :], par1[0:ST, a:a + NCON]).then_inc(ev["con_hi"], 1)

            for b in range(B):
                act.wait_ge(ev["out_conv"], b // 2 + 1)
                nc.scalar.activation(x1[:, b, :], bank[b // 2][:, HW * (b % 2):HW * (b % 2 + 1)], ACT.Copy,
                                     accum_out=pool1[:, b:b + 1]).then_inc(ev["x1_done"], 1)
            act.wait_ge(ev["h1_conv"], 1)
            nc.scalar.activation(hr[:, 0, :, :].rearrange("p h w -> p (h w)"), bank[3][:, 0:HW], ACT.Relu, bias=p1("b1")).then_inc(ev["h1_relu"], 1)
            act.wait_ge(ev["h2_conv"], 1)
            nc.scalar.activation(hr[:, 1, :, :].rearrange("p h w -> p (h w)"), bank[5][:, 0:HW], ACT.Relu, bias=p1("b2")).then_inc(ev["h2_relu"], 1)
            act.wait_ge(ev["gate_mm"], 1)
            act.wait_ge(ev["prep"], 2)
            for i in range(2):
                nc.scalar.activation(gate[:, i, :, :].rearrange("p b h -> p (b h)"),
                                     bank[3][:, B * H * i:B * H * (i + 1)], ACT.Tanh, bias=hb[:, i:i + 1],
                                     scale=1.0 / 12).then_inc(ev["gate_tanh"], 1)
            for b in range(B):
                act.wait_ge(ev["t3_done"], b + 1)
                nc.scalar.activation(map_b[0][:, b, :], t3[:, b, :], ACT.Relu).then_inc(ev["x2_hi"], 1)
                nc.scalar.activation(x2[:, b, :], t3[:, b, :], ACT.Relu).then_inc(ev["x2_done"], 1)

            def lead_scale(b):
                act.wait_ge(ev["n_proj"], b + 1)
                nc.scalar.mul(qst[:, b, :], bank[2 * b][0:ST, 0:HW], 1.0 / C).then_inc(ev["n_qk_hi"], 1)
                nc.scalar.copy(kst[:, b, :], bank[2 * b][0:ST, HW:2 * HW]).then_inc(ev["n_qk_hi"], 1)

            def values(b):
                act.wait_ge(ev["a_g"], b + 1)
                nc.scalar.copy(gt[:, b, :, :].rearrange("p j l -> p (j l)"),
                               bank[2 * b + 1][:, 0:NCH * L]).then_inc(ev["a_g_sb"], 1)

            def exp_self(b, k=0):
                act.wait_ge(ev["n_max"], k + b + 1)
                o = bank[2 * b + k // B]
                for i in range(NCH):
                    nc.scalar.activation(prob[:, b, i, :], o[:, HW * i:HW * (i + 1)], ACT.Exp,
                                         bias=nmax[:, b, i:i + 1],
                                         accum_out=rsum[:, b, i:i + 1]).then_inc(ev["n_exp"], 1)

            def turned_self(b, k=0):
                act.wait_ge(ev["n_tp"], k + b + 1)
                nc.scalar.copy(cols(pt_sb, b), bank[2 * b + 1 - k // B][:, :]).then_inc(ev["n_pt_sb"], 1)

            def lead_query(b):
                act.wait_ge(ev["e_proj"], b + 1)
                nc.scalar.mul(qst[:, b, :], bank[2 * b][0:ST, 0:HW], float(C) ** -0.5).then_inc(ev["e_q_hi"], 1)

            def exp_concepts(b):
                act.wait_ge(ev["e_max"], b + 1)
                for i in range(NCH):
                    nc.scalar.activation(prob2[:, b, i, :], bank[2 * b + 1][:, NCON * i:NCON * (i + 1)], ACT.Exp,
                                         bias=nmax2[:, b, i:i + 1],
                                         accum_out=rsum2[:, b, i:i + 1]).then_inc(ev["e_exp"], 1)

            def turned_concepts(b):
                act.wait_ge(ev["e_tp"], b + 1)
                nc.scalar.copy(pt2[:, b, :], bank[2 * b][0:NCON, 0:HW]).then_inc(ev["e_pt_sb"], 1)

            def lead_x3(b):
                act.wait_ge(ev["e_done"], b + 1)
                nc.scalar.copy(map_b[0][:, b, :], x3[:, b, :]).then_inc(ev["e_hi"], 1)

            def lead_bias(b):
                act.wait_ge(ev["n_proj"], B + b + 1)
                nc.scalar.activation(qst[:, b, :], bank[2 * b + 1][0:ST, 0:HW], ACT.Identity,
                                     bias=p1("bq", ST)).then_inc(ev["n_qk_hi"], 1)
                nc.scalar.activation(kst[:, b, :], bank[2 * b + 1][0:ST, HW:2 * HW], ACT.Identity,
                                     bias=p1("bk", ST)).then_inc(ev["n_qk_hi"], 1)

            def values3(b):
                act.wait_ge(ev["f_vt"], b + 1)
                nc.scalar.copy(vt3[:, b, :], bank[2 * b][:, 0:NCH * C]).then_inc(ev["f_vt_sb"], 1)

            def exp_last(b):
                exp_self(b, B)

            def turned_last(b):
                turned_self(b, B)

            for step, b in ((lead_scale, 0), (values, 0), (lead_scale, 1), (values, 1), (lead_scale, 2),
                            (values, 2), (exp_self, 0), (exp_self, 1), (turned_self, 0), (lead_scale, 3),
                            (turned_self, 1), (exp_self, 2), (values, 3), (turned_self, 2), (exp_self, 3),
                            (lead_query, 0), (turned_self, 3), (exp_concepts, 0), (lead_query, 1),
                            (turned_concepts, 0), (exp_concepts, 1), (lead_query, 2), (turned_concepts, 1),
                            (exp_concepts, 2), (lead_query, 3), (lead_x3, 0), (turned_concepts, 2),
                            (exp_concepts, 3), (lead_x3, 1), (lead_bias, 0), (turned_concepts, 3), (values3, 0),
                            (lead_x3, 2), (lead_bias, 1), (exp_last, 0), (lead_x3, 3), (lead_bias, 2),
                            (values3, 1), (exp_last, 1), (lead_bias, 3), (turned_last, 0), (values3, 2),
                            (exp_last, 2), (turned_last, 1), (values3, 3), (exp_last, 3), (turned_last, 2),
                            (turned_last, 3)):
                step(b)
        @block.vector
        def _(dve):
            def low(out_ap, whole, hi):
                return nc.vector.tensor_tensor(out_ap, whole, hi.bitcast(F32), ALU.subtract)

            nc.vector.memset(h2p[0][:, :, :].bitcast(F32), 0.0).then_inc(ev["border_x"], 1)
            for pad in (padh["x"], padl["x"]):
                nc.vector.memset(pad[:, :, 0:HP:HP - 1, :].bitcast(F32), 0.0).then_inc(ev["border_x"], 1)
                nc.vector.memset(pad[:, :, 1:1 + H, 0:WP:WP - 1].bitcast(F32), 0.0).then_inc(ev["border_x"], 1)

            def x_low(i):
                dve.wait_ge(ev["x_hi"], i + 1)
                low(inner(padl["x"], 2 * i, 2), flat4(x_sb[:, 2 * i:2 * i + 2, :]),
                    inner(padh["x"], 2 * i, 2)).then_inc(ev["x_lo"], 1)

            def w_low(n, i):
                dve.wait_ge(ev["w_hi"], 3 * W_ORDER.index(n) + i + 1)
                c = slice(third * i, third * (i + 1))
                low(wl[n][:, c], ws[n][:, c], wh[n][:, c]).then_inc(ev["w_lo"], 1)

            def map_split(whole, m, i, done, hi, lo):
                dve.wait_ge(done, i + 1)
                nc.vector.tensor_copy(two(m[0], i), two(whole, i)).then_inc(hi, 1)
                dve.wait_ge(hi, i + 1)
                low(two(m[1], i), two(whole, i), two(m[0], i)).then_inc(lo, 1)

            x_low(0)
            for i in range(3):
                w_low("sam", i)
            x_low(1)
            dve.wait_ge(d_early, 16)
            nc.vector.tensor_scalar(bn_tmp[:, 0, :], p0("bn_var"), 1e-5, None, ALU.add).then_inc(ev["bn_var"], 1)
            for i in range(3):
                w_low("cam", i)
            dve.wait_ge(ev["bn_std"], 1)
            nc.vector.reciprocal(bn_tmp[:, 2, :], bn_tmp[:, 1, :]).then_inc(ev["bn_step"], 1)
            dve.wait_ge(ev["bn_step"], 1)
            nc.vector.tensor_tensor(bn_inv[:, :], bn_tmp[:, 2, :], p0("bn_scale"), ALU.mult).then_inc(ev["bn_step"], 1)
            dve.wait_ge(ev["bn_step"], 2)
            nc.vector.tensor_tensor(bn_tmp[:, 3, :], bn_inv[:, :], p0("bn_mean"), ALU.mult).then_inc(ev["bn_step"], 1)
            dve.wait_ge(ev["bn_step"], 3)
            nc.vector.tensor_tensor(bn_shift[:, :], p0("bn_bias"), bn_tmp[:, 3, :],
                                    ALU.subtract).then_inc(ev["bn_step"], 1)
            dve.wait_ge(ev["par0_hi"], 1)
            low(par0_p[1][:, :], par0[:, EARLY_KEEP:EARLY_W], par0_p[0][:, :]).then_inc(ev["par0_lo"], 1)
            for i in range(3):
                w_low("out_s", i)
            map_split(xs, map_a, 0, ev["xs_done"], ev["xs_hi"], ev["xs_lo"])
            for i in range(3):
                w_low("out_c", i)
            map_split(xs, map_a, 1, ev["xs_done"], ev["xs_hi"], ev["xs_lo"])

            def qk_low(b):
                dve.wait_ge(ev["s_qk_hi"], 2 * (b + 1))
                o = bank[QK_BANK[b]]
                nc.vector.scalar_tensor_tensor(qst[2 * GAP:ST, b, :], o[2 * GAP:ST, 0:HW], 0.25,
                                               qst[2 * GAP:ST, b, :].bitcast(F32), ALU.mult,
                                               ALU.subtract).then_inc(ev["s_qk_lo"], 1)
                low(kst[GAP:2 * GAP, b, :], o[GAP:2 * GAP, HW:2 * HW], kst[GAP:2 * GAP, b, :]).then_inc(ev["s_qk_lo"], 1)

            def v_low(i):
                dve.wait_ge(ev["s_vt_hi"], i + 1)
                low(pair(vt[1], i), bank[6 + i][:, :], pair(vt[0], i)).then_inc(ev["s_vt_lo"], 1)

            def s_max(b):
                dve.wait_ge(ev["s_score"], b + 1)
                nc.vector.tensor_reduce(nmax[:, b, :], bank[QK_BANK[b]][:, :].rearrange("p (i s) -> p i s", i=NCH),
                                        AX.X, ALU.max, negate=True).then_inc(ev["s_max"], 1)

            def s_norm(b):
                dve.wait_ge(ev["s_exp"], NCH * (b + 1))
                nc.vector.reciprocal(rinv[:, b, :], rsum[:, b, :]).then_inc(ev["s_rinv"], 1)
                dve.wait_ge(ev["s_rinv"], b + 1)
                for i in range(NCH):
                    nc.vector.tensor_scalar(prob[:, b, i, :], prob[:, b, i, :], rinv[:, b, i:i + 1], None,
                                            ALU.mult).then_inc(ev["s_norm"], 1)

            def s_pt_low(b):
                dve.wait_ge(ev["s_pt_hi"], b + 1)
                low(cols(ptp[1], b), bank[6 + b % 2][:, :], cols(ptp[0], b)).then_inc(ev["s_pt_lo"], 1)

            def s_residual(b):
                dve.wait_ge(ev["s_av"], b + 1)
                nc.vector.scalar_tensor_tensor(att_s[:, b, :], bank[4 + b % 2][:, 0:HW], p0("gam_sam"), xs[:, b, :],
                                               ALU.mult, ALU.add).then_inc(ev["s_att"], 1)

            def s_low(i):
                dve.wait_ge(ev["s_hi"], i + 1)
                low(inner(padl["s"], 2 * i, 2), flat4(att_s[:, 2 * i:2 * i + 2, :]),
                    inner(padh["s"], 2 * i, 2)).then_inc(ev["s_lo"], 1)

            def yt_low(i):
                dve.wait_ge(ev["c_yt_hi"], i + 1)
                low(pair(vt[1], i), bank[2 + i][:, :], pair(vt[0], i)).then_inc(ev["c_yt_lo"], 1)

            def c_max(i):
                c = slice(2 * i, 2 * i + 2)
                dve.wait_ge(ev["c_gram"], i + 1)
                nc.vector.tensor_reduce(cmax[:, c], bank[2 + i][:, 0:2 * C].rearrange("p (b c) -> p b c", b=2), AX.X,
                                        ALU.max).then_inc(ev["c_max"], 1)
                dve.wait_ge(ev["c_max"], i + 1)
                nc.vector.tensor_scalar(cnm[:, c], cmax[:, c], -float(HW) ** -0.5, None,
                                        ALU.mult).then_inc(ev["c_nm"], 1)

            def c_norm(i):
                dve.wait_ge(ev["c_exp"], 2 * (i + 1))
                c = slice(2 * i, 2 * i + 2)
                nc.vector.reciprocal(cinv[:, c], csum[:, c]).then_inc(ev["c_rinv"], 1)
                dve.wait_ge(ev["c_rinv"], i + 1)
                for b in (2 * i, 2 * i + 1):
                    nc.vector.tensor_scalar(cprob[:, b, :], cprob[:, b, :], cinv[:, b:b + 1], None,
                                            ALU.mult).then_inc(ev["c_norm"], 1)

            def c_pt_low(i):
                dve.wait_ge(ev["c_pt_hi"], i + 1)
                c = slice(2 * i, 2 * i + 2)
                low(ptp[1][:, c, 0, 0:C], bank[6 + i][:, 0:2 * C].rearrange("p (b c) -> p b c", b=2),
                    ptp[0][:, c, 0, 0:C]).then_inc(ev["c_pt_lo"], 1)

            def c_residual(i):
                dve.wait_ge(ev["c_av"], i + 1)
                nc.vector.scalar_tensor_tensor(two(att_c, i), bank[4 + i][:, :], p0("gam_cam"), two(xc, i),
                                               ALU.mult, ALU.add).then_inc(ev["c_att"], 1)

            def c_low(i):
                dve.wait_ge(ev["c_hi"], i + 1)
                low(inner(padl["c"], 2 * i, 2), flat4(att_c[:, 2 * i:2 * i + 2, :]),
                    inner(padh["c"], 2 * i, 2)).then_inc(ev["c_lo"], 1)

            qk_low(0)
            qk_low(1)
            v_low(0)
            qk_low(2)
            qk_low(3)
            v_low(1)
            s_max(0)
            s_max(1)
            s_max(2)
            s_norm(0)
            s_max(3)
            s_norm(1)
            s_pt_low(0)
            s_norm(2)
            s_pt_low(1)
            s_norm(3)
            s_residual(0)
            s_pt_low(2)
            s_residual(1)
            s_pt_low(3)
            s_low(0)
            map_split(xc, map_b, 0, ev["xc_done"], ev["xc_hi"], ev["xc_lo"])
            yt_low(0)
            s_residual(2)
            s_residual(3)
            c_max(0)
            s_low(1)
            c_norm(0)
            c_pt_low(0)
            yt_low(1)
            map_split(xc, map_b, 1, ev["xc_done"], ev["xc_hi"], ev["xc_lo"])
            c_residual(0)
            c_max(1)
            c_low(0)
            c_norm(1)
            c_pt_low(1)
            c_residual(1)
            c_low(1)

            dve.wait_ge(ev["par1_hi"], 1)
            low(par1_p[1][:, :], par1[:, LATE_KEEP:LATE_W], par1_p[0][:, :]).then_inc(ev["par1_lo"], 1)
            a = LATE_AT["con_t"][0]
            dve.wait_ge(ev["con_hi"], 1)
            low(con_st[GAP:2 * GAP, :], par1[GAP:2 * GAP, a:a + NCON], con_st[GAP:2 * GAP, :]).then_inc(ev["con_lo"], 1)
            a = LATE_AT["cm1_b"][0]
            nc.vector.tensor_scalar(thr[:, :], par1[:, a:a + 3], -float(HW), None, ALU.mult).then_inc(ev["prep"], 1)
            a = LATE_AT["ca_bh"][0]
            nc.vector.tensor_scalar(hb[:, :], par1[:, a:a + 2], 0.5, None, ALU.mult).then_inc(ev["prep"], 1)
            nc.vector.tensor_scalar(gsc[:, 0:1], p1("gam_sa"), L ** -0.5 * float(C) ** -0.5, None,
                                    ALU.mult).then_inc(ev["prep"], 1)
            nc.vector.tensor_scalar(gsc[:, 1:2], p1("gam_moca"), L ** -0.5, None, ALU.mult).then_inc(ev["prep"], 1)
            nc.vector.tensor_tensor(gbv[:, :], p1("gam3"), p1("bv"), ALU.mult).then_inc(ev["prep"], 1)

            for b in range(B):
                dve.wait_ge(ev["x1_done"], b + 1)
                nc.vector.tensor_copy(map_a[0][:, b, :], x1[:, b, :]).then_inc(ev["x1_hi"], 1)
                dve.wait_ge(ev["x1_hi"], b + 1)
                low(map_a[1][:, b, :], x1[:, b, :], map_a[0][:, b, :]).then_inc(ev["x1_lo"], 1)
            dve.wait_ge(ev["m_logit"], 1)
            dve.wait_ge(ev["zeroed"], 8)
            nc.vector.tensor_scalar(mpad[:, 1:1 + H, 1:1 + W], bank[2][:, 0:HW].rearrange("p (h w) -> p h w", h=H),
                                    p1("sm_b"), 0.0, ALU.add, ALU.is_gt).then_inc(ev["m_step"], 1)
            dve.wait_ge(ev["m_step"], 1)
            nc.vector.tensor_tensor(mrow[:, 0, :, :], mpad[:, :, 0:W], mpad[:, :, 1:1 + W],
                                    ALU.max).then_inc(ev["m_step"], 1)
            dve.wait_ge(ev["m_step"], 2)
            nc.vector.tensor_tensor(mrow[:, 1, :, :], mrow[:, 0, :, :], mpad[:, :, 2:2 + W],
                                    ALU.max).then_inc(ev["m_step"], 1)
            dve.wait_ge(ev["m_step"], 3)
            nc.vector.tensor_tensor(mdil[:, 0, :, :], mrow[:, 1, 0:H, :], mrow[:, 1, 1:1 + H, :],
                                    ALU.max).then_inc(ev["m_step"], 1)
            dve.wait_ge(ev["m_step"], 4)
            nc.vector.tensor_tensor(mdil[:, 1, :, :], mdil[:, 0, :, :], mrow[:, 1, 2:2 + H, :],
                                    ALU.max).then_inc(ev["m_step"], 1)
            dve.wait_ge(ev["cm1_logit"], 1)
            nc.vector.tensor_scalar(cm[:, 0:1], bank[4][:, 0:1], thr[:, 0:1], None, ALU.is_gt).then_inc(ev["cm1_done"], 1)
            dve.wait_ge(ev["cm1_done"], 1)
            dve.wait_ge(ev["m_step"], 5)
            dve.wait_ge(ev["h1_relu"], 1)
            nc.vector.scalar_tensor_tensor(h1[:, :, :], hr[:, 0, :, :], cm[:, 0:1], mdil[:, 1, :, :],
                                           ALU.mult, ALU.mult, accum_out=pool2[:, 0:1]).then_inc(ev["h1_done"], 1)
            dve.wait_ge(ev["h1_done"], 1)
            hi, lo = (t[:, 1:1 + H, 1:1 + W] for t in hpad)
            nc.vector.tensor_copy(hi, h1[:, :, :]).then_inc(ev["h1_hi"], 1)
            dve.wait_ge(ev["h1_hi"], 1)
            low(lo, h1[:, :, :], hi).then_inc(ev["h1_lo"], 1)
            nc.vector.tensor_copy(mflat[:, :, :], mpad[:, 1:1 + H, 1:1 + W]).then_inc(ev["m_lines"], 1)
            nc.vector.tensor_reduce(linem[:, 0, :], mpad[:, 1:1 + H, 1:1 + W], AX.X, ALU.add).then_inc(ev["m_lines"], 1)
            nc.vector.tensor_reduce(linem[:, 1, :], mpad[:, 1:1 + H, 1:1 + W].rearrange("p h w -> p w h"), AX.X,
                                    ALU.add).then_inc(ev["m_lines"], 1)
            dve.wait_ge(ev["cm2_logit"], 1)
            nc.vector.tensor_scalar(cm[:, 1:2], bank[0][:, 0:1], thr[:, 1:2], None, ALU.is_gt).then_inc(ev["cm2_done"], 1)
            dve.wait_ge(ev["cm2_done"], 1)
            dve.wait_ge(ev["m_lines"], 1)
            dve.wait_ge(ev["h2_relu"], 1)
            nc.vector.scalar_tensor_tensor(h2[:, :, :], hr[:, 1, :, :], cm[:, 1:2], mflat[:, :, :].bitcast(F32),
                                           ALU.mult, ALU.mult, accum_out=pool2[:, 1:2]).then_inc(ev["h2_done"], 1)
            dve.wait_ge(ev["h2_done"], 1)
            nc.vector.tensor_scalar(pool3g[:, :], p1("group"), pool2[:, 1:2], None, ALU.mult).then_inc(ev["h2_pool"], 1)
            nc.vector.tensor_reduce(lineh[:, 0, :], h2[:, :, :], AX.X, ALU.add).then_inc(ev["h2_lines"], 1)
            nc.vector.tensor_reduce(lineh[:, 1, :], h2[:, :, :].rearrange("p h w -> p w h"), AX.X,
                                    ALU.add).then_inc(ev["h2_lines"], 1)
            dve.wait_ge(ev["cm3_logit"], 1)
            nc.vector.tensor_scalar(cm3[:, :], bank[1][:, 0:B], thr[:, 2:3], None, ALU.is_gt).then_inc(ev["cm3_done"], 1)
            dve.wait_ge(ev["cm3_done"], 1)
            nc.vector.tensor_scalar(cm3s[:, :], cm3[:, :], 1.0 / W, None, ALU.mult).then_inc(ev["cm3_done"], 1)
            nc.vector.tensor_copy(h2p[0][:, :, :], h2[:, :, :]).then_inc(ev["h2_hi"], 1)
            dve.wait_ge(ev["h2_hi"], 1)
            low(h2p[1][:, :, :], h2[:, :, :], h2p[0][:, :, :]).then_inc(ev["h2_lo"], 1)
            dve.wait_ge(ev["cm3_done"], 2)
            dve.wait_ge(ev["line_mm"], 1)
            nc.vector.tensor_tensor(yin[:, :, :, :].rearrange("p b i h -> p b (i h)"),
                                    bank[0][:, 0:B * 2 * H].rearrange("p (b l) -> p b l", b=B),
                                    cm3s[:, :].unsqueeze(2).broadcast_to([P, B, 2 * H]),
                                    ALU.mult).then_inc(ev["yin_done"], 1)
            f = lambda t: t[:, :, :, :].rearrange("p b i h -> p (b i h)")
            dve.wait_ge(ev["y_mm"], 1)
            nc.vector.tensor_scalar(f(yb), bank[2][0:MIP, 0:B * 2 * H], p1("ca_b1", MIP), None,
                                    ALU.add).then_inc(ev["y_step"], 1)
            dve.wait_ge(ev["y_step"], 1)
            nc.vector.tensor_scalar(f(yr), f(yb), 3.0, 0.0, ALU.add, ALU.max).then_inc(ev["y_step"], 1)
            dve.wait_ge(ev["y_step"], 2)
            nc.vector.scalar_tensor_tensor(f(ys), f(yr), 6.0, f(yb), ALU.min, ALU.mult).then_inc(ev["y_step"], 1)
            def x2_low(b):
                dve.wait_ge(ev["x2_hi"], b + 1)
                nc.vector.scalar_tensor_tensor(map_b[1][:, b, :], t3[:, b, :], 0.0, map_b[0][:, b, :].bitcast(F32),
                                               ALU.max, ALU.subtract).then_inc(ev["x2_lo"], 1)

            dve.wait_ge(ev["gate_tanh"], 2)
            nc.vector.tensor_scalar(gate1[:, :, :, :].rearrange("p i b h -> p (i b h)"),
                                    gate[:, :, :, :].rearrange("p i b h -> p (i b h)"), 1.0, None,
                                    ALU.add).then_inc(ev["gate_done"], 1)
            dve.wait_ge(ev["gate_done"], 1)
            nc.vector.scalar_tensor_tensor(gate[:, 0, :, :], gate1[:, 0, :, :], 0.25,
                                           cm3[:, :].unsqueeze(2).broadcast_to([P, B, H]), ALU.mult,
                                           ALU.mult).then_inc(ev["gate_done"], 1)
            dve.wait_ge(ev["gate_done"], 2)
            dve.wait_ge(ev["h3_mm"], 1)
            for b in range(B + 1):
                if b < B:
                    nc.vector.tensor_tensor(t1[:, b, :, :],
                                            bank[6 + b // 2][:, HW * (b % 2):HW * (b % 2 + 1)].rearrange(
                                                "p (h w) -> p h w", h=H),
                                            gate[:, 0, b, :].unsqueeze(2).broadcast_to([P, H, W]),
                                            ALU.mult).then_inc(ev["t1_done"], 1)
                    dve.wait_ge(ev["t1_done"], b + 1)
                    nc.vector.tensor_tensor(t2[:, b, :, :], t1[:, b, :, :],
                                            gate1[:, 1, b, :].unsqueeze(1).broadcast_to([P, H, W]),
                                            ALU.mult).then_inc(ev["t2_done"], 1)
                if b >= 2:
                    x2_low(b - 2)
            x2_low(B - 1)

            def rest_scale(b):
                dve.wait_ge(ev["n_qk_hi"], 2 * (b + 1))
                nc.vector.scalar_tensor_tensor(qst[2 * GAP:ST, b, :], bank[2 * b][2 * GAP:ST, 0:HW], 1.0 / C,
                                               qst[2 * GAP:ST, b, :].bitcast(F32), ALU.mult,
                                               ALU.subtract).then_inc(ev["n_qk_lo"], 1)
                low(kst[GAP:2 * GAP, b, :], bank[2 * b][GAP:2 * GAP, HW:2 * HW],
                    kst[GAP:2 * GAP, b, :]).then_inc(ev["n_qk_lo"], 1)

            def max_self(b, k=0):
                dve.wait_ge(ev["n_score"], k + b + 1)
                o = bank[2 * b + k // B]
                nc.vector.tensor_reduce(nmax[:, b, :], o[:, :].rearrange("p (i s) -> p i s", i=NCH),
                                        AX.X, ALU.max, negate=True).then_inc(ev["n_max"], 1)

            sel = p1("sel16").unsqueeze(1).broadcast_to([P, L, L]).rearrange("p m l -> p l m")

            def spread_rows(b, o, ri, done):
                for i in range(NCH):
                    nc.vector.scalar_tensor_tensor(wide[:, b, i, :].rearrange("p (l m) -> p l m", l=L),
                                                   o[:, L * i:L * (i + 1)].unsqueeze(1).broadcast_to([P, L, L]),
                                                   ri[:, b, i:i + 1], sel, ALU.mult, ALU.mult).then_inc(done, 1)

            def inverse_self(b, k=0):
                dve.wait_ge(ev["n_exp"], NCH * (k + b + 1))
                nc.vector.reciprocal(rinv[:, b, :], rsum[:, b, :]).then_inc(ev["n_rinv"], 1)

            def spread_self(b):
                dve.wait_ge(ev["n_rinv"], b + 1)
                dve.wait_ge(ev["n_av"], b + 1)
                spread_rows(b, bank[2 * b], rinv, ev["a_wide"])

            def add_self(b):
                dve.wait_ge(ev["a_out"], b + 1)
                dve.wait_ge(ev["x2_done"], b + 1)
                nc.vector.scalar_tensor_tensor(sa[:, b, :], bank[2 * b + 1][:, 0:HW], gsc[:, 0:1],
                                               x2[:, b, :], ALU.mult, ALU.add).then_inc(ev["a_done"], 1)

            def rest_query(b):
                dve.wait_ge(ev["e_q_hi"], b + 1)
                nc.vector.scalar_tensor_tensor(qst[2 * GAP:ST, b, :], bank[2 * b][2 * GAP:ST, 0:HW],
                                               float(C) ** -0.5, qst[2 * GAP:ST, b, :].bitcast(F32), ALU.mult,
                                               ALU.subtract).then_inc(ev["e_q_lo"], 1)

            def max_concepts(b):
                dve.wait_ge(ev["e_score"], b + 1)
                nc.vector.tensor_reduce(nmax2[:, b, :],
                                        bank[2 * b + 1][:, 0:NCH * NCON].rearrange("p (i s) -> p i s", i=NCH), AX.X,
                                        ALU.max, negate=True).then_inc(ev["e_max"], 1)

            def inverse_concepts(b):
                dve.wait_ge(ev["e_exp"], NCH * (b + 1))
                nc.vector.reciprocal(rinv2[:, b, :], rsum2[:, b, :]).then_inc(ev["e_rinv"], 1)

            def spread_concepts(b):
                dve.wait_ge(ev["e_rinv"], b + 1)
                dve.wait_ge(ev["e_av"], b + 1)
                spread_rows(b, bank[2 * b + 1], rinv2, ev["e_wide"])

            def add_concepts(b):
                dve.wait_ge(ev["e_out"], b + 1)
                nc.vector.scalar_tensor_tensor(x3[:, b, :], bank[2 * b][:, 0:HW], gsc[:, 1:2],
                                               sa[:, b, :], ALU.mult, ALU.add).then_inc(ev["e_done"], 1)

            def rest_x3(b):
                dve.wait_ge(ev["e_hi"], b + 1)
                low(map_b[1][:, b, :], x3[:, b, :], map_b[0][:, b, :]).then_inc(ev["e_lo"], 1)

            def rest_bias(b):
                dve.wait_ge(ev["n_qk_hi"], 2 * (B + b + 1))
                o = bank[2 * b + 1]
                at = LATE_AT["bq"][0]
                nc.vector.scalar_tensor_tensor(qst[2 * GAP:ST, b, :], o[2 * GAP:ST, 0:HW],
                                               par1[2 * GAP:ST, at:at + 1], qst[2 * GAP:ST, b, :].bitcast(F32),
                                               ALU.add, ALU.subtract).then_inc(ev["n_qk_lo"], 1)
                at = LATE_AT["bk"][0]
                nc.vector.scalar_tensor_tensor(kst[GAP:2 * GAP, b, :], o[GAP:2 * GAP, HW:2 * HW],
                                               par1[GAP:2 * GAP, at:at + 1], kst[GAP:2 * GAP, b, :].bitcast(F32),
                                               ALU.add, ALU.subtract).then_inc(ev["n_qk_lo"], 1)

            def max_last(b):
                max_self(b, B)

            def normalise_last(b):
                inverse_self(b, B)
                dve.wait_ge(ev["n_rinv"], B + b + 1)
                for i in range(NCH):
                    nc.vector.tensor_scalar(prob[:, b, i, :], prob[:, b, i, :], rinv[:, b, i:i + 1], None,
                                            ALU.mult).then_inc(ev["f_norm"], 1)

            def add_last(b):
                dve.wait_ge(ev["n_av"], B + b + 1)
                dve.wait_ge(ev["f_xb"], b + 1)
                nc.vector.scalar_tensor_tensor(y[:, b, :], bank[2 * b + 1][:, 0:HW], p1("gam3"),
                                               x3b[:, b, :], ALU.mult, ALU.add).then_inc(ev["f_done"], 1)

            for step, b in ((rest_scale, 0), (rest_scale, 1), (max_self, 0), (max_self, 1), (rest_scale, 2),
                            (inverse_self, 0), (max_self, 2), (inverse_self, 1), (rest_scale, 3), (spread_self, 0),
                            (spread_self, 1), (add_self, 0), (max_self, 3), (inverse_self, 2), (add_self, 1),
                            (rest_query, 0), (spread_self, 2), (max_concepts, 0), (inverse_self, 3),
                            (rest_query, 1), (add_self, 2), (spread_self, 3), (max_concepts, 1),
                            (inverse_concepts, 0), (spread_concepts, 0), (rest_query, 2), (add_self, 3),
                            (inverse_concepts, 1), (max_concepts, 2), (add_concepts, 0), (spread_concepts, 1),
                            (rest_query, 3), (rest_x3, 0), (inverse_concepts, 2), (max_concepts, 3),
                            (add_concepts, 1), (spread_concepts, 2), (rest_x3, 1), (inverse_concepts, 3),
                            (rest_bias, 0), (add_concepts, 2), (spread_concepts, 3), (rest_x3, 2), (max_last, 0),
                            (rest_bias, 1), (add_concepts, 3), (normalise_last, 0), (rest_x3, 3), (max_last, 1),
                            (rest_bias, 2), (normalise_last, 1), (max_last, 2), (rest_bias, 3), (add_last, 0),
                            (normalise_last, 2), (max_last, 3), (add_last, 1), (normalise_last, 3), (add_last, 2),
                            (add_last, 3)):
                step(b)
        @block.tensor
        def _(pe):
            mm = nc.tensor.matmul

            def mm3(o, w, v, first=True, last=True):
                mm(o, w[0], v[0], start=first, stop=False, skip_group_check=True)
                mm(o, w[0], v[1], start=False, stop=False, skip_group_check=True)
                return mm(o, w[1], v[0], start=False, stop=last, skip_group_check=True)

            def tap(n, pad, o, half, t, first, last):
                dy, dx = TAPS[t]
                v = [p[:, 2 * half:2 * half + 2, dy:dy + H, dx:dx + W] for p in (padh[pad], padl[pad])]
                c = slice(C * t, C * (t + 1))
                return mm3(o[:, :].rearrange("p (b h w) -> p b h w", b=2, h=H), (wh[n][:, c], wl[n][:, c]), v,
                           first, last)

            def weights_split(n, t):
                pe.wait_ge(ev["w_lo"], 3 * W_ORDER.index(n) + t // 3 + 1)

            def batch(m, b):
                return [p[:, b, :] for p in m]

            def chunk(m, b, j):
                return [p[:, b, P * j:P * (j + 1)] for p in m]

            def transposes(o, b):
                for i in range(NCH):
                    for j in range(NCH):
                        m = nc.tensor.transpose(o[:, HW * j + P * i:HW * j + P * (i + 1)],
                                                prob[:, b, i, P * j:P * (j + 1)], ident)
                return m

            def keep_clock(k, n, t=None):
                t = par0_p[0][:, 0:2 * P] if t is None else t
                for _ in range(n):
                    mm(bank[k][:, 0:2 * P], t[:, 0:P], t, start=True, stop=True, skip_group_check=True)

            pe.wait_ge(ev["border_x"], 1)
            keep_clock(7, START, hw(h2p[0]))
            for half in range(2):
                pe.wait_ge(ev["x_lo"], half + 1)
                for t in range(NT):
                    if half == 0 and t % 3 == 0:
                        weights_split("sam", t)
                    m = tap("sam", "x", bank[half], half, t, t == 0, t == NT - 1)
                m.then_inc(ev["sam_conv"], 1)

            def cam_taps(k0, k1):
                for k in range(k0, k1):
                    half, t = divmod(k, NT)
                    if t % 3 == 0:
                        weights_split("cam", t)
                    m = tap("cam", "x", bank[2 + half], half, t, t == 0, t == NT - 1)
                    if t == NT - 1:
                        m.then_inc(ev["cam_conv"], 1)

            def out_s_taps(k0, k1):
                for k in range(k0, k1):
                    half, t = divmod(k, NT)
                    if t == 0:
                        pe.wait_ge(ev["s_lo"], half + 1)
                    if t % 3 == 0:
                        weights_split("out_s", t)
                    tap("out_s", "s", bank[half], half, t, t == 0, False)

            def qk(b):
                pe.wait_ge(ev["xs_lo"], b // 2 + 1)
                o = bank[QK_BANK[b]]
                mm3(o[0:ST, 0:HW], parts("w_q"), batch(map_a, b))
                mm3(o[0:ST, HW:2 * HW], parts("w_k"), batch(map_a, b)).then_inc(ev["s_proj"], 1)

            def v(i):
                for b in (2 * i, 2 * i + 1):
                    for j in range(NCH):
                        c = C * (NCH * (b % 2) + j)
                        m = mm3(bank[6 + i][:, c:c + C], chunk(map_a, b, j), parts("w_v"))
                m.then_inc(ev["s_vt"], 1)

            def s_score(b):
                pe.wait_ge(ev["s_qk_lo"], 2 * (b + 1))
                for i in range(NCH):
                    m = mm(bank[QK_BANK[b]][:, HW * i:HW * (i + 1)], qst[:, b, P * i:P * (i + 1)], kst[:, b, :],
                           start=True, stop=True)
                m.then_inc(ev["s_score"], 1)

            def s_transpose(b):
                pe.wait_ge(ev["s_norm"], NCH * (b + 1))
                if b < 2:
                    pe.wait_ge(ev["s_vt_lo"], b + 1)
                else:
                    pe.wait_ge(ev["s_pt_lo"], b - 1)
                transposes(bank[6 + b % 2], b).then_inc(ev["s_tp"], 1)

            def s_apply(b):
                pe.wait_ge(ev["s_pt_lo"], b + 1)
                if b >= 2:
                    pe.wait_ge(ev["s_att"], b - 1)
                for j in range(NCH):
                    m = mm3(bank[4 + b % 2][:, 0:HW], [p[:, b, j, :] for p in vt], [p[:, b, j, :] for p in ptp],
                            j == 0, j == NCH - 1)
                m.then_inc(ev["s_av"], 1)

            def c_transpose_in(i):
                pe.wait_ge(ev["xc_done"], i + 1)
                for b in (2 * i, 2 * i + 1):
                    for j in range(NCH):
                        c = C * (NCH * (b % 2) + j)
                        m = nc.tensor.transpose(bank[2 + i][:, c:c + C], xc[:, b, P * j:P * (j + 1)], ident)
                m.then_inc(ev["c_yt"], 1)

            def c_gram(i):
                pe.wait_ge(ev["c_yt_lo"], i + 1)
                for b in (2 * i, 2 * i + 1):
                    for j in range(NCH):
                        yj = [p[:, b, j, :] for p in vt]
                        m = mm3(bank[2 + i][:, C * (b % 2):C * (b % 2 + 1)], yj, yj, j == 0, j == NCH - 1)
                m.then_inc(ev["c_gram"], 1)

            def c_transpose(i):
                pe.wait_ge(ev["c_norm"], 2 * (i + 1))
                pe.wait_ge(ev["s_pt_lo"], B - 1 + i)
                for b in (2 * i, 2 * i + 1):
                    m = nc.tensor.transpose(bank[6 + i][:, C * (b % 2):C * (b % 2 + 1)], cprob[:, b, :], ident)
                m.then_inc(ev["c_tp"], 1)

            def c_apply(i):
                pe.wait_ge(ev["c_pt_lo"], i + 1)
                pe.wait_ge(ev["xc_lo"], i + 1)
                pe.wait_ge(ev["s_att"], B - 1 + i)
                for b in (2 * i, 2 * i + 1):
                    m = mm3(bank[4 + i][:, HW * (b % 2):HW * (b % 2 + 1)], [p[:, b, 0, 0:C] for p in ptp],
                            batch(map_b, b))
                m.then_inc(ev["c_av"], 1)

            pe.wait_ge(ev["par0_lo"], 1)
            qk(0)
            qk(1)
            v(0)
            cam_taps(0, 3)
            qk(2)
            qk(3)
            v(1)
            s_score(0)
            s_score(1)
            s_score(2)
            s_score(3)
            cam_taps(3, 7)
            s_transpose(0)
            cam_taps(7, 8)
            s_transpose(1)
            cam_taps(8, 9)
            s_apply(0)
            s_transpose(2)
            cam_taps(9, 10)
            s_apply(1)
            s_transpose(3)
            cam_taps(10, 12)
            c_transpose_in(0)
            s_apply(2)
            cam_taps(12, 14)
            s_apply(3)
            cam_taps(14, 16)
            c_gram(0)
            cam_taps(16, 18)
            out_s_taps(0, 2)
            c_transpose(0)
            out_s_taps(2, 3)
            c_transpose_in(1)
            out_s_taps(3, 6)
            c_apply(0)
            out_s_taps(6, 7)
            c_gram(1)
            out_s_taps(7, 11)
            c_transpose(1)
            out_s_taps(11, 15)
            c_apply(1)
            out_s_taps(15, 18)
            for half in range(2):
                pe.wait_ge(ev["c_lo"], half + 1)
                for t in range(NT):
                    if half == 0 and t % 3 == 0:
                        weights_split("out_c", t)
                    m = tap("out_c", "c", bank[half], half, t, False, t == NT - 1)
                m.then_inc(ev["out_conv"], 1)

            def window(w, b):
                a = WIN - WID * b
                return [p[:, a:a + P] for p in w]

            pe.wait_ge(ev["par1_lo"], 1)
            for b in range(B):
                pe.wait_ge(ev["x1_lo"], b + 1)
                m = mm3(bank[2][:, 0:HW], window(parts("sm_win"), b), batch(map_a, b), b == 0, b == B - 1)
                if b == B - 1:
                    m.then_inc(ev["m_logit"], 1)
                m = mm3(bank[3][:, 0:HW], window(parts("w1_win"), b), batch(map_a, b), b == 0, b == B - 1)
            m.then_inc(ev["h1_conv"], 1)
            for b in range(B):
                m = mm(bank[4][:, 0:1], window([p1("cm1_win")], b)[0], pool1[:, b:b + 1], start=(b == 0),
                       stop=(b == B - 1))
            m.then_inc(ev["cm1_logit"], 1)
            keep_clock(0, 14)
            pe.wait_ge(ev["spread"], B + 2)
            pe.wait_ge(ev["h1_done"], 1)
            mm(bank[0][:, 0:1], cm2bd[:, :], pool2[:, 0:1], start=True, stop=True).then_inc(ev["cm2_logit"], 1)
            pe.wait_ge(ev["h1_lo"], 1)
            for t, (dy, dx) in enumerate(TAPS):
                m = mm3(bank[5][:, 0:HW].rearrange("p (h w) -> p h w", h=H), [p[:, t, :] for p in w2bd],
                        [p[:, dy:dy + H, dx:dx + W] for p in hpad], t == 0, t == NT - 1)
            m.then_inc(ev["h2_conv"], 1)
            pe.wait_ge(ev["m_lines"], 3)
            for b in range(B):
                for k in range(2):
                    mm(bank[6 + b // 2][:, HW * (b % 2):HW * (b % 2 + 1)], b3p[k][:, b, :], hw(mflat),
                       start=(b % 2 == 0 and k == 0), stop=False, skip_group_check=True)
            pe.wait_ge(ev["cm2_done"], 1)
            for b in range(B):
                mm(bank[0][:, 2 * H * b:2 * H * (b + 1)], b3z[:, b, :], hw(linem), start=(b == 0), stop=False,
                   skip_group_check=True)
            pe.wait_ge(ev["h2_pool"], 1)
            mm(bank[1][:, 0:B], p1("cm3_rep"), pool3g[:, :], start=True, stop=True).then_inc(ev["cm3_logit"], 1)
            pe.wait_ge(ev["h2_lines"], 2)
            for b in range(B):
                m = mm(bank[0][:, 2 * H * b:2 * H * (b + 1)], w3z[:, b, :], hw(lineh), start=False,
                       stop=(b == B - 1), skip_group_check=True)
            m.then_inc(ev["line_mm"], 1)
            pe.wait_ge(ev["h2_lo"], 1)
            for b in range(B):
                m = mm3(bank[6 + b // 2][:, HW * (b % 2):HW * (b % 2 + 1)], [p[:, b, :] for p in w3p],
                        [hw(p) for p in h2p], False, b % 2 == 1)
                if b == 1:
                    pe.wait_ge(ev["yin_done"], 1)
                    mm(bank[2][0:MIP, 0:B * 2 * H], p1("ca_w1"), yin[:, :, :, :].rearrange("p b i h -> p (b i h)"),
                       start=True, stop=True).then_inc(ev["y_mm"], 1)
            m.then_inc(ev["h3_mm"], 1)
            keep_clock(5, 3)
            pe.wait_ge(ev["y_step"], 3)
            mm(bank[3][:, 0:B * H].rearrange("p (b h) -> p b h", b=B), p1("ca_wh", MIP), ys[:, :, 0, :],
               start=True, stop=True)
            mm(bank[3][:, B * H:2 * B * H].rearrange("p (b h) -> p b h", b=B), p1("ca_ww", MIP), ys[:, :, 1, :],
               start=True, stop=True).then_inc(ev["gate_mm"], 1)

            keep_clock(5, 28)

            def project(b):
                pe.wait_ge(ev["x2_lo"], b + 1)
                mm3(bank[2 * b][0:ST, 0:HW], parts("w_th"), batch(map_b, b))
                mm3(bank[2 * b][0:ST, HW:2 * HW], parts("w_ph"), batch(map_b, b)).then_inc(ev["n_proj"], 1)
                if b == B - 1:
                    pe.wait_ge(ev["t1_done"], B)
                for j in range(NCH):
                    m = mm3(bank[2 * b + 1][:, L * j:L * (j + 1)], chunk(map_b, b, j), parts("w_g"))
                m.then_inc(ev["a_g"], 1)

            def scores(b, k=0):
                pe.wait_ge(ev["n_qk_lo"], 2 * (k + b + 1))
                for i in range(NCH):
                    m = mm(bank[2 * b + k // B][:, HW * i:HW * (i + 1)], qst[:, b, P * i:P * (i + 1)], kst[:, b, :],
                           start=True, stop=True)
                m.then_inc(ev["n_score"], 1)

            def turn_self(b):
                pe.wait_ge(ev["n_exp"], NCH * (b + 1))
                pe.wait_ge(ev["a_g_sb"], b + 1)
                transposes(bank[2 * b + 1], b).then_inc(ev["n_tp"], 1)

            def apply_self(b):
                pe.wait_ge(ev["n_pt_sb"], b + 1)
                for i in range(NCH):
                    for j in range(NCH):
                        m = mm(bank[2 * b][:, L * i:L * (i + 1)], pt_sb[:, b, j, P * i:P * (i + 1)],
                               gt[:, b, j, :], start=(j == 0), stop=(j == NCH - 1))
                m.then_inc(ev["n_av"], 1)

            def out_rows(b, o):
                for i in range(NCH):
                    m = mm(o[:, 0:HW], p1("w_o_rep")[:, C * i:C * (i + 1)], wide[:, b, i, :], start=(i == 0),
                           stop=(i == NCH - 1))
                return m

            def out_self(b):
                pe.wait_ge(ev["a_wide"], NCH * (b + 1))
                out_rows(b, bank[2 * b + 1]).then_inc(ev["a_out"], 1)

            def query(b):
                pe.wait_ge(ev["a_done"], b + 1)
                mm(bank[2 * b][0:ST, 0:HW], p1("w_th"), sa[:, b, :], start=True, stop=True).then_inc(ev["e_proj"], 1)

            def scores_concepts(b):
                pe.wait_ge(ev["con_lo"], 1)
                pe.wait_ge(ev["e_q_lo"], b + 1)
                for i in range(NCH):
                    m = mm(bank[2 * b + 1][:, NCON * i:NCON * (i + 1)], qst[:, b, P * i:P * (i + 1)], con_st[:, :],
                           start=True, stop=True)
                m.then_inc(ev["e_score"], 1)

            def turn_concepts(b):
                pe.wait_ge(ev["e_exp"], NCH * (b + 1))
                for i in range(NCH):
                    m = nc.tensor.transpose(bank[2 * b][0:NCON, P * i:P * (i + 1)], prob2[:, b, i, :], ident)
                m.then_inc(ev["e_tp"], 1)

            def apply_concepts(b):
                pe.wait_ge(ev["e_pt_sb"], b + 1)
                for i in range(NCH):
                    m = mm(bank[2 * b + 1][:, L * i:L * (i + 1)], pt2[:, b, P * i:P * (i + 1)], p1("con", NCON),
                           start=True, stop=True)
                m.then_inc(ev["e_av"], 1)

            def out_concepts(b):
                pe.wait_ge(ev["e_wide"], NCH * (b + 1))
                out_rows(b, bank[2 * b]).then_inc(ev["e_out"], 1)

            def project_last(b):
                pe.wait_ge(ev["e_lo"], b + 1)
                mm3(bank[2 * b + 1][0:ST, 0:HW], parts("w_q3"), batch(map_b, b))
                mm3(bank[2 * b + 1][0:ST, HW:2 * HW], parts("w_k3"), batch(map_b, b)).then_inc(ev["n_proj"], 1)
                for j in range(NCH):
                    m = mm3(bank[2 * b][:, C * j:C * (j + 1)], chunk(map_b, b, j), parts("w_v3"))
                m.then_inc(ev["f_vt"], 1)

            def scores_last(b):
                scores(b, B)

            def turn_last(b):
                pe.wait_ge(ev["f_norm"], NCH * (b + 1))
                pe.wait_ge(ev["f_vt_sb"], b + 1)
                transposes(bank[2 * b], b).then_inc(ev["n_tp"], 1)

            def apply_last(b):
                pe.wait_ge(ev["n_pt_sb"], B + b + 1)
                for j in range(NCH):
                    m = mm(bank[2 * b + 1][:, 0:HW], vt3[:, b, C * j:C * (j + 1)], pt_sb[:, b, j, :], start=(j == 0),
                           stop=(j == NCH - 1))
                m.then_inc(ev["n_av"], 1)

            for step, b in ((project, 0), (project, 1), (project, 2), (scores, 0), (scores, 1), (project, 3),
                            (turn_self, 0), (scores, 2), (turn_self, 1), (apply_self, 0), (apply_self, 1),
                            (out_self, 0), (scores, 3), (turn_self, 2), (query, 0), (out_self, 1), (apply_self, 2),
                            (turn_self, 3), (scores_concepts, 0), (query, 1), (out_self, 2), (apply_self, 3),
                            (turn_concepts, 0), (scores_concepts, 1), (query, 2), (apply_concepts, 0),
                            (out_self, 3), (turn_concepts, 1), (out_concepts, 0), (scores_concepts, 2),
                            (apply_concepts, 1), (query, 3), (turn_concepts, 2), (out_concepts, 1),
                            (scores_concepts, 3), (apply_concepts, 2), (project_last, 0), (turn_concepts, 3),
                            (out_concepts, 2), (apply_concepts, 3), (project_last, 1), (scores_last, 0),
                            (out_concepts, 3), (project_last, 2), (scores_last, 1), (project_last, 3),
                            (turn_last, 0), (scores_last, 2), (apply_last, 0), (turn_last, 1), (scores_last, 3),
                            (apply_last, 1), (turn_last, 2), (apply_last, 2), (turn_last, 3), (apply_last, 3)):
                step(b)


def kernel(**inputs):
    import numpy as np
    import concourse.bacc as bacc
    from concourse.bass_utils import run_bass_kernel_spmd

    a = {k: np.asarray(v) for k, v in inputs.items()}
    g0 = lambda n: a["L0_conv_" + n]
    g1 = lambda n: a["L1_conv_" + n]
    g2 = lambda n: a["L2_conv_" + n]
    g3 = lambda n: a["L3_conv_" + n]
    f32 = a["x"].dtype

    def taps(w):
        return np.transpose(w, (1, 2, 3, 0)).reshape(w.shape[1], -1)

    def stack(u):
        w = np.zeros((u.shape[0], 3, GAP), f32)
        w[:, :, 0:L] = u[:, None, :]
        return w.reshape(u.shape[0], ST)

    def window(w):
        z = np.zeros((C, WIN), f32)
        return np.concatenate([z, w, z], axis=1)

    def pack(table, values):
        cols, width = columns(table)
        m = np.zeros((P, width), f32)
        for name, (at, w) in cols.items():
            v = np.asarray(values[name], f32)
            v = v.reshape(-1, w)
            m[0:v.shape[0], at:at + w] = v
        return m

    col = lambda v: np.reshape(v, (-1, 1))
    full = lambda v: np.broadcast_to(np.reshape(v, (1, 1)), (P, 1))
    four = lambda v: np.concatenate([v] * B, axis=0)

    early = pack(EARLY + EARLY_SPLIT, {
        "bn_scale": np.stack([g0("bn_sam_scale"), g0("bn_cam_scale")], 1),
        "bn_bias": np.stack([g0("bn_sam_bias"), g0("bn_cam_bias")], 1),
        "bn_mean": np.stack([g0("bn_sam_mean"), g0("bn_cam_mean")], 1),
        "bn_var": np.stack([g0("bn_sam_var"), g0("bn_cam_var")], 1),
        "gam_sam": full(g0("gamma_sam")), "gam_cam": full(g0("gamma_cam")),
        "ident": np.eye(P, dtype=f32),
        "w_q": stack(g0("w_qk")[0:L, :, 0, 0].T), "w_k": stack(g0("w_qk")[L:2 * L, :, 0, 0].T),
        "w_v": g0("w_v")[:, :, 0, 0].T,
    })
    w2t = np.transpose(g1("w2"), (1, 2, 3, 0)).reshape(WID, NT * WID)
    sel16 = np.zeros((P, L), f32)
    sel16[np.arange(P), np.arange(P) % L] = 1
    group = np.zeros((P, B), f32)
    group[np.arange(P), np.arange(P) // WID] = 1
    late = pack(LATE + LATE_SPLIT, {
        "sm_b": full(g1("sm_b")), "b1": four(col(g1("b1"))), "b2": four(col(g1("b2"))),
        "cm1_b": four(col(g1("cm1_b"))), "cm2_b": four(col(g1("cm2_b"))), "cm3_b": col(g1("cm3_b")),
        "ca_b1": col(g1("ca_b1")), "ca_bh": col(g1("ca_bh")), "ca_bw": col(g1("ca_bw")),
        "gam_sa": full(g2("gamma_sa")), "gam_moca": full(g2("gamma_moca")), "gam3": full(g3("gamma")),
        "bq": stack(g3("bq").reshape(1, L)).T, "bk": stack(g3("bk").reshape(1, L)).T, "bv": col(g3("bv")),
        "group": group, "sel16": sel16,
        "sm_win": window(np.repeat(g1("sm_w").reshape(C, 1), WID, axis=1)),
        "w1_win": window(g1("w1")[:, :, 0, 0].T), "cm1_win": window(g1("cm1_w").T),
        "w2_rep": four(w2t), "cm2_rep": four(g1("cm2_w").T), "cm3_rep": four(g1("cm3_w").T),
        "w3_rep": four(g1("w3")[:, :, 0, 0].T), "b3_row": np.broadcast_to(g1("b3").reshape(1, C), (P, C)),
        "ca_w1": g1("ca_w1")[:, :, 0, 0].T, "ca_wh": g1("ca_wh")[:, :, 0, 0].T, "ca_ww": g1("ca_ww")[:, :, 0, 0].T,
        "w_th": stack(g2("w_theta").T), "w_ph": stack(g2("w_phi").T), "w_g": g2("w_g").T,
        "w_o_rep": np.concatenate(np.split(np.repeat(g2("w_o").T, HW // L, axis=0), NCH, axis=0), axis=1),
        "con_t": stack(g2("concepts")).T, "con": g2("concepts"),
        "w_q3": stack(g3("Wq").T), "w_k3": stack(g3("Wk").T), "w_v3": g3("Wv").T,
    })
    w_out = g0("w_out")
    arrays = {
        "x": a["x"],
        "w_sam": taps(g0("w_sam")), "w_cam": taps(g0("w_cam")),
        "w_out": np.concatenate([taps(w_out[:, 0:C]), taps(w_out[:, C:2 * C])], axis=1),
        "early": early, "late": late,
    }
    arrays = {k: np.ascontiguousarray(v) for k, v in arrays.items()}
    nc = bacc.Bacc("TRN2", target_bir_lowering=False, num_devices=1)
    args = [nc.dram_tensor(f"in_{k}", v.shape, mybir.dt.from_np(v.dtype), kind="ExternalInput").ap()
            for k, v in arrays.items()]
    out = nc.dram_tensor("out_0", a["x"].shape, F32, kind="ExternalOutput").ap()
    build(nc, *args, out)
    r = run_bass_kernel_spmd(nc, [{f"in_{k}": v for k, v in arrays.items()}], core_ids=[0])
    return r.results[0]["out_0"]
```

```python
from contextlib import ExitStack

import concourse.bass as bass
from concourse import mybir

F32 = mybir.dt.float32
F32R = mybir.dt.float32r
ALU = mybir.AluOpType
ACT = mybir.ActivationFunctionType
AX = mybir.AxisListType

B, C, H, W = 4, 128, 16, 16
HW = H * W
P = 128
HP, WP = H + 2, W + 2
TAPS = [(dy, dx) for dy in range(3) for dx in range(3)]
NT = len(TAPS)
L = 16
WID = 32
MIP = 16
NCON = 64
NCH = HW // P
OUT_BANK = [0, 0, 1, 6]
QK_BANK = [4, 5, 0, 1]
GAP = 32
ST = 3 * GAP
START = 16
WIN = P - WID

EARLY = [("bn_scale", 2), ("bn_bias", 2), ("bn_mean", 2), ("bn_var", 2), ("gam_sam", 1), ("gam_cam", 1),
         ("ident", P), ("w_v", C)]
EARLY_SPLIT = [("w_qk", ST)]
LATE = [("sm_b", 1), ("b1", 1), ("b2", 1), ("cm1_b", 1), ("cm2_b", 1), ("cm3_b", 1), ("ca_b1", 1),
        ("ca_bh", 1), ("ca_bw", 1), ("gam_sa", 1), ("gam_moca", 1), ("gam3", 1), ("bq", 1), ("bk", 1),
        ("bv", 1), ("group", B), ("sel16", L), ("cm1_win", WIN + WID + WIN),
        ("w2_rep", NT * WID), ("cm2_rep", WID), ("cm3_rep", C), ("w3_rep", C), ("b3_row", C),
        ("ca_w1", MIP), ("ca_wh", C), ("ca_ww", C), ("con_t", NCON), ("con", L),
        ("w_o_rep", NCH * C), ("w_tpg", ST + L), ("w_q3", ST), ("w_k3", ST), ("w_v3", C)]
LATE_SPLIT = [("sm_win", WIN + WID + WIN), ("w1_win", WIN + WID + WIN)]


def columns(table):
    at, out = 0, {}
    for name, width in table:
        out[name] = (at, width)
        at += width
    return out, at


EARLY_AT, EARLY_W = columns(EARLY + EARLY_SPLIT)
LATE_AT, LATE_W = columns(LATE + LATE_SPLIT)
EARLY_KEEP = columns(EARLY)[1]
LATE_KEEP = columns(LATE)[1]


def build(nc, x, w_sam, w_cam, w_out, early, late, out):
    with ExitStack() as ctx:
        def sb(name, shape, dt=F32):
            return ctx.enter_context(nc.sbuf_tensor(name, shape, dt))

        def sem(name):
            return ctx.enter_context(nc.semaphore(name))

        bank = [ctx.enter_context(nc.psum_tensor(f"bank{i}", [P, 512], F32)) for i in range(8)]

        par0 = sb("par0", [P, EARLY_W])
        par1 = sb("par1", [P, LATE_W])

        def p0(name, rows=P):
            a, w = EARLY_AT[name]
            return par0[0:rows, a:a + w]

        def p1(name, rows=P):
            a, w = LATE_AT[name]
            return par1[0:rows, a:a + w]

        ident = p0("ident")
        par0_p = [sb(f"par0_{n}", [P, EARLY_W - EARLY_KEEP], F32R) for n in ("hi", "lo")]
        par1_p = [sb(f"par1_{n}", [P, LATE_W - LATE_KEEP], F32R) for n in ("hi", "lo")]

        def parts(name):
            if name in EARLY_AT:
                a, w = EARLY_AT[name]
                return [t[:, a - EARLY_KEEP:a - EARLY_KEEP + w] for t in par0_p]
            a, w = LATE_AT[name]
            return [t[:, a - LATE_KEEP:a - LATE_KEEP + w] for t in par1_p]

        W_ORDER = ["sam", "cam", "out_s", "out_c"]
        w_raw = sb("w_raw", [P, 2, NT * C])
        w_hi = sb("w_hi", [P, len(W_ORDER), NT * C], F32R)
        w_lo = sb("w_lo", [P, len(W_ORDER), NT * C], F32R)
        ws = {n: w_raw[:, i % 2, :] for i, n in enumerate(W_ORDER)}
        wh = {n: w_hi[:, i, :] for i, n in enumerate(W_ORDER)}
        wl = {n: w_lo[:, i, :] for i, n in enumerate(W_ORDER)}
        x_sb = sb("x_sb", [P, B, HW])
        padh = {n: sb(f"padh_{n}", [P, B, HP, WP], F32R) for n in ("x", "s", "c")}
        padl = {n: sb(f"padl_{n}", [P, B, HP, WP], F32R) for n in ("x", "s", "c")}

        table_out = sb("table_out", [P, 1])
        bn_inv = sb("bn_inv", [P, 2])
        bn_shift = sb("bn_shift", [P, 2])
        bn_tmp = sb("bn_tmp", [P, 4, 2])
        xs = sb("xs", [P, B, HW])
        xc = sb("xc", [P, B, HW])
        map_a = [sb(f"map_a{i}", [P, B, HW], F32R) for i in range(2)]
        map_b = [sb(f"map_b{i}", [P, B, HW], F32R) for i in range(2)]
        qst = sb("qst", [ST, B, HW], F32R)
        kst = sb("kst", [ST, B, HW], F32R)
        vt = [sb(f"vt{i}", [P, B, NCH, C], F32R) for i in range(2)]
        ptp = [sb(f"ptp{i}", [P, B, NCH, HW], F32R) for i in range(2)]
        prob = sb("prob", [P, B, NCH, HW])
        raw = w_raw[:, :, :].rearrange("p a n -> p (a n)")
        pt_sb = raw[:, 0:B * NCH * HW].rearrange("p (b j s) -> p b j s", b=B, j=NCH)
        nmax = sb("nmax", [P, B, NCH])
        rsum = sb("rsum", [P, B, NCH])
        rinv = sb("rinv", [P, B, NCH])
        cprob = prob[:, :, 0, 0:C]
        cmax = sb("cmax", [P, B])
        cnm = sb("cnm", [P, B])
        csum = sb("csum", [P, B])
        cinv = sb("cinv", [P, B])
        att_s = sb("att_s", [P, B, HW])
        att_c = sb("att_c", [P, B, HW])
        yt = att_c

        x1 = sb("x1", [P, B, HW])
        pool1 = sb("pool1", [P, B])
        w2bd = [w[:, 0, :].rearrange("p (t o) -> p t o", t=NT) for w in (w_hi, w_lo)]
        cm2bd = sb("cm2bd", [P, P])
        w3z = sb("w3z", [P, B, C])
        b3z = sb("b3z", [P, B, C])
        spare = [p[:, :, :, :].rearrange("p b h w -> p (b h w)") for p in (padh["x"], padl["x"])]
        w3p = [t[:, 0:B * C].rearrange("p (b c) -> p b c", b=B) for t in spare]
        b3p = [t[:, B * C:2 * B * C].rearrange("p (b c) -> p b c", b=B) for t in spare]
        thr = sb("thr", [P, 3])
        hb = sb("hb", [P, 2])
        b1p3 = sb("b1p3", [MIP, 1])
        cm = sb("cm", [P, 2])
        mpad = sb("mpad", [P, HP, WP], F32R)
        ident_r = sb("ident_r", [P, P], F32R)
        hr = sb("hr", [P, 2, H, W])
        hpad = [sb(f"hpad{i}", [P, HP, WP], F32R) for i in range(2)]
        h2 = sb("h2", [P, H, W])
        h2p = [sb(f"h2p{i}", [P, H, W], F32R) for i in range(2)]
        pool2 = sb("pool2", [P, 3])
        pool3g = sb("pool3g", [P, B])
        cm3 = sb("cm3", [P, B])
        cm3s = sb("cm3s", [P, B])
        linem = sb("linem", [P, 2, H])
        lineh = sb("lineh", [P, 2, H])
        yin = sb("yin", [P, B, 2, H])
        yb = sb("yb", [MIP, B, 2, H])
        yr = sb("yr", [MIP, B, 2, H])
        ys = sb("ys", [MIP, B, 2, H])
        gate = sb("gate", [P, 2, B, H])
        gate1 = sb("gate1", [P, 2, B, H])
        t1 = xs[:, :, :].rearrange("p b (h w) -> p b h w", h=H)
        t2 = xc[:, :, :].rearrange("p b (h w) -> p b h w", h=H)
        t3 = att_s
        x2 = xc

        g_sb = sb("g_sb", [L, B, HW])
        gt = sb("gt", [P, B, NCH, L])
        gsc = sb("gsc", [P, 2])
        con_st = sb("con_st", [ST, NCON], F32R)
        wide = prob
        sa = xs
        prob2 = prob[:, :, :, 0:NCON]
        pt2 = pt_sb[0:NCON, :, 0, :]
        nmax2 = sb("nmax2", [P, B, NCH])
        rsum2 = sb("rsum2", [P, B, NCH])
        rinv2 = sb("rinv2", [P, B, NCH])
        x3 = x1

        gbv = sb("gbv", [P, 1])
        vt3 = att_s
        x3b = att_c
        y = x_sb

        d_x = [sem(f"d_x{i}") for i in range(2)]
        d_w = [[sem(f"d_w{k}_{i}") for i in range(3)] for k in range(2)]
        d_early, d_late, d_y = sem("d_early"), sem("d_late"), sem("d_y")
        ev = {n: sem(n) for n in (
            "border_x border table x_hi x_lo w_hi w_lo par0_hi par0_lo par1_hi par1_lo bn_var bn_std bn_step "
            "sam_conv cam_conv out_conv xs_done xs_hi xs_lo xc_done xc_hi xc_lo x1_done x1_hi x1_lo "
            "s_proj s_vt s_qk_hi s_qk_lo s_vt_hi s_vt_lo s_score s_max s_exp s_rinv s_norm s_tp s_pt_hi s_pt_lo "
            "s_av s_att s_hi s_lo "
            "c_yt c_yt_sb c_gram c_max c_nm c_exp c_rinv c_norm c_tp c_pt_hi c_pt_lo c_av c_att c_hi c_lo "
            "zeroed spread_raw spread_hi spread prep m_logit h1_conv cm1_logit mask m_count m_lines h1_relu "
            "h1_parts h1_hi h1_lo cm1_done h2_conv cm2_logit h2_relu h2_done h2_hi h2_lo cm2_done h2_lines h2_pool cm3_logit "
            "cm3_done line_mm yin_done y_mm y_step gate_mm gate_tanh gate_done h3_mm t1_done t2_done t3_done t3_first "
            "x2_done "
            "n_proj a_qk_hi n_qk_hi n_qk_lo n_score n_max n_exp n_rinv n_tp n_pt_sb n_av "
            "a_gt a_g a_g_sb a_wide a_out a_done con_hi con_lo "
            "e_proj e_q_hi e_q_lo e_score e_max e_exp e_rinv e_tp e_pt_sb e_av e_wide e_out e_done "
            "f_vt f_vt_sb f_norm f_xb f_done").split()}

        x_dram = x.rearrange("b c h w -> c b (h w)")
        out_dram = out.rearrange("b c h w -> c b (h w)")
        w_dram = {"sam": w_sam, "cam": w_cam, "out_s": w_out[:, 0:NT * C], "out_c": w_out[:, NT * C:2 * NT * C]}
        third = NT * C // 3
        HALF = 2 * HW

        def inner(pad, b, n=1):
            return pad[:, b:b + n, 1:1 + H, 1:1 + W]

        def flat4(ap):
            return ap.rearrange("p b (h w) -> p b h w", h=H)

        def two(t, i):
            return t[:, 2 * i:2 * i + 2, :].rearrange("p b s -> p (b s)")

        def cols(t, b):
            return t[:, b, :, :].rearrange("p j s -> p (j s)")

        def pair(t, i):
            return t[:, 2 * i:2 * i + 2, :, :].rearrange("p b j c -> p (b j c)")

        def hw(t):
            return t[:, :, :].rearrange("p h w -> p (h w)")

        block = ctx.enter_context(nc.Block())

        @block.sync
        def _(sp):
            def load_x(i):
                sp.dma_start(x_sb[:, 2 * i:2 * i + 2, :], x_dram[:, 2 * i:2 * i + 2, :]).then_inc(d_x[i], 16)

            load_x(0)
            for k, n in enumerate(W_ORDER):
                for i in range(3):
                    if k >= 2:
                        sp.wait_ge(ev["w_lo"], 3 * (k - 2) + i + 1)
                    sp.dma_start(ws[n][:, third * i:third * (i + 1)],
                                 w_dram[n][:, third * i:third * (i + 1)]).then_inc(d_w[k % 2][i], 16)
                if n == "sam":
                    load_x(1)
                    sp.dma_start(par0[:, :], early).then_inc(d_early, 16)
            sp.dma_start(par1[:, :], late).then_inc(d_late, 16)
            for b in range(B):
                sp.wait_ge(ev["f_done"], b + 1)
                sp.dma_start(out_dram[:, b, :], y[:, b, :]).then_inc(d_y, 16)
            sp.wait_ge(d_y, 16 * B)

        @block.gpsimd
        def _(pool):
            for n in ("s", "c"):
                for pad in (padh[n], padl[n]):
                    nc.gpsimd.memset(pad[:, :, 0:HP:HP - 1, :].bitcast(F32), 0.0).then_inc(ev["border"], 1)
                    nc.gpsimd.memset(pad[:, :, 1:1 + H, 0:WP:WP - 1].bitcast(F32), 0.0).then_inc(ev["border"], 1)
            nc.gpsimd.memset(mpad[:, :, :].bitcast(F32), 0.0).then_inc(ev["zeroed"], 1)
            for t in (cm2bd, w3z, b3z):
                nc.gpsimd.memset(t[:], 0.0).then_inc(ev["zeroed"], 1)
            pool.wait_ge(ev["sam_conv"], 2)
            for t in (*hpad, *w2bd):
                nc.gpsimd.memset(t[:, :, :].bitcast(F32), 0.0).then_inc(ev["zeroed"], 1)
            pool.wait_ge(ev["zeroed"], 8)
            pool.wait_ge(d_late, 16)
            n_raw = 0
            for b in range(B):
                r, c = slice(WID * b, WID * (b + 1)), slice(WID * b, WID * (b + 1))
                a = LATE_AT["w2_rep"][0]
                w2 = par1[r, a:a + NT * WID].rearrange("p (t o) -> p t o", t=NT)
                nc.gpsimd.tensor_copy(w2bd[0][r, :, c], w2).then_inc(ev["spread_hi"], 1)
                pool.wait_ge(ev["spread_hi"], b + 1)
                nc.gpsimd.tensor_tensor(w2bd[1][r, :, c], w2, w2bd[0][r, :, c].bitcast(F32),
                                        ALU.subtract).then_inc(ev["spread"], 1)
                a = LATE_AT["cm2_rep"][0]
                nc.gpsimd.tensor_copy(cm2bd[r, c], par1[r, a:a + WID]).then_inc(ev["spread_raw"], 1)
                a = LATE_AT["w3_rep"][0]
                nc.gpsimd.tensor_copy(w3z[r, b, :], par1[r, a:a + C]).then_inc(ev["spread_raw"], 1)
                a = LATE_AT["b3_row"][0]
                nc.gpsimd.tensor_copy(b3z[WID * b:WID * b + 1, b, :],
                                      par1[WID * b:WID * b + 1, a:a + C]).then_inc(ev["spread_raw"], 1)
            pool.wait_ge(ev["spread_raw"], 3 * B)
            pool.wait_ge(ev["cam_conv"], 2)
            for k, (whole, p) in enumerate(((w3z, w3p), (b3z, b3p))):
                nc.gpsimd.tensor_copy(p[0][:, :, :], whole[:, :, :]).then_inc(ev["spread_hi"], 1)
                pool.wait_ge(ev["spread_hi"], B + k + 1)
                nc.gpsimd.tensor_tensor(p[1][:, :, :], whole[:, :, :], p[0][:, :, :].bitcast(F32),
                                        ALU.subtract).then_inc(ev["spread"], 1)
            for b in range(1, B):
                pool.wait_ge(ev["t2_done"], b + 1)
                pool.wait_ge(ev["x1_done"], b + 1)
                nc.gpsimd.tensor_tensor(t3[:, b, :], t2[:, b, :, :].rearrange("p h w -> p (h w)"), x1[:, b, :],
                                        ALU.add).then_inc(ev["t3_done"], 1)
            pool.wait_ge(ev["prep"], 5)
            for b in range(B):
                pool.wait_ge(ev["e_done"], b + 1)
                nc.gpsimd.tensor_scalar(x3b[:, b, :], x3[:, b, :], gbv[:, 0:1], None, ALU.add).then_inc(ev["f_xb"], 1)

        @block.scalar
        def _(act):
            def load_table(function):
                nc.scalar.activation(table_out[:, :], hw(h2p[0]).bitcast(F32)[:, 0:1],
                                     function).then_inc(ev["table"], 1)

            act.wait_ge(ev["border_x"], 1)
            load_table(ACT.Sqrt)

            def x_high(i):
                act.wait_ge(d_x[i], 16)
                nc.scalar.copy(inner(padh["x"], 2 * i, 2), flat4(x_sb[:, 2 * i:2 * i + 2, :])).then_inc(ev["x_hi"], 1)

            def w_high(n, i):
                k = W_ORDER.index(n)
                act.wait_ge(d_w[k % 2][i], 16 * (k // 2 + 1))
                nc.scalar.copy(wh[n][:, third * i:third * (i + 1)],
                               ws[n][:, third * i:third * (i + 1)]).then_inc(ev["w_hi"], 1)

            act.wait_ge(ev["border_x"], 5)
            x_high(0)
            for i in range(3):
                w_high("sam", i)
            x_high(1)
            for i in range(3):
                w_high("cam", i)
            act.wait_ge(ev["bn_var"], 1)
            nc.scalar.activation(bn_tmp[:, 1, :], bn_tmp[:, 0, :], ACT.Sqrt).then_inc(ev["bn_std"], 1)
            nc.scalar.copy(ident_r[:, :], ident).then_inc(ev["par0_hi"], 1)
            nc.scalar.copy(par0_p[0][:, :], par0[:, EARLY_KEEP:EARLY_W]).then_inc(ev["par0_hi"], 1)
            for i in range(3):
                w_high("out_s", i)
            act.wait_ge(ev["bn_step"], 4)
            for i in range(2):
                act.wait_ge(ev["sam_conv"], i + 1)
                nc.scalar.activation(two(xs, i), bank[i][:, :], ACT.Relu, bias=bn_shift[:, 0:1],
                                     scale=bn_inv[:, 0:1]).then_inc(ev["xs_done"], 1)
                if i == 0:
                    for j in range(3):
                        w_high("out_c", j)
                    act.wait_ge(ev["table"], 1)
                    load_table(ACT.Exp)

            def qk_high(b):
                act.wait_ge(ev["s_proj"], b + 1)
                o = bank[QK_BANK[b]]
                nc.scalar.mul(qst[0:2 * GAP, b, :], o[0:2 * GAP, 0:HW], 0.25).then_inc(ev["s_qk_hi"], 1)
                nc.scalar.copy(kst[2 * GAP:ST, b, :], o[2 * GAP:ST, 0:HW]).then_inc(ev["s_qk_hi"], 1)
                nc.scalar.copy(kst[0:GAP, b, :], o[2 * GAP:ST, 0:HW]).then_inc(ev["s_qk_hi"], 1)

            def v_high(i):
                act.wait_ge(ev["s_vt"], i + 1)
                nc.scalar.copy(pair(vt[0], i), bank[6 + i][:, :]).then_inc(ev["s_vt_hi"], 1)

            def s_exp(b):
                act.wait_ge(ev["s_max"], b + 1)
                for i in range(NCH):
                    nc.scalar.activation(prob[:, b, i, :], bank[QK_BANK[b]][:, HW * i:HW * (i + 1)], ACT.Exp,
                                         bias=nmax[:, b, i:i + 1],
                                         accum_out=rsum[:, b, i:i + 1]).then_inc(ev["s_exp"], 1)

            def s_pt_high(b):
                act.wait_ge(ev["s_tp"], b + 1)
                nc.scalar.copy(cols(ptp[0], b), bank[6 + b % 2][:, :]).then_inc(ev["s_pt_hi"], 1)

            def s_high(i):
                act.wait_ge(ev["s_att"], 2 * i + 2)
                act.wait_ge(ev["border"], 8)
                nc.scalar.copy(inner(padh["s"], 2 * i, 2), flat4(att_s[:, 2 * i:2 * i + 2, :])).then_inc(ev["s_hi"], 1)

            def xc_relu(i):
                act.wait_ge(ev["cam_conv"], i + 1)
                nc.scalar.activation(two(xc, i), bank[2 + i][:, :], ACT.Relu, bias=bn_shift[:, 1:2],
                                     scale=bn_inv[:, 1:2]).then_inc(ev["xc_done"], 1)

            def turned_in(i):
                act.wait_ge(ev["c_yt"], i + 1)
                nc.scalar.copy(two(yt, i), bank[2 + i][:, :]).then_inc(ev["c_yt_sb"], 1)

            def c_exp(i):
                act.wait_ge(ev["c_nm"], i + 1)
                for b in (2 * i, 2 * i + 1):
                    nc.scalar.activation(cprob[:, b, :], bank[2 + i][:, C * (b % 2):C * (b % 2 + 1)], ACT.Exp,
                                         bias=cnm[:, b:b + 1], scale=float(HW) ** -0.5,
                                         accum_out=csum[:, b:b + 1]).then_inc(ev["c_exp"], 1)

            def c_pt_high(i):
                act.wait_ge(ev["c_tp"], i + 1)
                nc.scalar.copy(ptp[0][:, 2 * i:2 * i + 2, 0, 0:C],
                               bank[6 + i][:, 0:2 * C].rearrange("p (b c) -> p b c", b=2)).then_inc(ev["c_pt_hi"], 1)

            def c_high(i):
                act.wait_ge(ev["c_att"], i + 1)
                nc.scalar.copy(inner(padh["c"], 2 * i, 2), flat4(att_c[:, 2 * i:2 * i + 2, :])).then_inc(ev["c_hi"], 1)

            qk_high(0)
            qk_high(1)
            v_high(0)
            qk_high(2)
            qk_high(3)
            v_high(1)
            s_exp(0)
            s_exp(1)
            s_exp(2)
            s_pt_high(0)
            s_exp(3)
            s_pt_high(1)
            xc_relu(0)
            s_pt_high(2)
            s_high(0)
            s_pt_high(3)
            turned_in(0)
            s_high(1)
            c_exp(0)
            xc_relu(1)
            c_pt_high(0)
            turned_in(1)
            c_exp(1)
            c_high(0)
            c_pt_high(1)
            c_high(1)
            act.wait_ge(d_late, 16)
            nc.scalar.copy(par1_p[0][:, :], par1[:, LATE_KEEP:LATE_W]).then_inc(ev["par1_hi"], 1)
            a = LATE_AT["con_t"][0]
            nc.scalar.copy(con_st[:, :], par1[0:ST, a:a + NCON]).then_inc(ev["con_hi"], 1)

            for b in range(B):
                act.wait_ge(ev["out_conv"], max(1, b))
                nc.scalar.activation(x1[:, b, :], bank[OUT_BANK[b]][:, HW * (b == 1):HW * (b == 1) + HW], ACT.Copy,
                                     accum_out=pool1[:, b:b + 1]).then_inc(ev["x1_done"], 1)
            act.wait_ge(ev["h1_conv"], 1)
            nc.scalar.activation(hr[:, 0, :, :].rearrange("p h w -> p (h w)"), bank[3][:, 0:HW], ACT.Relu,
                                 bias=p1("b1")).then_inc(ev["h1_relu"], 1)
            act.wait_ge(ev["h2_conv"], 1)
            nc.scalar.activation(hr[:, 1, :, :].rearrange("p h w -> p (h w)"), bank[5][:, 0:HW], ACT.Relu,
                                 bias=p1("b2")).then_inc(ev["h2_relu"], 1)
            act.wait_ge(ev["gate_mm"], 1)
            act.wait_ge(ev["prep"], 2)
            for i in range(2):
                nc.scalar.activation(gate[:, i, :, :].rearrange("p b h -> p (b h)"),
                                     bank[3][:, B * H * i:B * H * (i + 1)], ACT.Tanh, bias=hb[:, i:i + 1],
                                     scale=1.0 / 12).then_inc(ev["gate_tanh"], 1)

            def relu_x2(b):
                act.wait_ge(ev["t3_done" if b else "t3_first"], max(b, 1))
                nc.scalar.activation(x2[:, b, :], t3[:, b, :], ACT.Relu).then_inc(ev["x2_done"], 1)

            def lead_scale(b):
                act.wait_ge(ev["n_proj"], b + 1)
                o = bank[2 * b]
                nc.scalar.mul(qst[0:2 * GAP, b, :], o[0:2 * GAP, 0:HW], 1.0 / C).then_inc(ev["a_qk_hi"], 1)
                nc.scalar.copy(kst[2 * GAP:ST, b, :], o[2 * GAP:ST, 0:HW]).then_inc(ev["a_qk_hi"], 1)
                nc.scalar.copy(kst[0:GAP, b, :], o[2 * GAP:ST, 0:HW]).then_inc(ev["a_qk_hi"], 1)

            def values(b):
                act.wait_ge(ev["n_proj"], b + 1)
                nc.scalar.copy(g_sb[:, b, :], bank[2 * b][ST:ST + L, 0:HW]).then_inc(ev["a_gt"], 1)

            def turned_values(b):
                act.wait_ge(ev["a_g"], b + 1)
                nc.scalar.copy(gt[:, b, :, :].rearrange("p j l -> p (j l)"),
                               bank[2 * b + 1][:, 0:NCH * L]).then_inc(ev["a_g_sb"], 1)

            def exp_self(b, k=0):
                act.wait_ge(ev["n_max"], k + b + 1)
                o = bank[2 * b + k // B]
                for i in range(NCH):
                    nc.scalar.activation(prob[:, b, i, :], o[:, HW * i:HW * (i + 1)], ACT.Exp,
                                         bias=nmax[:, b, i:i + 1],
                                         accum_out=rsum[:, b, i:i + 1]).then_inc(ev["n_exp"], 1)

            def turned_self(b, k=0):
                act.wait_ge(ev["n_tp"], k + b + 1)
                nc.scalar.copy(cols(pt_sb, b), bank[2 * b + 1 - k // B][:, :]).then_inc(ev["n_pt_sb"], 1)

            def lead_query(b):
                act.wait_ge(ev["e_proj"], b + 1)
                nc.scalar.mul(qst[0:2 * GAP, b, :], bank[2 * b][0:2 * GAP, 0:HW],
                              float(C) ** -0.5).then_inc(ev["e_q_hi"], 1)

            def exp_concepts(b):
                act.wait_ge(ev["e_max"], b + 1)
                for i in range(NCH):
                    nc.scalar.activation(prob2[:, b, i, :], bank[2 * b + 1][:, NCON * i:NCON * (i + 1)], ACT.Exp,
                                         bias=nmax2[:, b, i:i + 1],
                                         accum_out=rsum2[:, b, i:i + 1]).then_inc(ev["e_exp"], 1)

            def turned_concepts(b):
                act.wait_ge(ev["e_tp"], b + 1)
                nc.scalar.copy(pt2[:, b, :], bank[2 * b][0:NCON, 0:HW]).then_inc(ev["e_pt_sb"], 1)

            def lead_bias(b):
                act.wait_ge(ev["n_proj"], B + b + 1)
                nc.scalar.activation(qst[:, b, :], bank[2 * b + 1][0:ST, 0:HW], ACT.Identity,
                                     bias=p1("bq", ST)).then_inc(ev["n_qk_hi"], 1)
                nc.scalar.activation(kst[:, b, :], bank[2 * b + 1][0:ST, HW:2 * HW], ACT.Identity,
                                     bias=p1("bk", ST)).then_inc(ev["n_qk_hi"], 1)

            def values3(b):
                act.wait_ge(ev["f_vt"], b + 1)
                nc.scalar.copy(vt3[:, b, :], bank[2 * b][:, 0:NCH * C]).then_inc(ev["f_vt_sb"], 1)

            def exp_last(b):
                exp_self(b, B)

            def turned_last(b):
                turned_self(b, B)

            for step, b in ((relu_x2, 0), (relu_x2, 1), (lead_scale, 0), (values, 0), (values, 1), (lead_scale, 1),
                            (turned_values, 0), (turned_values, 1), (relu_x2, 2), (relu_x2, 3), (exp_self, 0),
                            (lead_scale, 2), (turned_self, 0), (exp_self, 1), (values, 2), (lead_scale, 3),
                            (turned_self, 1), (turned_values, 2), (values, 3), (exp_self, 2), (turned_values, 3),
                            (lead_query, 0), (turned_self, 2), (exp_self, 3), (lead_query, 1), (turned_self, 3),
                            (exp_concepts, 0), (turned_concepts, 0), (lead_query, 2), (exp_concepts, 1),
                            (turned_concepts, 1), (exp_concepts, 2), (lead_query, 3), (turned_concepts, 2),
                            (lead_bias, 0), (exp_concepts, 3), (values3, 0), (turned_concepts, 3), (exp_last, 0),
                            (values3, 1), (lead_bias, 1), (lead_bias, 2), (values3, 2), (lead_bias, 3),
                            (turned_last, 0), (exp_last, 1), (values3, 3), (exp_last, 2), (turned_last, 1),
                            (exp_last, 3), (turned_last, 2), (turned_last, 3)):
                step(b)
        @block.vector
        def _(dve):
            def low(out_ap, whole, hi):
                return nc.vector.tensor_tensor(out_ap, whole, hi.bitcast(F32), ALU.subtract)

            nc.vector.memset(h2p[0][:, :, :].bitcast(F32), 0.0).then_inc(ev["border_x"], 1)
            for pad in (padh["x"], padl["x"]):
                nc.vector.memset(pad[:, :, 0:HP:HP - 1, :].bitcast(F32), 0.0).then_inc(ev["border_x"], 1)
                nc.vector.memset(pad[:, :, 1:1 + H, 0:WP:WP - 1].bitcast(F32), 0.0).then_inc(ev["border_x"], 1)

            def x_low(i):
                dve.wait_ge(ev["x_hi"], i + 1)
                low(inner(padl["x"], 2 * i, 2), flat4(x_sb[:, 2 * i:2 * i + 2, :]),
                    inner(padh["x"], 2 * i, 2)).then_inc(ev["x_lo"], 1)

            def w_low(n, i):
                dve.wait_ge(ev["w_hi"], 3 * W_ORDER.index(n) + i + 1)
                c = slice(third * i, third * (i + 1))
                low(wl[n][:, c], ws[n][:, c], wh[n][:, c]).then_inc(ev["w_lo"], 1)

            def map_split(whole, m, i, done, hi, lo):
                dve.wait_ge(done, i + 1)
                nc.vector.tensor_copy(two(m[0], i), two(whole, i)).then_inc(hi, 1)
                dve.wait_ge(hi, i + 1)
                low(two(m[1], i), two(whole, i), two(m[0], i)).then_inc(lo, 1)

            x_low(0)
            for i in range(3):
                w_low("sam", i)
            x_low(1)
            dve.wait_ge(d_early, 16)
            nc.vector.tensor_scalar(bn_tmp[:, 0, :], p0("bn_var"), 1e-5, None, ALU.add).then_inc(ev["bn_var"], 1)
            for i in range(3):
                w_low("cam", i)
            dve.wait_ge(ev["bn_std"], 1)
            nc.vector.reciprocal(bn_tmp[:, 2, :], bn_tmp[:, 1, :]).then_inc(ev["bn_step"], 1)
            dve.wait_ge(ev["bn_step"], 1)
            nc.vector.tensor_tensor(bn_inv[:, :], bn_tmp[:, 2, :], p0("bn_scale"), ALU.mult).then_inc(ev["bn_step"], 1)
            dve.wait_ge(ev["bn_step"], 2)
            nc.vector.tensor_tensor(bn_tmp[:, 3, :], bn_inv[:, :], p0("bn_mean"), ALU.mult).then_inc(ev["bn_step"], 1)
            dve.wait_ge(ev["bn_step"], 3)
            nc.vector.tensor_tensor(bn_shift[:, :], p0("bn_bias"), bn_tmp[:, 3, :],
                                    ALU.subtract).then_inc(ev["bn_step"], 1)
            dve.wait_ge(ev["par0_hi"], 2)
            low(par0_p[1][:, :], par0[:, EARLY_KEEP:EARLY_W], par0_p[0][:, :]).then_inc(ev["par0_lo"], 1)
            for i in range(3):
                w_low("out_s", i)
            map_split(xs, map_a, 0, ev["xs_done"], ev["xs_hi"], ev["xs_lo"])
            for i in range(3):
                w_low("out_c", i)
            map_split(xs, map_a, 1, ev["xs_done"], ev["xs_hi"], ev["xs_lo"])

            def qk_low(b):
                dve.wait_ge(ev["s_qk_hi"], 3 * b + 1)
                o = bank[QK_BANK[b]]
                nc.vector.scalar_tensor_tensor(qst[2 * GAP:ST, b, :], o[0:GAP, 0:HW], 0.25,
                                               qst[0:GAP, b, :].bitcast(F32), ALU.mult,
                                               ALU.subtract).then_inc(ev["s_qk_lo"], 1)
                dve.wait_ge(ev["s_qk_hi"], 3 * (b + 1))
                low(kst[GAP:2 * GAP, b, :], o[2 * GAP:ST, 0:HW], kst[2 * GAP:ST, b, :]).then_inc(ev["s_qk_lo"], 1)

            def v_low(i):
                dve.wait_ge(ev["s_vt_hi"], i + 1)
                low(pair(vt[1], i), bank[6 + i][:, :], pair(vt[0], i)).then_inc(ev["s_vt_lo"], 1)

            def s_max(b):
                dve.wait_ge(ev["s_score"], b + 1)
                nc.vector.tensor_reduce(nmax[:, b, :], bank[QK_BANK[b]][:, :].rearrange("p (i s) -> p i s", i=NCH),
                                        AX.X, ALU.max, negate=True).then_inc(ev["s_max"], 1)

            def s_norm(b):
                dve.wait_ge(ev["s_exp"], NCH * (b + 1))
                nc.vector.reciprocal(rinv[:, b, :], rsum[:, b, :]).then_inc(ev["s_rinv"], 1)
                dve.wait_ge(ev["s_rinv"], b + 1)
                for i in range(NCH):
                    nc.vector.tensor_scalar(prob[:, b, i, :], prob[:, b, i, :], rinv[:, b, i:i + 1], None,
                                            ALU.mult).then_inc(ev["s_norm"], 1)

            def s_pt_low(b):
                dve.wait_ge(ev["s_pt_hi"], b + 1)
                low(cols(ptp[1], b), bank[6 + b % 2][:, :], cols(ptp[0], b)).then_inc(ev["s_pt_lo"], 1)

            def s_residual(b):
                dve.wait_ge(ev["s_av"], b + 1)
                nc.vector.scalar_tensor_tensor(att_s[:, b, :], bank[4 + b % 2][:, 0:HW], p0("gam_sam"), xs[:, b, :],
                                               ALU.mult, ALU.add).then_inc(ev["s_att"], 1)

            def s_low(i):
                dve.wait_ge(ev["s_hi"], i + 1)
                low(inner(padl["s"], 2 * i, 2), flat4(att_s[:, 2 * i:2 * i + 2, :]),
                    inner(padh["s"], 2 * i, 2)).then_inc(ev["s_lo"], 1)

            def c_max(i):
                c = slice(2 * i, 2 * i + 2)
                dve.wait_ge(ev["c_gram"], i + 1)
                nc.vector.tensor_reduce(cmax[:, c], bank[2 + i][:, 0:2 * C].rearrange("p (b c) -> p b c", b=2), AX.X,
                                        ALU.max).then_inc(ev["c_max"], 1)
                dve.wait_ge(ev["c_max"], i + 1)
                nc.vector.tensor_scalar(cnm[:, c], cmax[:, c], -float(HW) ** -0.5, None,
                                        ALU.mult).then_inc(ev["c_nm"], 1)

            def c_norm(i):
                dve.wait_ge(ev["c_exp"], 2 * (i + 1))
                c = slice(2 * i, 2 * i + 2)
                nc.vector.reciprocal(cinv[:, c], csum[:, c]).then_inc(ev["c_rinv"], 1)
                dve.wait_ge(ev["c_rinv"], i + 1)
                for b in (2 * i, 2 * i + 1):
                    nc.vector.tensor_scalar(cprob[:, b, :], cprob[:, b, :], cinv[:, b:b + 1], None,
                                            ALU.mult).then_inc(ev["c_norm"], 1)

            def c_pt_low(i):
                dve.wait_ge(ev["c_pt_hi"], i + 1)
                c = slice(2 * i, 2 * i + 2)
                low(ptp[1][:, c, 0, 0:C], bank[6 + i][:, 0:2 * C].rearrange("p (b c) -> p b c", b=2),
                    ptp[0][:, c, 0, 0:C]).then_inc(ev["c_pt_lo"], 1)

            def c_residual(i):
                dve.wait_ge(ev["c_av"], i + 1)
                nc.vector.scalar_tensor_tensor(two(att_c, i), bank[4 + i][:, :], p0("gam_cam"), two(xc, i),
                                               ALU.mult, ALU.add).then_inc(ev["c_att"], 1)

            def c_low(i):
                dve.wait_ge(ev["c_hi"], i + 1)
                low(inner(padl["c"], 2 * i, 2), flat4(att_c[:, 2 * i:2 * i + 2, :]),
                    inner(padh["c"], 2 * i, 2)).then_inc(ev["c_lo"], 1)

            qk_low(0)
            qk_low(1)
            v_low(0)
            qk_low(2)
            qk_low(3)
            v_low(1)
            s_max(0)
            s_max(1)
            s_max(2)
            s_norm(0)
            s_max(3)
            s_norm(1)
            s_norm(2)
            s_pt_low(0)
            s_norm(3)
            s_pt_low(1)
            s_residual(0)
            s_pt_low(2)
            s_residual(1)
            s_pt_low(3)
            s_low(0)
            map_split(xc, map_b, 0, ev["xc_done"], ev["xc_hi"], ev["xc_lo"])
            s_residual(2)
            s_residual(3)
            c_max(0)
            s_low(1)
            c_norm(0)
            c_pt_low(0)
            map_split(xc, map_b, 1, ev["xc_done"], ev["xc_hi"], ev["xc_lo"])
            c_residual(0)
            c_max(1)
            c_norm(1)
            c_low(0)
            c_pt_low(1)
            c_residual(1)
            c_low(1)

            dve.wait_ge(ev["par1_hi"], 1)
            low(par1_p[1][:, :], par1[:, LATE_KEEP:LATE_W], par1_p[0][:, :]).then_inc(ev["par1_lo"], 1)
            a = LATE_AT["con_t"][0]
            dve.wait_ge(ev["con_hi"], 1)
            low(con_st[GAP:2 * GAP, :], par1[GAP:2 * GAP, a:a + NCON], con_st[GAP:2 * GAP, :]).then_inc(ev["con_lo"], 1)
            a = LATE_AT["cm1_b"][0]
            nc.vector.tensor_scalar(thr[:, :], par1[:, a:a + 3], -float(HW), None, ALU.mult).then_inc(ev["prep"], 1)
            a = LATE_AT["ca_bh"][0]
            nc.vector.tensor_scalar(hb[:, :], par1[:, a:a + 2], 0.5, None, ALU.mult).then_inc(ev["prep"], 1)
            nc.vector.tensor_scalar(gsc[:, 0:1], p1("gam_sa"), L ** -0.5 * float(C) ** -0.5, None,
                                    ALU.mult).then_inc(ev["prep"], 1)
            nc.vector.tensor_scalar(gsc[:, 1:2], p1("gam_moca"), L ** -0.5, None, ALU.mult).then_inc(ev["prep"], 1)
            nc.vector.tensor_tensor(gbv[:, :], p1("gam3"), p1("bv"), ALU.mult).then_inc(ev["prep"], 1)
            nc.vector.tensor_scalar(b1p3[:, :], p1("ca_b1", MIP), 3.0, None, ALU.add).then_inc(ev["prep"], 1)

            for b in range(B - 1):
                dve.wait_ge(ev["x1_done"], b + 1)
                nc.vector.tensor_copy(map_a[0][:, b, :], x1[:, b, :]).then_inc(ev["x1_hi"], 1)
                dve.wait_ge(ev["x1_hi"], b + 1)
                low(map_a[1][:, b, :], x1[:, b, :], map_a[0][:, b, :]).then_inc(ev["x1_lo"], 1)
            inside = lambda t: t[:, 1:1 + H, 1:1 + W]
            dve.wait_ge(ev["m_logit"], 1)
            dve.wait_ge(ev["zeroed"], 8)
            nc.vector.tensor_scalar(inside(mpad), bank[2][:, 0:HW].rearrange("p (h w) -> p h w", h=H),
                                    p1("sm_b"), 0.0, ALU.add, ALU.is_gt).then_inc(ev["mask"], 1)
            dve.wait_ge(ev["cm1_logit"], 1)
            nc.vector.tensor_scalar(cm[:, 0:1], bank[4][:, 0:1], thr[:, 0:1], None,
                                    ALU.is_gt).then_inc(ev["cm1_done"], 1)
            dve.wait_ge(ev["cm1_done"], 1)
            dve.wait_ge(ev["h1_relu"], 1)
            nc.vector.tensor_scalar(h2p[0][:, :, :], hr[:, 0, :, :], cm[:, 0:1], None,
                                    ALU.mult).then_inc(ev["h1_hi"], 1)
            dve.wait_ge(ev["h1_hi"], 1)
            nc.vector.scalar_tensor_tensor(h2p[1][:, :, :], hr[:, 0, :, :], cm[:, 0:1], h2p[0][:, :, :].bitcast(F32),
                                           ALU.mult, ALU.subtract).then_inc(ev["h1_lo"], 1)
            dve.wait_ge(ev["m_count"], 1)
            dve.wait_ge(ev["h1_lo"], 1)
            for k in range(2):
                nc.vector.scalar_tensor_tensor(inside(hpad[k]),
                                               bank[7][:, 0:HW].rearrange("p (h w) -> p h w", h=H), 0.0,
                                               h2p[k][:, :, :].bitcast(F32), ALU.is_gt, ALU.mult,
                                               accum_out=pool2[:, k:k + 1]).then_inc(ev["h1_parts"], 1)
            dve.wait_ge(ev["mask"], 1)
            m = inside(mpad).bitcast(F32)
            nc.vector.tensor_reduce(linem[:, 0, :], m, AX.X, ALU.add).then_inc(ev["m_lines"], 1)
            nc.vector.tensor_reduce(linem[:, 1, :], m.rearrange("p h w -> p w h"), AX.X,
                                    ALU.add).then_inc(ev["m_lines"], 1)
            dve.wait_ge(ev["cm2_logit"], 1)
            nc.vector.tensor_scalar(cm[:, 1:2], bank[0][:, 0:1], thr[:, 1:2], None,
                                    ALU.is_gt).then_inc(ev["cm2_done"], 1)
            dve.wait_ge(ev["cm2_done"], 1)
            dve.wait_ge(ev["h2_relu"], 1)
            nc.vector.scalar_tensor_tensor(h2[:, :, :], hr[:, 1, :, :], cm[:, 1:2], m,
                                           ALU.mult, ALU.mult, accum_out=pool2[:, 2:3]).then_inc(ev["h2_done"], 1)
            dve.wait_ge(ev["h2_done"], 1)
            nc.vector.tensor_scalar(pool3g[:, :], p1("group"), pool2[:, 2:3], None, ALU.mult).then_inc(ev["h2_pool"], 1)
            nc.vector.tensor_reduce(lineh[:, 0, :], h2[:, :, :], AX.X, ALU.add).then_inc(ev["h2_lines"], 1)
            nc.vector.tensor_reduce(lineh[:, 1, :], h2[:, :, :].rearrange("p h w -> p w h"), AX.X,
                                    ALU.add).then_inc(ev["h2_lines"], 1)
            dve.wait_ge(ev["cm3_logit"], 1)
            nc.vector.tensor_scalar(cm3[:, :], bank[1][:, 0:B], thr[:, 2:3], None,
                                    ALU.is_gt).then_inc(ev["cm3_done"], 1)
            dve.wait_ge(ev["cm3_done"], 1)
            nc.vector.tensor_scalar(cm3s[:, :], cm3[:, :], 1.0 / W, None, ALU.mult).then_inc(ev["cm3_done"], 1)
            nc.vector.tensor_copy(h2p[0][:, :, :], h2[:, :, :]).then_inc(ev["h2_hi"], 1)
            dve.wait_ge(ev["h2_hi"], 1)
            low(h2p[1][:, :, :], h2[:, :, :], h2p[0][:, :, :]).then_inc(ev["h2_lo"], 1)
            dve.wait_ge(ev["cm3_done"], 2)
            dve.wait_ge(ev["line_mm"], 1)
            nc.vector.tensor_tensor(yin[:, :, :, :].rearrange("p b i h -> p b (i h)"),
                                    bank[0][:, 0:B * 2 * H].rearrange("p (b l) -> p b l", b=B),
                                    cm3s[:, :].unsqueeze(2).broadcast_to([P, B, 2 * H]),
                                    ALU.mult).then_inc(ev["yin_done"], 1)
            f = lambda t: t[:, :, :, :].rearrange("p b i h -> p (b i h)")
            dve.wait_ge(ev["y_mm"], 1)
            dve.wait_ge(ev["prep"], 6)
            nc.vector.tensor_scalar(f(yb), bank[2][0:MIP, 0:B * 2 * H], p1("ca_b1", MIP), None,
                                    ALU.add).then_inc(ev["y_step"], 1)
            nc.vector.tensor_scalar(f(yr), bank[2][0:MIP, 0:B * 2 * H], b1p3[:, :], 0.0, ALU.add,
                                    ALU.max).then_inc(ev["y_step"], 1)
            dve.wait_ge(ev["y_step"], 2)
            nc.vector.scalar_tensor_tensor(f(ys), f(yr), 6.0, f(yb), ALU.min, ALU.mult).then_inc(ev["y_step"], 1)
            dve.wait_ge(ev["gate_tanh"], 2)
            nc.vector.tensor_scalar(gate1[:, :, :, :].rearrange("p i b h -> p (i b h)"),
                                    gate[:, :, :, :].rearrange("p i b h -> p (i b h)"), 1.0, None,
                                    ALU.add).then_inc(ev["gate_done"], 1)
            dve.wait_ge(ev["gate_done"], 1)
            nc.vector.scalar_tensor_tensor(gate[:, 0, :, :], gate1[:, 0, :, :], 0.25,
                                           cm3[:, :].unsqueeze(2).broadcast_to([P, B, H]), ALU.mult,
                                           ALU.mult).then_inc(ev["gate_done"], 1)
            dve.wait_ge(ev["gate_done"], 2)
            dve.wait_ge(ev["h3_mm"], 1)

            def gate_rows(b):
                nc.vector.tensor_tensor(t1[:, b, :, :],
                                        bank[6 + b // 2][:, HW * (b % 2):HW * (b % 2 + 1)].rearrange(
                                            "p (h w) -> p h w", h=H),
                                        gate[:, 0, b, :].unsqueeze(2).broadcast_to([P, H, W]),
                                        ALU.mult).then_inc(ev["t1_done"], 1)

            def gate_columns(b):
                dve.wait_ge(ev["t1_done"], b + 1)
                nc.vector.tensor_tensor(t2[:, b, :, :], t1[:, b, :, :],
                                        gate1[:, 1, b, :].unsqueeze(1).broadcast_to([P, H, W]),
                                        ALU.mult).then_inc(ev["t2_done"], 1)

            def gated(b):
                gate_rows(b)
                gate_columns(b)

            gate_rows(0)
            gate_rows(1)
            gate_columns(0)
            gate_columns(1)
            dve.wait_ge(ev["t2_done"], 1)
            nc.vector.tensor_tensor(t3[:, 0, :], t2[:, 0, :, :].rearrange("p h w -> p (h w)"), x1[:, 0, :],
                                    ALU.add).then_inc(ev["t3_first"], 1)

            def rest_scale(b):
                o = bank[2 * b]
                dve.wait_ge(ev["a_qk_hi"], 3 * b + 1)
                nc.vector.scalar_tensor_tensor(qst[2 * GAP:ST, b, :], o[0:GAP, 0:HW], 1.0 / C,
                                               qst[0:GAP, b, :].bitcast(F32), ALU.mult,
                                               ALU.subtract).then_inc(ev["n_qk_lo"], 1)
                dve.wait_ge(ev["a_qk_hi"], 3 * (b + 1))
                low(kst[GAP:2 * GAP, b, :], o[2 * GAP:ST, 0:HW], kst[2 * GAP:ST, b, :]).then_inc(ev["n_qk_lo"], 1)

            def max_self(b, k=0):
                dve.wait_ge(ev["n_score"], k + b + 1)
                o = bank[2 * b + k // B]
                nc.vector.tensor_reduce(nmax[:, b, :], o[:, :].rearrange("p (i s) -> p i s", i=NCH),
                                        AX.X, ALU.max, negate=True).then_inc(ev["n_max"], 1)

            sel = p1("sel16").unsqueeze(1).broadcast_to([P, L, L]).rearrange("p m l -> p l m")

            def spread_rows(b, o, ri, done):
                for i in range(NCH):
                    nc.vector.scalar_tensor_tensor(wide[:, b, i, :].rearrange("p (l m) -> p l m", l=L),
                                                   o[:, L * i:L * (i + 1)].unsqueeze(1).broadcast_to([P, L, L]),
                                                   ri[:, b, i:i + 1], sel, ALU.mult, ALU.mult).then_inc(done, 1)

            def inverse_self(b, k=0):
                dve.wait_ge(ev["n_exp"], NCH * (k + b + 1))
                nc.vector.reciprocal(rinv[:, b, :], rsum[:, b, :]).then_inc(ev["n_rinv"], 1)

            def spread_self(b):
                dve.wait_ge(ev["n_rinv"], b + 1)
                dve.wait_ge(ev["n_av"], b + 1)
                spread_rows(b, bank[2 * b], rinv, ev["a_wide"])

            def add_self(b):
                dve.wait_ge(ev["a_out"], b + 1)
                dve.wait_ge(ev["x2_done"], b + 1)
                nc.vector.scalar_tensor_tensor(sa[:, b, :], bank[2 * b + 1][:, 0:HW], gsc[:, 0:1],
                                               x2[:, b, :], ALU.mult, ALU.add).then_inc(ev["a_done"], 1)

            def rest_query(b):
                dve.wait_ge(ev["e_q_hi"], b + 1)
                nc.vector.scalar_tensor_tensor(qst[2 * GAP:ST, b, :], bank[2 * b][0:GAP, 0:HW],
                                               float(C) ** -0.5, qst[0:GAP, b, :].bitcast(F32), ALU.mult,
                                               ALU.subtract).then_inc(ev["e_q_lo"], 1)

            def max_concepts(b):
                dve.wait_ge(ev["e_score"], b + 1)
                nc.vector.tensor_reduce(nmax2[:, b, :],
                                        bank[2 * b + 1][:, 0:NCH * NCON].rearrange("p (i s) -> p i s", i=NCH), AX.X,
                                        ALU.max, negate=True).then_inc(ev["e_max"], 1)

            def inverse_concepts(b):
                dve.wait_ge(ev["e_exp"], NCH * (b + 1))
                nc.vector.reciprocal(rinv2[:, b, :], rsum2[:, b, :]).then_inc(ev["e_rinv"], 1)

            def spread_concepts(b):
                dve.wait_ge(ev["e_rinv"], b + 1)
                dve.wait_ge(ev["e_av"], b + 1)
                spread_rows(b, bank[2 * b + 1], rinv2, ev["e_wide"])

            def add_concepts(b):
                dve.wait_ge(ev["e_out"], b + 1)
                nc.vector.scalar_tensor_tensor(x3[:, b, :], bank[2 * b][:, 0:HW], gsc[:, 1:2],
                                               sa[:, b, :], ALU.mult, ALU.add).then_inc(ev["e_done"], 1)

            def rest_bias(b):
                dve.wait_ge(ev["n_qk_hi"], 2 * (b + 1))
                o = bank[2 * b + 1]
                at = LATE_AT["bq"][0]
                nc.vector.scalar_tensor_tensor(qst[2 * GAP:ST, b, :], o[2 * GAP:ST, 0:HW],
                                               par1[2 * GAP:ST, at:at + 1], qst[2 * GAP:ST, b, :].bitcast(F32),
                                               ALU.add, ALU.subtract).then_inc(ev["n_qk_lo"], 1)
                at = LATE_AT["bk"][0]
                nc.vector.scalar_tensor_tensor(kst[GAP:2 * GAP, b, :], o[GAP:2 * GAP, HW:2 * HW],
                                               par1[GAP:2 * GAP, at:at + 1], kst[GAP:2 * GAP, b, :].bitcast(F32),
                                               ALU.add, ALU.subtract).then_inc(ev["n_qk_lo"], 1)

            def max_last(b):
                max_self(b, B)

            def normalise_last(b):
                inverse_self(b, B)
                dve.wait_ge(ev["n_rinv"], B + b + 1)
                for i in range(NCH):
                    nc.vector.tensor_scalar(prob[:, b, i, :], prob[:, b, i, :], rinv[:, b, i:i + 1], None,
                                            ALU.mult).then_inc(ev["f_norm"], 1)

            def add_last(b):
                dve.wait_ge(ev["n_av"], B + b + 1)
                dve.wait_ge(ev["f_xb"], b + 1)
                nc.vector.scalar_tensor_tensor(y[:, b, :], bank[2 * b + 1][:, 0:HW], p1("gam3"),
                                               x3b[:, b, :], ALU.mult, ALU.add).then_inc(ev["f_done"], 1)

            for step, b in ((gated, 2), (gated, 3), (rest_scale, 0), (max_self, 0), (rest_scale, 1),
                            (inverse_self, 0), (max_self, 1), (rest_scale, 2), (inverse_self, 1), (spread_self, 0),
                            (max_self, 2), (rest_scale, 3), (add_self, 0), (spread_self, 1), (inverse_self, 2),
                            (max_self, 3), (rest_query, 0), (add_self, 1), (inverse_self, 3), (spread_self, 2),
                            (rest_query, 1), (max_concepts, 0), (add_self, 2), (inverse_concepts, 0),
                            (spread_self, 3), (max_concepts, 1), (rest_query, 2), (spread_concepts, 0),
                            (inverse_concepts, 1), (add_self, 3), (max_concepts, 2), (add_concepts, 0),
                            (inverse_concepts, 2), (rest_query, 3), (spread_concepts, 1), (max_concepts, 3),
                            (spread_concepts, 2), (rest_bias, 0), (add_concepts, 1), (inverse_concepts, 3),
                            (add_concepts, 2), (spread_concepts, 3), (max_last, 0), (add_concepts, 3),
                            (normalise_last, 0), (rest_bias, 1), (rest_bias, 2), (max_last, 1), (rest_bias, 3),
                            (max_last, 2), (normalise_last, 1), (max_last, 3), (normalise_last, 2), (add_last, 0),
                            (normalise_last, 3), (add_last, 1), (add_last, 2), (add_last, 3)):
                step(b)
        @block.tensor
        def _(pe):
            mm = nc.tensor.matmul

            def mm3(o, w, v, first=True, last=True):
                mm(o, w[0], v[0], start=first, stop=False, skip_group_check=True)
                mm(o, w[0], v[1], start=False, stop=False, skip_group_check=True)
                return mm(o, w[1], v[0], start=False, stop=last, skip_group_check=True)

            def tap(n, pad, o, half, t, first, last):
                dy, dx = TAPS[t]
                v = [p[:, 2 * half:2 * half + 2, dy:dy + H, dx:dx + W] for p in (padh[pad], padl[pad])]
                c = slice(C * t, C * (t + 1))
                return mm3(o[:, :].rearrange("p (b h w) -> p b h w", b=2, h=H), (wh[n][:, c], wl[n][:, c]), v,
                           first, last)

            def tap_batch(n, pad, b, t, first, last):
                dy, dx = TAPS[t]
                c = slice(C * t, C * (t + 1))
                return mm3(bank[OUT_BANK[b]][:, 0:HW].rearrange("p (h w) -> p h w", h=H), (wh[n][:, c], wl[n][:, c]),
                           [p[:, b, dy:dy + H, dx:dx + W] for p in (padh[pad], padl[pad])], first, last)

            def weights_split(n, t):
                pe.wait_ge(ev["w_lo"], 3 * W_ORDER.index(n) + t // 3 + 1)

            def batch(m, b):
                return [p[:, b, :] for p in m]

            def transposes(o, b, done, before):
                for i in range(NCH):
                    pe.wait_ge(done, before + i + 1)
                    for j in range(NCH):
                        m = nc.tensor.transpose(o[:, HW * j + P * i:HW * j + P * (i + 1)],
                                                prob[:, b, i, P * j:P * (j + 1)], ident)
                return m

            def keep_clock(k, n, t=None):
                t = wh["out_c"][:, 0:2 * P] if t is None else t
                for _ in range(n):
                    mm(bank[k][:, 0:t.shape[-1]], t[:, 0:P], t[:, :], start=True, stop=True, skip_group_check=True)

            pe.wait_ge(ev["border_x"], 1)
            keep_clock(7, START, hw(h2p[0]))
            for k, (w, p) in enumerate(((wh, padh), (wh, padl), (wl, padh))):
                if k == 0:
                    pe.wait_ge(ev["x_hi"], 1)
                    pe.wait_ge(ev["w_hi"], 1)
                elif k == 1:
                    pe.wait_ge(ev["x_lo"], 1)
                else:
                    pe.wait_ge(ev["w_lo"], 1)
                for t in range(3):
                    dy, dx = TAPS[t]
                    mm(bank[0][:, :].rearrange("p (b h w) -> p b h w", b=2, h=H), w["sam"][:, C * t:C * (t + 1)],
                       p["x"][:, 0:2, dy:dy + H, dx:dx + W], start=(k == 0 and t == 0), stop=False,
                       skip_group_check=True)
            for half in range(2):
                pe.wait_ge(ev["x_lo"], half + 1)
                for t in range(0 if half else 3, NT):
                    if half == 0 and t % 3 == 0:
                        weights_split("sam", t)
                    m = tap("sam", "x", bank[half], half, t, t == 0, t == NT - 1)
                m.then_inc(ev["sam_conv"], 1)

            def cam_taps(k0, k1):
                for k in range(k0, k1):
                    half, t = divmod(k, NT)
                    if t % 3 == 0:
                        weights_split("cam", t)
                    m = tap("cam", "x", bank[2 + half], half, t, t == 0, t == NT - 1)
                    if t == NT - 1:
                        m.then_inc(ev["cam_conv"], 1)

            def out_s_taps(k0, k1):
                for k in range(k0, k1):
                    half, t = divmod(k, NT)
                    if t == 0:
                        pe.wait_ge(ev["s_lo"], half + 1)
                    if t % 3 == 0:
                        weights_split("out_s", t)
                    if half == 0:
                        tap("out_s", "s", bank[0], half, t, t == 0, False)
                    else:
                        for b in (2, 3):
                            tap_batch("out_s", "s", b, t, t == 0, False)

            def qk(b):
                pe.wait_ge(ev["xs_lo"], b // 2 + 1)
                o = bank[QK_BANK[b]]
                mm3(o[0:ST, 0:HW], parts("w_qk"), batch(map_a, b)).then_inc(ev["s_proj"], 1)

            def v(i):
                pe.wait_ge(ev["xs_done"], i + 1)
                for b in (2 * i, 2 * i + 1):
                    for j in range(NCH):
                        c = C * (NCH * (b % 2) + j)
                        m = mm(bank[6 + i][:, c:c + C], xs[:, b, P * j:P * (j + 1)], p0("w_v"), start=True,
                               stop=True)
                m.then_inc(ev["s_vt"], 1)

            def s_score(b):
                pe.wait_ge(ev["s_qk_lo"], 2 * (b + 1))
                for i in range(NCH):
                    m = mm(bank[QK_BANK[b]][:, HW * i:HW * (i + 1)], qst[:, b, P * i:P * (i + 1)], kst[:, b, :],
                           start=True, stop=True)
                m.then_inc(ev["s_score"], 1)

            def s_transpose(b):
                if b < 2:
                    pe.wait_ge(ev["s_vt_lo"], b + 1)
                else:
                    pe.wait_ge(ev["s_pt_lo"], b - 1)
                transposes(bank[6 + b % 2], b, ev["s_norm"], NCH * b).then_inc(ev["s_tp"], 1)

            def s_apply(b):
                pe.wait_ge(ev["s_pt_lo"], b + 1)
                if b >= 2:
                    pe.wait_ge(ev["s_att"], b - 1)
                for j in range(NCH):
                    m = mm3(bank[4 + b % 2][:, 0:HW], [p[:, b, j, :] for p in vt], [p[:, b, j, :] for p in ptp],
                            j == 0, j == NCH - 1)
                m.then_inc(ev["s_av"], 1)

            def c_transpose_in(i):
                pe.wait_ge(ev["xc_done"], i + 1)
                for b in (2 * i, 2 * i + 1):
                    for j in range(NCH):
                        c = C * (NCH * (b % 2) + j)
                        m = nc.tensor.transpose(bank[2 + i][:, c:c + C], xc[:, b, P * j:P * (j + 1)], ident)
                m.then_inc(ev["c_yt"], 1)

            def c_gram(i):
                pe.wait_ge(ev["c_yt_sb"], i + 1)
                for b in (2 * i, 2 * i + 1):
                    for j in range(NCH):
                        yj = yt[:, b, C * j:C * (j + 1)]
                        m = mm(bank[2 + i][:, C * (b % 2):C * (b % 2 + 1)], yj, yj, start=(j == 0),
                               stop=(j == NCH - 1))
                m.then_inc(ev["c_gram"], 1)

            def c_transpose(i):
                pe.wait_ge(ev["c_norm"], 2 * (i + 1))
                pe.wait_ge(ev["s_pt_lo"], B - 1 + i)
                for b in (2 * i, 2 * i + 1):
                    m = nc.tensor.transpose(bank[6 + i][:, C * (b % 2):C * (b % 2 + 1)], cprob[:, b, :], ident)
                m.then_inc(ev["c_tp"], 1)

            def c_apply(i):
                pe.wait_ge(ev["c_pt_lo"], i + 1)
                pe.wait_ge(ev["xc_lo"], i + 1)
                pe.wait_ge(ev["s_att"], B - 1 + i)
                for b in (2 * i, 2 * i + 1):
                    m = mm3(bank[4 + i][:, HW * (b % 2):HW * (b % 2 + 1)], [p[:, b, 0, 0:C] for p in ptp],
                            batch(map_b, b))
                m.then_inc(ev["c_av"], 1)

            pe.wait_ge(ev["par0_lo"], 1)
            qk(0)
            qk(1)
            v(0)
            cam_taps(0, 2)
            qk(2)
            qk(3)
            v(1)
            s_score(0)
            s_score(1)
            s_score(2)
            s_score(3)
            cam_taps(2, 7)
            s_transpose(0)
            cam_taps(7, 8)
            s_transpose(1)
            cam_taps(8, 9)
            s_apply(0)
            s_transpose(2)
            cam_taps(9, 10)
            s_apply(1)
            s_transpose(3)
            cam_taps(10, 12)
            c_transpose_in(0)
            s_apply(2)
            cam_taps(12, 14)
            s_apply(3)
            cam_taps(14, 16)
            c_gram(0)
            cam_taps(16, 18)
            out_s_taps(0, 2)
            c_transpose(0)
            out_s_taps(2, 3)
            c_transpose_in(1)
            out_s_taps(3, 6)
            c_apply(0)
            out_s_taps(6, 7)
            c_gram(1)
            out_s_taps(7, 11)
            c_transpose(1)
            out_s_taps(11, 15)
            c_apply(1)
            out_s_taps(15, 18)
            pe.wait_ge(ev["c_lo"], 1)
            for t in range(NT):
                if t % 3 == 0:
                    weights_split("out_c", t)
                m = tap("out_c", "c", bank[0], 0, t, False, t == NT - 1)
            m.then_inc(ev["out_conv"], 1)
            pe.wait_ge(ev["c_lo"], 2)
            for t in range(NT):
                m = tap_batch("out_c", "c", 2, t, False, t == NT - 1)
            m.then_inc(ev["out_conv"], 1)

            def window(w, b):
                a = WIN - WID * b
                return [p[:, a:a + P] for p in w]

            def mask_and_reduce(b):
                pe.wait_ge(ev["x1_lo"], b + 1)
                mm3(bank[2][:, 0:HW], window(parts("sm_win"), b), batch(map_a, b), b == 0, False)
                mm3(bank[3][:, 0:HW], window(parts("w1_win"), b), batch(map_a, b), b == 0, False)

            def channel_logit(b):
                return mm(bank[4][:, 0:1], window([p1("cm1_win")], b)[0], pool1[:, b:b + 1], start=(b == 0),
                          stop=(b == B - 1))

            pe.wait_ge(ev["par1_lo"], 1)
            mask_and_reduce(0)
            mask_and_reduce(1)
            channel_logit(0)
            channel_logit(1)
            for t in range(NT):
                m = tap_batch("out_c", "c", 3, t, False, t == NT - 1)
            m.then_inc(ev["out_conv"], 1)
            mask_and_reduce(2)
            channel_logit(2)
            pe.wait_ge(ev["x1_done"], B)
            mm(bank[2][:, 0:HW], window([p1("sm_win")], B - 1)[0], x1[:, B - 1, :], start=False, stop=True,
               skip_group_check=True).then_inc(ev["m_logit"], 1)
            mm(bank[3][:, 0:HW], window([p1("w1_win")], B - 1)[0], x1[:, B - 1, :], start=False, stop=True,
               skip_group_check=True).then_inc(ev["h1_conv"], 1)
            channel_logit(B - 1).then_inc(ev["cm1_logit"], 1)
            pe.wait_ge(ev["mask"], 1)
            for t, (dy, dx) in enumerate(TAPS):
                m = mm(bank[7][:, 0:HW].rearrange("p (h w) -> p h w", h=H), ident_r[:, :],
                       mpad[:, dy:dy + H, dx:dx + W], start=(t == 0), stop=(t == NT - 1))
            m.then_inc(ev["m_count"], 1)
            pe.wait_ge(ev["spread"], B + 2)
            o = bank[5][:, 0:HW].rearrange("p (h w) -> p h w", h=H)
            pe.wait_ge(ev["h1_parts"], 1)
            for t, (dy, dx) in enumerate(TAPS):
                for w in w2bd:
                    mm(o, w[:, t, :], hpad[0][:, dy:dy + H, dx:dx + W], start=(t == 0 and w is w2bd[0]), stop=False,
                       skip_group_check=True)
            pe.wait_ge(ev["h1_parts"], 2)
            for k in range(2):
                m = mm(bank[0][:, 0:1], cm2bd[:, :], pool2[:, k:k + 1], start=(k == 0), stop=(k == 1))
            m.then_inc(ev["cm2_logit"], 1)
            for t, (dy, dx) in enumerate(TAPS):
                m = mm(o, w2bd[0][:, t, :], hpad[1][:, dy:dy + H, dx:dx + W], start=False, stop=(t == NT - 1),
                       skip_group_check=True)
            m.then_inc(ev["h2_conv"], 1)
            for b in range(B):
                for k in range(2):
                    mm(bank[6 + b // 2][:, HW * (b % 2):HW * (b % 2 + 1)].rearrange("p (h w) -> p h w", h=H),
                       b3p[k][:, b, :], mpad[:, 1:1 + H, 1:1 + W],
                       start=(b % 2 == 0 and k == 0), stop=False, skip_group_check=True)
            pe.wait_ge(ev["m_lines"], 2)
            pe.wait_ge(ev["cm2_done"], 1)
            for b in range(B):
                mm(bank[0][:, 2 * H * b:2 * H * (b + 1)], b3z[:, b, :], hw(linem), start=(b == 0), stop=False,
                   skip_group_check=True)
            pe.wait_ge(ev["h2_pool"], 1)
            mm(bank[1][:, 0:B], p1("cm3_rep"), pool3g[:, :], start=True, stop=True).then_inc(ev["cm3_logit"], 1)
            pe.wait_ge(ev["h2_lines"], 2)
            for b in range(B):
                m = mm(bank[0][:, 2 * H * b:2 * H * (b + 1)], w3z[:, b, :], hw(lineh), start=False,
                       stop=(b == B - 1), skip_group_check=True)
            m.then_inc(ev["line_mm"], 1)
            pe.wait_ge(ev["h2_lo"], 1)
            for b in range(B):
                m = mm3(bank[6 + b // 2][:, HW * (b % 2):HW * (b % 2 + 1)], [p[:, b, :] for p in w3p],
                        [hw(p) for p in h2p], False, b % 2 == 1)
                if b == 0:
                    pe.wait_ge(ev["yin_done"], 1)
                    mm(bank[2][0:MIP, 0:B * 2 * H], p1("ca_w1"), yin[:, :, :, :].rearrange("p b i h -> p (b i h)"),
                       start=True, stop=True).then_inc(ev["y_mm"], 1)
            m.then_inc(ev["h3_mm"], 1)
            pe.wait_ge(ev["y_step"], 3)
            mm(bank[3][:, 0:B * H].rearrange("p (b h) -> p b h", b=B), p1("ca_wh", MIP), ys[:, :, 0, :],
               start=True, stop=True)
            mm(bank[3][:, B * H:2 * B * H].rearrange("p (b h) -> p b h", b=B), p1("ca_ww", MIP), ys[:, :, 1, :],
               start=True, stop=True).then_inc(ev["gate_mm"], 1)

            keep_clock(5, 24)

            def project(b):
                if b in (1, 2):
                    keep_clock(2 * b, 4)
                pe.wait_ge(ev["x2_done"], b + 1)
                mm(bank[2 * b][0:ST + L, 0:HW], p1("w_tpg"), x2[:, b, :], start=True,
                   stop=True).then_inc(ev["n_proj"], 1)

            def turn_values(b):
                pe.wait_ge(ev["a_gt"], b + 1)
                if b == B - 1:
                    pe.wait_ge(ev["t1_done"], B)
                for j in range(NCH):
                    m = nc.tensor.transpose(bank[2 * b + 1][:, L * j:L * (j + 1)], g_sb[:, b, P * j:P * (j + 1)],
                                            ident[0:L, 0:L])
                m.then_inc(ev["a_g"], 1)

            def scores(b, k=0):
                pe.wait_ge(ev["n_qk_lo"], 2 * (k + b + 1))
                if k == 0:
                    pe.wait_ge(ev["a_gt"], b + 1)
                for i in range(NCH):
                    m = mm(bank[2 * b + k // B][:, HW * i:HW * (i + 1)], qst[:, b, P * i:P * (i + 1)], kst[:, b, :],
                           start=True, stop=True)
                m.then_inc(ev["n_score"], 1)

            def turn_self(b):
                pe.wait_ge(ev["a_g_sb"], b + 1)
                transposes(bank[2 * b + 1], b, ev["n_exp"], NCH * b).then_inc(ev["n_tp"], 1)

            def apply_self(b):
                pe.wait_ge(ev["n_pt_sb"], b + 1)
                for i in range(NCH):
                    for j in range(NCH):
                        m = mm(bank[2 * b][:, L * i:L * (i + 1)], pt_sb[:, b, j, P * i:P * (i + 1)],
                               gt[:, b, j, :], start=(j == 0), stop=(j == NCH - 1))
                m.then_inc(ev["n_av"], 1)

            def out_rows(b, o, done):
                for i in range(NCH):
                    pe.wait_ge(done, NCH * b + i + 1)
                    m = mm(o[:, 0:HW], p1("w_o_rep")[:, C * i:C * (i + 1)], wide[:, b, i, :], start=(i == 0),
                           stop=(i == NCH - 1))
                return m

            def out_self(b):
                out_rows(b, bank[2 * b + 1], ev["a_wide"]).then_inc(ev["a_out"], 1)

            def query(b):
                pe.wait_ge(ev["a_done"], b + 1)
                mm(bank[2 * b][0:2 * GAP, 0:HW], p1("w_tpg")[:, 0:2 * GAP], sa[:, b, :], start=True,
                   stop=True).then_inc(ev["e_proj"], 1)

            def scores_concepts(b):
                pe.wait_ge(ev["con_lo"], 1)
                pe.wait_ge(ev["e_q_lo"], b + 1)
                for i in range(NCH):
                    m = mm(bank[2 * b + 1][:, NCON * i:NCON * (i + 1)], qst[:, b, P * i:P * (i + 1)], con_st[:, :],
                           start=True, stop=True)
                m.then_inc(ev["e_score"], 1)

            def turn_concepts(b):
                for i in range(NCH):
                    pe.wait_ge(ev["e_exp"], NCH * b + i + 1)
                    m = nc.tensor.transpose(bank[2 * b][0:NCON, P * i:P * (i + 1)], prob2[:, b, i, :], ident)
                m.then_inc(ev["e_tp"], 1)

            def apply_concepts(b):
                pe.wait_ge(ev["e_pt_sb"], b + 1)
                for i in range(NCH):
                    m = mm(bank[2 * b + 1][:, L * i:L * (i + 1)], pt2[:, b, P * i:P * (i + 1)], p1("con", NCON),
                           start=True, stop=True)
                m.then_inc(ev["e_av"], 1)

            def out_concepts(b):
                out_rows(b, bank[2 * b], ev["e_wide"]).then_inc(ev["e_out"], 1)

            def project_last(b):
                pe.wait_ge(ev["e_done"], b + 1)
                mm(bank[2 * b + 1][0:ST, 0:HW], p1("w_q3"), x3[:, b, :], start=True, stop=True)
                mm(bank[2 * b + 1][0:ST, HW:2 * HW], p1("w_k3"), x3[:, b, :], start=True,
                   stop=True).then_inc(ev["n_proj"], 1)
                for j in range(NCH):
                    m = mm(bank[2 * b][:, C * j:C * (j + 1)], x3[:, b, P * j:P * (j + 1)], p1("w_v3"), start=True,
                           stop=True)
                m.then_inc(ev["f_vt"], 1)

            def scores_last(b):
                scores(b, B)

            def turn_last(b):
                pe.wait_ge(ev["f_vt_sb"], b + 1)
                transposes(bank[2 * b], b, ev["f_norm"], NCH * b).then_inc(ev["n_tp"], 1)

            def apply_last(b):
                pe.wait_ge(ev["n_pt_sb"], B + b + 1)
                for j in range(NCH):
                    m = mm(bank[2 * b + 1][:, 0:HW], vt3[:, b, C * j:C * (j + 1)], pt_sb[:, b, j, :], start=(j == 0),
                           stop=(j == NCH - 1))
                m.then_inc(ev["n_av"], 1)

            for step, b in ((project, 0), (project, 1), (turn_values, 0), (turn_values, 1), (scores, 0),
                            (project, 2), (project, 3), (scores, 1), (turn_self, 0), (apply_self, 0),
                            (turn_self, 1), (turn_values, 2), (scores, 2), (out_self, 0), (apply_self, 1),
                            (turn_values, 3), (scores, 3), (query, 0), (turn_self, 2), (out_self, 1),
                            (apply_self, 2), (query, 1), (turn_self, 3), (scores_concepts, 0), (out_self, 2),
                            (apply_self, 3), (turn_concepts, 0), (query, 2), (scores_concepts, 1),
                            (apply_concepts, 0), (out_self, 3), (turn_concepts, 1), (scores_concepts, 2),
                            (out_concepts, 0), (query, 3), (turn_concepts, 2), (apply_concepts, 1),
                            (project_last, 0), (scores_concepts, 3), (apply_concepts, 2), (out_concepts, 1),
                            (turn_concepts, 3), (out_concepts, 2), (apply_concepts, 3), (scores_last, 0),
                            (project_last, 1), (out_concepts, 3), (project_last, 2), (project_last, 3),
                            (scores_last, 1), (turn_last, 0), (scores_last, 2), (apply_last, 0), (scores_last, 3),
                            (turn_last, 1), (apply_last, 1), (turn_last, 2), (turn_last, 3), (apply_last, 2),
                            (apply_last, 3)):
                step(b)


def kernel(**inputs):
    import numpy as np
    import concourse.bacc as bacc
    from concourse.bass_utils import run_bass_kernel_spmd

    a = {k: np.asarray(v) for k, v in inputs.items()}
    g0 = lambda n: a["L0_conv_" + n]
    g1 = lambda n: a["L1_conv_" + n]
    g2 = lambda n: a["L2_conv_" + n]
    g3 = lambda n: a["L3_conv_" + n]
    f32 = a["x"].dtype

    def taps(w):
        return np.transpose(w, (1, 2, 3, 0)).reshape(w.shape[1], -1)

    def stack(u):
        w = np.zeros((u.shape[0], 3, GAP), f32)
        w[:, :, 0:L] = u[:, None, :]
        return w.reshape(u.shape[0], ST)

    def queries_keys(q, k):
        w = stack(q)
        w[:, 2 * GAP:2 * GAP + L] = k
        return w

    def window(w):
        z = np.zeros((C, WIN), f32)
        return np.concatenate([z, w, z], axis=1)

    def pack(table, values):
        cols, width = columns(table)
        m = np.zeros((P, width), f32)
        for name, (at, w) in cols.items():
            v = np.asarray(values[name], f32)
            v = v.reshape(-1, w)
            m[0:v.shape[0], at:at + w] = v
        return m

    col = lambda v: np.reshape(v, (-1, 1))
    full = lambda v: np.broadcast_to(np.reshape(v, (1, 1)), (P, 1))
    four = lambda v: np.concatenate([v] * B, axis=0)

    early = pack(EARLY + EARLY_SPLIT, {
        "bn_scale": np.stack([g0("bn_sam_scale"), g0("bn_cam_scale")], 1),
        "bn_bias": np.stack([g0("bn_sam_bias"), g0("bn_cam_bias")], 1),
        "bn_mean": np.stack([g0("bn_sam_mean"), g0("bn_cam_mean")], 1),
        "bn_var": np.stack([g0("bn_sam_var"), g0("bn_cam_var")], 1),
        "gam_sam": full(g0("gamma_sam")), "gam_cam": full(g0("gamma_cam")),
        "ident": np.eye(P, dtype=f32),
        "w_qk": queries_keys(g0("w_qk")[0:L, :, 0, 0].T, g0("w_qk")[L:2 * L, :, 0, 0].T),
        "w_v": g0("w_v")[:, :, 0, 0].T,
    })
    w2t = np.transpose(g1("w2"), (1, 2, 3, 0)).reshape(WID, NT * WID)
    sel16 = np.zeros((P, L), f32)
    sel16[np.arange(P), np.arange(P) % L] = 1
    group = np.zeros((P, B), f32)
    group[np.arange(P), np.arange(P) // WID] = 1
    late = pack(LATE + LATE_SPLIT, {
        "sm_b": full(g1("sm_b")), "b1": four(col(g1("b1"))), "b2": four(col(g1("b2"))),
        "cm1_b": four(col(g1("cm1_b"))), "cm2_b": four(col(g1("cm2_b"))), "cm3_b": col(g1("cm3_b")),
        "ca_b1": col(g1("ca_b1")), "ca_bh": col(g1("ca_bh")), "ca_bw": col(g1("ca_bw")),
        "gam_sa": full(g2("gamma_sa")), "gam_moca": full(g2("gamma_moca")), "gam3": full(g3("gamma")),
        "bq": stack(g3("bq").reshape(1, L)).T, "bk": stack(g3("bk").reshape(1, L)).T, "bv": col(g3("bv")),
        "group": group, "sel16": sel16,
        "sm_win": window(np.repeat(g1("sm_w").reshape(C, 1), WID, axis=1)),
        "w1_win": window(g1("w1")[:, :, 0, 0].T), "cm1_win": window(g1("cm1_w").T),
        "w2_rep": four(w2t), "cm2_rep": four(g1("cm2_w").T), "cm3_rep": four(g1("cm3_w").T),
        "w3_rep": four(g1("w3")[:, :, 0, 0].T), "b3_row": np.broadcast_to(g1("b3").reshape(1, C), (P, C)),
        "ca_w1": g1("ca_w1")[:, :, 0, 0].T, "ca_wh": g1("ca_wh")[:, :, 0, 0].T, "ca_ww": g1("ca_ww")[:, :, 0, 0].T,
        "w_tpg": np.concatenate([queries_keys(g2("w_theta").T, g2("w_phi").T), g2("w_g").T], axis=1),
        "w_o_rep": np.concatenate(np.split(np.repeat(g2("w_o").T, HW // L, axis=0), NCH, axis=0), axis=1),
        "con_t": stack(g2("concepts")).T, "con": g2("concepts"),
        "w_q3": stack(g3("Wq").T), "w_k3": stack(g3("Wk").T), "w_v3": g3("Wv").T,
    })
    w_out = g0("w_out")
    arrays = {
        "x": a["x"],
        "w_sam": taps(g0("w_sam")), "w_cam": taps(g0("w_cam")),
        "w_out": np.concatenate([taps(w_out[:, 0:C]), taps(w_out[:, C:2 * C])], axis=1),
        "early": early, "late": late,
    }
    arrays = {k: np.ascontiguousarray(v) for k, v in arrays.items()}
    nc = bacc.Bacc("TRN2", target_bir_lowering=False, num_devices=1)
    args = [nc.dram_tensor(f"in_{k}", v.shape, mybir.dt.from_np(v.dtype), kind="ExternalInput").ap()
            for k, v in arrays.items()]
    out = nc.dram_tensor("out_0", a["x"].shape, F32, kind="ExternalOutput").ap()
    build(nc, *args, out)
    r = run_bass_kernel_spmd(nc, [{f"in_{k}": v for k, v in arrays.items()}], core_ids=[0])
    return r.results[0]["out_0"]
```
